# Optimizing a Trainium2 kernel written in Bass

```python
import numpy as np
import jax
import jax.numpy as jnp

def _softmax(x, axis=-1):
    return jax.nn.softmax(x, axis=axis)

def _gelu(x):
    return jax.nn.gelu(x, approximate=True)

def _silu(x):
    return jax.nn.silu(x)

def _sigmoid(x):
    return jax.nn.sigmoid(x)

def _layernorm(x, axis=-1, eps=1e-05):
    m = jnp.mean(x, axis=axis, keepdims=True)
    v = jnp.var(x, axis=axis, keepdims=True)
    return (x - m) / jnp.sqrt(v + eps)

def _scatter_add(tgt, idx, src, axis=0):
    return tgt.at[idx].add(src)

def _segment_sum(src, seg, n):
    return jax.ops.segment_sum(src, seg, n)
kernel_name = 'mk_vit_tower_postln_d1_tok_img2048_r4_e11057'

def setup_inputs(seed: int=0):
    np.random.seed(seed)
    _w = jnp.asarray

    def _rec_inputs():
        import jax
        import jax.numpy as jnp
        _rk = jax.random.key(seed)
        x = -0.00340659 + 1.00146 * jax.random.normal(jax.random.fold_in(_rk, 1), (16, 256, 64, 2), jnp.float32)
        return x
    x = _rec_inputs()

    def _L0_tok_setup():
        import jax, jax.numpy as jnp
        import numpy as np
        CH, H, N, N_SSM, SEQ_L = (1, 256, 64, 256, 512)

        def _kernel(C_ri, log_dt, B_ri, inv_A_real, A_imag, L):
            C = C_ri[..., 0] + 1j * C_ri[..., 1]
            B = B_ri[..., 0] + 1j * B_ri[..., 1]
            A = -jnp.exp(inv_A_real) + 1j * A_imag
            rep = log_dt.shape[0] // inv_A_real.shape[0]
            B = jnp.tile(B, (rep, 1))
            A = jnp.tile(A, (rep, 1))
            dt = jnp.exp(log_dt)
            dtA = A * dt[:, None]
            Ct = B[None] * C / (1.0 - dtA / 2) * dt[:, None]
            dA = (1.0 + dtA / 2) / (1.0 - dtA / 2)
            dA_log = jnp.log(dA)
            l = jnp.arange(L, dtype=jnp.float32)
            V = jnp.exp(dA_log[:, :, None] * l)
            K = 2.0 * jnp.einsum('chn,hnl->chl', Ct, V).real
            return K
        key = jax.random.key(seed)
        ks = jax.random.split(key, 5)
        return {'C_ri': jax.random.normal(ks[0], (CH, H, N, 2), dtype=jnp.float32), 'log_dt': jax.random.normal(ks[1], (H,), dtype=jnp.float32), 'B_ri': jax.random.normal(ks[2], (N_SSM, N, 2), dtype=jnp.float32), 'inv_A_real': jax.random.normal(ks[3], (N_SSM, N), dtype=jnp.float32), 'A_imag': jax.random.normal(ks[4], (N_SSM, N), dtype=jnp.float32), 'L': SEQ_L}
    _L0_tok_all = _L0_tok_setup()
    _L0_tok_in = {k: v for k, v in _L0_tok_all.items() if k in ('log_dt', 'B_ri', 'inv_A_real', 'A_imag')}
    del _L0_tok_all

    def _L0_attn_setup():
        import jax, jax.numpy as jnp
        import numpy as np
        B, S, D_MODEL = (2, 512, 512)
        N_HEADS, NOPE, ROPE_D, VDIM = (16, 128, 64, 128)
        Q_RANK, KV_RANK, EPS = (384, 128, 1e-06)

        def _rmsnorm(x, w, eps=EPS):
            return x * jax.lax.rsqrt(jnp.mean(x * x, axis=-1, keepdims=True) + eps) * w

        def _apply_rope(x):
            b, h, s, d = x.shape
            pos = jnp.arange(s, dtype=x.dtype)
            inv_freq = 1.0 / 10000.0 ** (jnp.arange(0, d, 2, dtype=x.dtype) / d)
            ang = pos[:, None] * inv_freq[None, :]
            cos, sin = (jnp.cos(ang), jnp.sin(ang))
            x1, x2 = (x[..., 0::2], x[..., 1::2])
            o1 = x1 * cos - x2 * sin
            o2 = x1 * sin + x2 * cos
            return jnp.stack([o1, o2], axis=-1).reshape(b, h, s, d)
        key = jax.random.key(seed)
        ks = jax.random.split(key, 9)
        sc = 0.02
        return {'x': jax.random.normal(ks[0], (B, S, D_MODEL), jnp.float32), 'wq_down': jax.random.normal(ks[1], (D_MODEL, Q_RANK), jnp.float32) * sc, 'q_norm_w': jnp.ones((Q_RANK,), jnp.float32), 'wq_up': jax.random.normal(ks[2], (Q_RANK, N_HEADS * NOPE), jnp.float32) * sc, 'wq_rope': jax.random.normal(ks[3], (Q_RANK, N_HEADS * ROPE_D), jnp.float32) * sc, 'wkv_down': jax.random.normal(ks[4], (D_MODEL, KV_RANK), jnp.float32) * sc, 'kv_norm_w': jnp.ones((KV_RANK,), jnp.float32), 'wkv_up': jax.random.normal(ks[5], (KV_RANK, N_HEADS * (NOPE + VDIM)), jnp.float32) * sc, 'wk_rope': jax.random.normal(ks[6], (D_MODEL, ROPE_D), jnp.float32) * sc, 'wo': jax.random.normal(ks[7], (N_HEADS * VDIM, D_MODEL), jnp.float32) * sc}
    _L0_attn_all = _L0_attn_setup()
    _L0_attn_in = {k: v for k, v in _L0_attn_all.items() if k in ('wq_down', 'q_norm_w', 'wq_up', 'wq_rope', 'wkv_down', 'kv_norm_w', 'wkv_up', 'wk_rope', 'wo')}
    del _L0_attn_all

    def _L0_ffn_setup():
        import jax, jax.numpy as jnp
        import numpy as np
        FP8_MAX = 448.0
        GLOBAL_DIV = 448.0 * 6.0

        def _fp8(x):
            return x.astype(jnp.float8_e4m3fn).astype(jnp.float32)

        def _reorder_quantize_x(x, idx):
            scale = jnp.max(jnp.abs(x)) / GLOBAL_DIV
            xr = (x / scale)[:, idx]
            scale_x = jnp.max(jnp.abs(xr), axis=1, keepdims=True) / FP8_MAX
            qx = _fp8(xr / scale_x)
            return (qx, scale_x, scale)

        def _qlinear(qx, scale_x, scale, W, idx, out_idx=None):
            Wr = W[:, idx]
            w_scale = jnp.max(jnp.abs(Wr), axis=1, keepdims=True) / FP8_MAX
            qw = _fp8(Wr / w_scale)
            y = qx * scale_x @ (qw * w_scale).T * scale
            if out_idx is not None:
                y = y[:, out_idx]
            return y
        key = jax.random.key(seed)
        ks = jax.random.split(key, 6)
        B, S, H, I = (2, 256, 512, 1408)
        return {'x': jax.random.normal(ks[0], (B, S, H), jnp.float32), 'w_gate': jax.random.normal(ks[1], (I, H), jnp.float32) * 0.02, 'w_up': jax.random.normal(ks[2], (I, H), jnp.float32) * 0.02, 'w_down': jax.random.normal(ks[3], (H, I), jnp.float32) * 0.02, 'up_reorder_index': jax.random.permutation(ks[4], jnp.arange(H, dtype=jnp.int64)), 'down_reorder_index': jax.random.permutation(ks[5], jnp.arange(I, dtype=jnp.int64))}
    _L0_ffn_all = _L0_ffn_setup()
    _L0_ffn_in = {k: v for k, v in _L0_ffn_all.items() if k in ('w_gate', 'w_up', 'w_down', 'up_reorder_index', 'down_reorder_index')}
    del _L0_ffn_all
    return {'x': x, 'L0_tok_log_dt': _L0_tok_in['log_dt'], 'L0_tok_B_ri': _L0_tok_in['B_ri'], 'L0_tok_inv_A_real': _L0_tok_in['inv_A_real'], 'L0_tok_A_imag': _L0_tok_in['A_imag'], 'L0_attn_wq_down': _L0_attn_in['wq_down'], 'L0_attn_q_norm_w': _L0_attn_in['q_norm_w'], 'L0_attn_wq_up': _L0_attn_in['wq_up'], 'L0_attn_wq_rope': _L0_attn_in['wq_rope'], 'L0_attn_wkv_down': _L0_attn_in['wkv_down'], 'L0_attn_kv_norm_w': _L0_attn_in['kv_norm_w'], 'L0_attn_wkv_up': _L0_attn_in['wkv_up'], 'L0_attn_wk_rope': _L0_attn_in['wk_rope'], 'L0_attn_wo': _L0_attn_in['wo'], 'L0_ffn_w_gate': _L0_ffn_in['w_gate'], 'L0_ffn_w_up': _L0_ffn_in['w_up'], 'L0_ffn_w_down': _L0_ffn_in['w_down'], 'L0_ffn_up_reorder_index': _L0_ffn_in['up_reorder_index'], 'L0_ffn_down_reorder_index': _L0_ffn_in['down_reorder_index']}

def reference(x, L0_tok_log_dt, L0_tok_B_ri, L0_tok_inv_A_real, L0_tok_A_imag, L0_attn_wq_down, L0_attn_q_norm_w, L0_attn_wq_up, L0_attn_wq_rope, L0_attn_wkv_down, L0_attn_kv_norm_w, L0_attn_wkv_up, L0_attn_wk_rope, L0_attn_wo, L0_ffn_w_gate, L0_ffn_w_up, L0_ffn_w_down, L0_ffn_up_reorder_index, L0_ffn_down_reorder_index):
    import jax
    import jax.numpy as jnp

    def _L0_tok_ref(C_ri, log_dt, B_ri, inv_A_real, A_imag, L):
        import jax, jax.numpy as jnp
        import numpy as np
        CH, H, N, N_SSM, SEQ_L = (1, 256, 64, 256, 512)

        def _kernel(C_ri, log_dt, B_ri, inv_A_real, A_imag, L):
            C = C_ri[..., 0] + 1j * C_ri[..., 1]
            B = B_ri[..., 0] + 1j * B_ri[..., 1]
            A = -jnp.exp(inv_A_real) + 1j * A_imag
            rep = log_dt.shape[0] // inv_A_real.shape[0]
            B = jnp.tile(B, (rep, 1))
            A = jnp.tile(A, (rep, 1))
            dt = jnp.exp(log_dt)
            dtA = A * dt[:, None]
            Ct = B[None] * C / (1.0 - dtA / 2) * dt[:, None]
            dA = (1.0 + dtA / 2) / (1.0 - dtA / 2)
            dA_log = jnp.log(dA)
            l = jnp.arange(L, dtype=jnp.float32)
            V = jnp.exp(dA_log[:, :, None] * l)
            K = 2.0 * jnp.einsum('chn,hnl->chl', Ct, V).real
            return K
        return _kernel(C_ri, log_dt, B_ri, inv_A_real, A_imag, L)

    def _L0_attn_ref(x, wq_down, q_norm_w, wq_up, wq_rope, wkv_down, kv_norm_w, wkv_up, wk_rope, wo):
        import jax, jax.numpy as jnp
        import numpy as np
        B, S, D_MODEL = (2, 512, 512)
        N_HEADS, NOPE, ROPE_D, VDIM = (16, 128, 64, 128)
        Q_RANK, KV_RANK, EPS = (384, 128, 1e-06)

        def _rmsnorm(x, w, eps=EPS):
            return x * jax.lax.rsqrt(jnp.mean(x * x, axis=-1, keepdims=True) + eps) * w

        def _apply_rope(x):
            b, h, s, d = x.shape
            pos = jnp.arange(s, dtype=x.dtype)
            inv_freq = 1.0 / 10000.0 ** (jnp.arange(0, d, 2, dtype=x.dtype) / d)
            ang = pos[:, None] * inv_freq[None, :]
            cos, sin = (jnp.cos(ang), jnp.sin(ang))
            x1, x2 = (x[..., 0::2], x[..., 1::2])
            o1 = x1 * cos - x2 * sin
            o2 = x1 * sin + x2 * cos
            return jnp.stack([o1, o2], axis=-1).reshape(b, h, s, d)
        bs, s, _ = x.shape
        q_c = _rmsnorm(x @ wq_down, q_norm_w)
        q_nope = (q_c @ wq_up).reshape(bs, s, N_HEADS, NOPE).transpose(0, 2, 1, 3)
        q_rope = (q_c @ wq_rope).reshape(bs, s, N_HEADS, ROPE_D).transpose(0, 2, 1, 3)
        q_rope = _apply_rope(q_rope)
        kv_c = _rmsnorm(x @ wkv_down, kv_norm_w)
        kv_up = (kv_c @ wkv_up).reshape(bs, s, N_HEADS, NOPE + VDIM)
        k_nope = kv_up[..., :NOPE].transpose(0, 2, 1, 3)
        v = kv_up[..., NOPE:].transpose(0, 2, 1, 3)
        k_rope = _apply_rope((x @ wk_rope).reshape(bs, s, 1, ROPE_D).transpose(0, 2, 1, 3))
        scale = 1.0 / np.sqrt(NOPE + ROPE_D)
        scores = jnp.einsum('bhqd,bhkd->bhqk', q_nope, k_nope)
        scores = scores + jnp.einsum('bhqd,bokd->bhqk', q_rope, k_rope)
        scores = scores * scale
        causal = jnp.tril(jnp.ones((s, s), bool))
        scores = jnp.where(causal[None, None], scores, -1000000000.0)
        probs = jax.nn.softmax(scores.astype(jnp.float32), axis=-1).astype(x.dtype)
        out = jnp.einsum('bhqk,bhkv->bhqv', probs, v)
        out = out.transpose(0, 2, 1, 3).reshape(bs, s, N_HEADS * VDIM)
        return out @ wo

    def _L0_ffn_ref(x, w_gate, w_up, w_down, up_reorder_index, down_reorder_index):
        import jax, jax.numpy as jnp
        import numpy as np
        FP8_MAX = 448.0
        GLOBAL_DIV = 448.0 * 6.0

        def _fp8(x):
            return x.astype(jnp.float8_e4m3fn).astype(jnp.float32)

        def _reorder_quantize_x(x, idx):
            scale = jnp.max(jnp.abs(x)) / GLOBAL_DIV
            xr = (x / scale)[:, idx]
            scale_x = jnp.max(jnp.abs(xr), axis=1, keepdims=True) / FP8_MAX
            qx = _fp8(xr / scale_x)
            return (qx, scale_x, scale)

        def _qlinear(qx, scale_x, scale, W, idx, out_idx=None):
            Wr = W[:, idx]
            w_scale = jnp.max(jnp.abs(Wr), axis=1, keepdims=True) / FP8_MAX
            qw = _fp8(Wr / w_scale)
            y = qx * scale_x @ (qw * w_scale).T * scale
            if out_idx is not None:
                y = y[:, out_idx]
            return y
        B, S, H = x.shape
        xf = x.reshape(B * S, H)
        qx, sx, sc = _reorder_quantize_x(xf, up_reorder_index)
        g = _qlinear(qx, sx, sc, w_gate, up_reorder_index, out_idx=down_reorder_index)
        u = _qlinear(qx, sx, sc, w_up, up_reorder_index, out_idx=down_reorder_index)
        t = jax.nn.silu(g) * u
        qt, st, sct = _reorder_quantize_x(t, down_reorder_index)
        y = _qlinear(qt, st, sct, w_down, down_reorder_index)
        return y.reshape(B, S, H)
    h = _L0_tok_ref(x, L0_tok_log_dt, L0_tok_B_ri, L0_tok_inv_A_real, L0_tok_A_imag, 512)
    h = _layernorm(h + _L0_attn_ref(h, L0_attn_wq_down, L0_attn_q_norm_w, L0_attn_wq_up, L0_attn_wq_rope, L0_attn_wkv_down, L0_attn_kv_norm_w, L0_attn_wkv_up, L0_attn_wk_rope, L0_attn_wo), axis=-1)
    h = _layernorm(h + _L0_ffn_ref(h, L0_ffn_w_gate, L0_ffn_w_up, L0_ffn_w_down, L0_ffn_up_reorder_index, L0_ffn_down_reorder_index), axis=-1)
    return h

_drawn_inputs = setup_inputs


def setup_inputs(seed=0):
    import zlib

    import numpy as np

    out = dict(_drawn_inputs(seed))
    spreads = {'L0_attn_q_norm_w': (1.0, 0.6), 'L0_attn_kv_norm_w': (1.0, 0.6)}
    factors = {'L0_attn_wq_up': 3.192, 'L0_attn_wq_rope': 3.203, 'L0_attn_wk_rope': 3.065}
    for name, (base, spread) in spreads.items():
        noise = np.random.default_rng([zlib.crc32(name.encode()), seed]).standard_normal(out[name].shape)
        drawn = base * np.exp(spread * noise) if base else spread * noise
        out[name] = jnp.asarray(drawn.astype(out[name].dtype))
    for name, factor in factors.items():
        out[name] = (out[name] * factor).astype(out[name].dtype)
    return out
```

```python
import concourse.bass as bass
from concourse import mybir
from contextlib import ExitStack

F32 = mybir.dt.float32
F16 = mybir.dt.float16
BF16 = mybir.dt.bfloat16
I32 = mybir.dt.int32
U32 = mybir.dt.uint32
ALU = mybir.AluOpType
ACT = mybir.ActivationFunctionType
AX = mybir.AxisListType

P = 128
NB, S, D = 16, 256, 512
NSTATE = 64
NT, KD = S // P, D // P
NH, RD, HD = 16, 64, 128
QR, KV = 384, 128
KQ = QR // P
FF = 1408
KF = FF // P
NCH, CH = 4, FF // 4
PAIRS, GROUPS = NH // 2, NH // 4
A_STEPS, B_STEPS = 8, 64
HBLK = 16
NBLK = P // HBLK
EPS_RMS, EPS_LN = 1e-6, 1e-5
SCALE = float((HD + RD) ** -0.5)
S_NOPE, S_RQ, S_RK = 16.0, 64.0, 0.25
S_VO = 64.0
assert S_NOPE == S_RQ * S_RK
MASK = -1e30
PRIMED = 1
FP8_MAX = 448.0
EXPONENT_BITS = 0x7F800000
LEAST_NORMAL = 2.0 ** -6
ROUNDER = 1.5 * 2.0 ** 20


class Chain:

    def __init__(self, eng, sem):
        self.eng, self.sem, self.n, self.base = eng, sem, 0, 0

    def link(self, ins):
        self.n += 1
        ins.then_inc(self.sem, 1)
        self.eng.wait_ge(self.sem, self.base + self.n)


def token_mixer(nc, x_c, log_dt, b_ri, inv_a, a_imag, seq):
    with ExitStack() as ctx:
        def sb(name, shape, dt=F32):
            return ctx.enter_context(nc.sbuf_tensor(name, shape, dt))

        def ps(name, shape, dt=F32):
            return ctx.enter_context(nc.psum_tensor(name, shape, dt))

        def sem(name):
            return ctx.enter_context(nc.semaphore(name))

        N = NSTATE
        NL = 9
        ident = sb("tm_ident", [P, P])
        dtc = sb("tm_logdt", [P, 2])
        dt = sb("tm_dt", [P, 2])
        bri = sb("tm_b", [P, 2, N, 2])
        ia = sb("tm_inva", [P, 2, N])
        ea = sb("tm_expa", [P, 2, N])
        ai = sb("tm_aimag", [P, 2, N])
        s = {k: sb("tm_" + k, [P, 2, N]) for k in
             ("zr", "zi", "m", "t", "den", "r", "gr", "gi", "fr", "fi", "u", "v")}
        wr = sb("tm_wr", [P, NL, 2, N])
        wi = sb("tm_wi", [P, NL, 2, N])
        cin = sb("tm_cin", [P, NB, N, 2])
        cs = sb("tm_cs", [P, NB, 3, N])
        U = sb("tm_u_pow", [P, B_STEPS, 2, N])
        T1 = sb("tm_t1", [P, B_STEPS // 2, N])
        T2 = sb("tm_t2", [P, B_STEPS // 2, N])
        G = sb("tm_g", [P, A_STEPS, 4, N])
        gi_ = sb("tm_gim", [P, A_STEPS, N])
        UT = sb("tm_ut", [P, P, B_STEPS])
        P1 = sb("tm_p1", [P, P, NB])
        P2 = sb("tm_p2", [P, P, NB])
        G1 = sb("tm_g1", [P, P, A_STEPS])
        G2 = sb("tm_g2", [P, P, A_STEPS])
        X1 = sb("tm_x1", [P, 2, HBLK, NB, A_STEPS])
        X2 = sb("tm_x2", [P, 2, HBLK, NB, A_STEPS])
        Y = sb("tm_y", [P, 2, HBLK, B_STEPS])
        tp = [ps(f"tm_tp{i}", [P, 4, P]) for i in range(2)]
        yp = [ps(f"tm_yp{i}", [P, 8, B_STEPS]) for i in range(4)]

        loaded, c_loaded = sem("tm_loaded"), sem("tm_c_loaded")
        ident0, ident_ok = sem("tm_ident0"), sem("tm_ident_ok")
        exp_ok = sem("tm_exp_ok")
        steps, psteps = sem("tm_dve_steps"), sem("tm_pool_steps")
        pow_ok, cs_ok = sem("tm_pow_ok"), sem("tm_cs_ok")
        tr_done, tr_read = sem("tm_tr_done"), sem("tm_tr_read")
        x1_ok, x2_ok = sem("tm_x1_ok"), sem("tm_x2_ok")
        y_done, y_read = sem("tm_y_done"), sem("tm_y_read")
        y_stored = [sem("tm_y_stored_even"), sem("tm_y_stored_odd")]
        TR_HB = (B_STEPS + 2 * A_STEPS + 2 * NB) // 4

        block = ctx.enter_context(nc.Block())

        @block.sync
        def _(sp):
            sp.dma_start(dtc[:, :], log_dt.rearrange("(k p) -> p k", p=P), allow_slow_non_contiguous=True).then_inc(loaded, 16)
            sp.dma_start(ia[:, :, :], inv_a.rearrange("(k p) n -> p k n", p=P)).then_inc(loaded, 16)
            sp.dma_start(ai[:, :, :], a_imag.rearrange("(k p) n -> p k n", p=P)).then_inc(loaded, 16)
            sp.dma_start(bri[:, :, :, :], b_ri.rearrange("(k p) n r -> p k n r", p=P)).then_inc(loaded, 16)
            for hb in range(2):
                if hb:
                    sp.wait_ge(cs_ok, 1)
                sp.dma_start(cin[:, :, :, :], x_c[:, hb * P:(hb + 1) * P, :, :].rearrange("c h n r -> h c n r")
                             ).then_inc(c_loaded, 16)
            for i in range(2 * NBLK):
                sp.wait_ge(y_read, 2 * (i + 1))
                for c in range(NB):
                    sp.dma_start(seq[c, i * HBLK:(i + 1) * HBLK, :].rearrange("h (a b) -> a h b", b=B_STEPS),
                                 Y[c * A_STEPS:(c + 1) * A_STEPS, i % 2, :, :]).then_inc(y_stored[i % 2], 16)
            for stored in y_stored:
                sp.wait_ge(stored, 16 * NB * NBLK)

        @block.gpsimd
        def _(pool):
            pool.memset(ident[:, :], 0.0).then_inc(ident0, 1)
            pool.wait_ge(ident0, 1)
            pool.affine_select(out=ident[:, :], in_=ident[:, :], compare_op=ALU.not_equal, fill=1.0, base=0,
                               pattern=[[-1, P]], channel_multiplier=1).then_inc(ident_ok, 1)
            for hb in range(2):
                pool.wait_ge(c_loaded, 16 * (hb + 1))
                if hb:
                    pool.wait_ge(tr_done, TR_HB)
                for slot, r in ((0, 0), (1, 1), (2, 0)):
                    ins = pool.tensor_copy(cs[:, :, slot, :], cin[:, :, :, r])
                ins.then_inc(cs_ok, 1)
                for k in range(NBLK):
                    i = hb * NBLK + k
                    if k == 0:
                        pool.wait_ge(tr_read, TR_HB * (hb + 1))
                    if i >= 2:
                        pool.wait_ge(y_done, 2 * (i - 1))
                    hs = slice(k * HBLK, (k + 1) * HBLK)
                    pool.tensor_tensor(X2[:, i % 2, :, :, :],
                                       P2[:, hs, :].unsqueeze(3).broadcast_to([P, HBLK, NB, A_STEPS]),
                                       G2[:, hs, :].unsqueeze(2).broadcast_to([P, HBLK, NB, A_STEPS]),
                                       ALU.mult).then_inc(x2_ok, 1)

        @block.vector
        def _(dve):
            ch = Chain(dve, steps)
            link = ch.link
            tt = dve.tensor_tensor

            def mul(o, a, b):
                link(tt(o, a, b, ALU.mult))

            dve.wait_ge(loaded, 64)
            dve.wait_ge(exp_ok, 2)
            for hb in range(2):
                link(dve.tensor_scalar(s["zr"][:, hb, :], ea[:, hb, :], dt[:, hb:hb + 1], -0.5, ALU.mult, ALU.mult))
                link(dve.tensor_scalar(s["zi"][:, hb, :], ai[:, hb, :], dt[:, hb:hb + 1], 0.5, ALU.mult, ALU.mult))
            z = {k: v[:, :, :] for k, v in s.items()}
            mul(z["m"], z["zr"], z["zr"])
            mul(z["t"], z["zi"], z["zi"])
            link(tt(z["m"], z["m"], z["t"], ALU.add))
            link(dve.tensor_scalar(z["u"], z["zr"], -1.0, 1.0, ALU.mult, ALU.add))
            mul(z["v"], z["u"], z["u"])
            link(tt(z["den"], z["v"], z["t"], ALU.add))
            link(dve.reciprocal(z["r"], z["den"]))
            mul(z["gr"], z["u"], z["r"])
            mul(z["gi"], z["zi"], z["r"])
            link(dve.tensor_scalar(z["v"], z["m"], -1.0, 1.0, ALU.mult, ALU.add))
            mul(wr[:, 0, :, :], z["v"], z["r"])
            link(dve.tensor_scalar(wi[:, 0, :, :], z["gi"], 2.0, None, ALU.mult))
            br, bi = bri[:, :, :, 0], bri[:, :, :, 1]
            mul(z["u"], br, z["gr"])
            mul(z["v"], bi, z["gi"])
            link(tt(z["u"], z["u"], z["v"], ALU.subtract))
            mul(z["v"], br, z["gi"])
            mul(z["t"], bi, z["gr"])
            link(tt(z["v"], z["v"], z["t"], ALU.add))
            for hb in range(2):
                link(dve.tensor_scalar(s["fr"][:, hb, :], s["u"][:, hb, :], dt[:, hb:hb + 1], 2.0, ALU.mult, ALU.mult))
                link(dve.tensor_scalar(s["fi"][:, hb, :], s["v"][:, hb, :], dt[:, hb:hb + 1], 2.0, ALU.mult, ALU.mult))
            for k in range(1, NL):
                a, b = wr[:, k - 1, :, :], wi[:, k - 1, :, :]
                mul(z["u"], a, a)
                mul(z["v"], b, b)
                link(tt(wr[:, k, :, :], z["u"], z["v"], ALU.subtract))
                link(dve.scalar_tensor_tensor(out=wi[:, k, :, :], in0=a, scalar=2.0, in1=b, op0=ALU.mult, op1=ALU.mult))

            def times(o_re, o_im, a_re, a_im, k, hb, n):
                w_re = wr[:, k, hb, :].unsqueeze(1).broadcast_to([P, n, N])
                w_im = wi[:, k, hb, :].unsqueeze(1).broadcast_to([P, n, N])
                t1, t2 = T1[:, 0:n, :], T2[:, 0:n, :]
                tt(t1, a_re, w_re, ALU.mult)
                link(tt(t2, a_im, w_im, ALU.mult))
                link(tt(o_re, t1, t2, ALU.subtract))
                tt(t1, a_re, w_im, ALU.mult)
                link(tt(t2, a_im, w_re, ALU.mult))
                link(tt(o_im, t1, t2, ALU.add))

            for hb in range(2):
                if hb:
                    dve.wait_ge(tr_done, TR_HB)
                dve.memset(U[:, 0, 0, :], 1.0)
                link(dve.memset(U[:, 0, 1, :], 0.0))
                for k in range(6):
                    n = 1 << k
                    times(U[:, n:2 * n, 0, :], U[:, n:2 * n, 1, :], U[:, 0:n, 0, :], U[:, 0:n, 1, :], k, hb, n)
                dve.tensor_copy(G[:, 0, 0, :], s["fr"][:, hb, :])
                link(dve.tensor_copy(gi_[:, 0, :], s["fi"][:, hb, :]))
                for k in range(3):
                    n = 1 << k
                    times(G[:, n:2 * n, 0, :], gi_[:, n:2 * n, :], G[:, 0:n, 0, :], gi_[:, 0:n, :], 6 + k, hb, n)
                dve.tensor_scalar(G[:, :, 1, :], G[:, :, 0, :], -1.0, None, ALU.mult)
                dve.tensor_scalar(G[:, :, 2, :], gi_[:, :, :], -1.0, None, ALU.mult)
                dve.tensor_scalar(G[:, :, 3, :], gi_[:, :, :], -1.0, None, ALU.mult).then_inc(pow_ok, 1)
                for k in range(NBLK):
                    i = hb * NBLK + k
                    if k == 0:
                        dve.wait_ge(tr_read, TR_HB * (hb + 1))
                    if i >= 2:
                        dve.wait_ge(y_done, 2 * (i - 1))
                    hs = slice(k * HBLK, (k + 1) * HBLK)
                    tt(X1[:, i % 2, :, :, :], P1[:, hs, :].unsqueeze(3).broadcast_to([P, HBLK, NB, A_STEPS]),
                       G1[:, hs, :].unsqueeze(2).broadcast_to([P, HBLK, NB, A_STEPS]), ALU.mult).then_inc(x1_ok, 1)

        @block.tensor
        def _(pe):
            pe.wait_ge(ident_ok, 1)
            n = 0

            def four(sources):
                nonlocal n
                if n >= 2:
                    pe.wait_ge(tr_read, n - 1)
                for j, src in enumerate(sources):
                    ins = pe.transpose(tp[n % 2][:, j, :], src, ident[:, :])
                ins.then_inc(tr_done, 1)
                n += 1

            for hb in range(2):
                pe.wait_ge(cs_ok, hb + 1)
                for q in range(NB // 4):
                    four([cs[:, 4 * q + j, 0:2, :] for j in range(4)])
                for q in range(NB // 4):
                    four([cs[:, 4 * q + j, 1:3, :] for j in range(4)])
                pe.wait_ge(pow_ok, hb + 1)
                for q in range(A_STEPS // 4):
                    four([G[:, 4 * q + j, 0:2, :] for j in range(4)])
                for q in range(A_STEPS // 4):
                    four([G[:, 4 * q + j, 2:4, :] for j in range(4)])
                for q in range(B_STEPS // 4):
                    four([U[:, 4 * q + j, :, :] for j in range(4)])
                pe.wait_ge(tr_read, TR_HB * (hb + 1))
                for k in range(NBLK):
                    i = hb * NBLK + k
                    pe.wait_ge(x1_ok, i + 1)
                    pe.wait_ge(x2_ok, i + 1)
                    for half in range(2):
                        g = 2 * i + half
                        if g >= 4:
                            pe.wait_ge(y_read, g - 3)
                        for j in range(8):
                            h = half * 8 + j
                            rhs = UT[:, k * HBLK + h, :]
                            pe.matmul(yp[g % 4][:, j, :], X1[:, i % 2, h, :, :], rhs, start=True, stop=False)
                            ins = pe.matmul(yp[g % 4][:, j, :], X2[:, i % 2, h, :, :], rhs, start=False, stop=True)
                        ins.then_inc(y_done, 1)

        @block.scalar
        def _(act):
            act.wait_ge(loaded, 64)
            act.activation(dt[:, :], dtc[:, :], ACT.Exp).then_inc(exp_ok, 1)
            act.activation(ea[:, :, :], ia[:, :, :], ACT.Exp).then_inc(exp_ok, 1)
            n = 0
            for hb in range(2):
                for dst, count in ((P1, NB), (P2, NB), (G1, A_STEPS), (G2, A_STEPS), (UT, B_STEPS)):
                    for q in range(count // 4):
                        act.wait_ge(tr_done, n + 1)
                        if hb and q == 0:
                            act.wait_ge(y_done, 2 * NBLK)
                        act.activation(dst[:, :, 4 * q:4 * q + 4].rearrange("p h j -> p j h"), tp[n % 2][:, :, :],
                                       ACT.Copy).then_inc(tr_read, 1)
                        n += 1
                for k in range(NBLK):
                    i = hb * NBLK + k
                    if i >= 2:
                        act.wait_ge(y_stored[i % 2], 16 * NB * (i // 2))
                    for half in range(2):
                        g = 2 * i + half
                        act.wait_ge(y_done, g + 1)
                        act.activation(Y[:, i % 2, half * 8:half * 8 + 8, :], yp[g % 4][:, :, :],
                                       ACT.Copy).then_inc(y_read, 1)




def attention_weights(nc, A, W):
    with ExitStack() as ctx:
        def sb(name, shape, dt=F32):
            return ctx.enter_context(nc.sbuf_tensor(name, shape, dt))

        def sem(name):
            return ctx.enter_context(nc.semaphore(name))

        ident = W["ident"]
        wkv = sb("wkv_up", [P, NH, 2, HD])
        wqu = sb("wq_up", [P, KQ, NH, HD])
        wo = sb("wo", [P, NH, D])
        wr = sb("wq_rope", [P, KQ, GROUPS, P, 2])
        qw = sb("q_norm", [P, KQ])
        kw = sb("kv_norm", [P, 1])
        qws = sb("q_norm_scaled", [P, KQ])
        qwr = sb("q_norm_rope", [P, KQ])
        qkT = sb("qkT", [P, 2, 4, P])
        vT = sb("vT", [P, 2, P])
        wt = sb("w_nope", [P, 2, KQ, P])
        vt = sb("w_out", [P, 2, D])
        tq = [ctx.enter_context(nc.psum_tensor(f"aw_tq{i}", [P, 4, P], F32)) for i in range(2)]
        tv = [ctx.enter_context(nc.psum_tensor(f"aw_tv{i}", [P, 4, P], F32)) for i in range(2)]
        vo = [ctx.enter_context(nc.psum_tensor(f"aw_vo{i}", [P, D], F32)) for i in range(2)]
        kv_in, q_in, o_in, r_in, small_in, keep_in = (sem("aw_" + n) for n in
                                                      ("kv_in", "q_in", "o_in", "r_in", "small_in", "keep_in"))
        kv_ok, qw_ok = sem("aw_kv_ok"), sem("aw_qw_ok")
        tr_ok, tr_sb = sem("aw_tr_ok"), sem("aw_tr_sb")
        prod, wt_ok, vt_ok = sem("aw_prod"), sem("aw_wt_ok"), sem("aw_vt_ok")
        hi_ok, lo_ok, rs_ok, rh_ok, rl_ok = (sem("aw_" + n) for n in ("hi", "lo", "rs", "rh", "rl"))
        block = ctx.enter_context(nc.Block())

        @block.sync
        def _(sp):
            sp.dma_start(kw[:, :], A["kv_norm_w"].rearrange("(p o) -> p o", o=1)).then_inc(small_in, 16)
            sp.dma_start(qw[:, :], A["q_norm_w"].rearrange("(k p) -> p k", p=P),
                         allow_slow_non_contiguous=True).then_inc(small_in, 16)
            sp.dma_start(wkv[:, :, :, :], A["wkv_up"].rearrange("p (h t d) -> p h t d", h=NH, t=2)).then_inc(kv_in, 16)
            sp.dma_start(wqu[:, :, :, :], A["wq_up"].rearrange("(k p) (h d) -> p k h d", p=P, h=NH)).then_inc(q_in, 16)
            sp.dma_start(wo[:, :, :], A["wo"].rearrange("(h p) n -> p h n", p=P)).then_inc(o_in, 16)
            sp.dma_start(wr[:, :, :, :, :], A["wq_rope"].rearrange("(k p) (g m c) -> p k g m c", p=P, g=GROUPS, c=2)
                         ).then_inc(r_in, 16)
            for col, name in ((0, "wq_down"), (QR, "wkv_down"), (QR + KV, "wk_rope")):
                n = A[name].shape[1]
                sp.dma_start(W["down"][:, :, col:col + n], A[name].rearrange("(k p) n -> p k n", p=P)
                             ).then_inc(keep_in, 16)
            for name in ("qcos", "qsin", "kcos", "ksin"):
                sp.dma_start(W[name], A[name]).then_inc(keep_in, 16)
            sp.wait_ge(keep_in, 16 * 7)

        @block.tensor
        def _(pe):
            pe.wait_ge(q_in, 16)
            pe.wait_ge(kv_ok, 1)
            for h in range(NH + 1):
                if h < NH:
                    i = h % 2
                    if h >= 2:
                        pe.wait_ge(wt_ok, h - 1)
                    for k in range(KQ):
                        pe.transpose(tq[i][:, k, :], wqu[:, k, h, :], ident[:, :])
                    pe.transpose(tq[i][:, 3, :], wkv[:, h, 0, :], ident[:, :])
                    pe.transpose(tv[i][:, 0, :], wkv[:, h, 1, :], ident[:, :]).then_inc(tr_ok, 1)
                if h >= 1:
                    g, i = h - 1, (h - 1) % 2
                    pe.wait_ge(tr_sb, 2 * (g + 1))
                    if g == 0:
                        pe.wait_ge(o_in, 16)
                    if g >= 2:
                        pe.wait_ge(vt_ok, g - 1)
                    for k in range(KQ):
                        pe.matmul(tv[i][:, 1 + k, :], qkT[:, i, k, :], qkT[:, i, 3, :], start=True, stop=True)
                    pe.matmul(vo[i][:, :], vT[:, i, :], wo[:, g, :], start=True, stop=True).then_inc(prod, 1)

        @block.scalar
        def _(act):
            for h in range(NH + 1):
                if h < NH:
                    i = h % 2
                    act.wait_ge(tr_ok, h + 1)
                    if h >= 2:
                        act.wait_ge(prod, h - 1)
                    act.activation(qkT[:, i, :, :], tq[i][:, :, :], ACT.Copy).then_inc(tr_sb, 1)
                    act.activation(vT[:, i, :], tv[i][:, 0, :], ACT.Copy).then_inc(tr_sb, 1)
                if h >= 1:
                    g, i = h - 1, (h - 1) % 2
                    act.wait_ge(prod, g + 1)
                    if g >= 2:
                        act.wait_ge(lo_ok, 2 * (g - 1))
                    act.activation(vt[:, i, :], vo[i][:, :], ACT.Copy, scale=S_VO).then_inc(vt_ok, 1)

        @block.vector
        def _(dve):
            dve.wait_ge(small_in, 32)
            dve.tensor_scalar(qws[:, :], qw[:, :], S_NOPE, None, ALU.mult)
            dve.tensor_scalar(qwr[:, :], qw[:, :], S_RQ, None, ALU.mult).then_inc(qw_ok, 1)
            dve.wait_ge(kv_in, 16)
            dve.tensor_scalar(wkv[:, :, :, :], wkv[:, :, :, :], kw[:, 0:1], None, ALU.mult).then_inc(kv_ok, 1)
            dve.wait_ge(r_in, 16)
            dve.wait_ge(qw_ok, 1)
            for k in range(KQ):
                dve.tensor_scalar(wr[:, k, :, :, :], wr[:, k, :, :, :], qwr[:, k:k + 1], None, ALU.mult).then_inc(rs_ok, 1)
            dve.wait_ge(rs_ok, KQ)
            for k in range(KQ):
                for c in range(2):
                    dve.tensor_copy(W["ropeH"][:, k, :, c, :], wr[:, k, :, :, c]).then_inc(rh_ok, 1)
            for h in range(NH):
                i = h % 2
                dve.wait_ge(prod, h + 1)
                if h >= 2:
                    dve.wait_ge(lo_ok, 2 * (h - 1))
                dve.tensor_tensor(wt[:, i, :, :], tv[i][:, 1:4, :],
                                  qws[:, :].unsqueeze(2).broadcast_to([P, KQ, P]), ALU.mult).then_inc(wt_ok, 1)
                dve.wait_ge(wt_ok, h + 1)
                dve.tensor_copy(W["nopeH"][:, :, h, :], wt[:, i, :, :]).then_inc(hi_ok, 1)
                dve.wait_ge(vt_ok, h + 1)
                dve.tensor_copy(W["outH"][:, h, :], vt[:, i, :]).then_inc(hi_ok, 1)

        @block.gpsimd
        def _(pool):
            for k in range(KQ):
                for c in range(2):
                    pool.wait_ge(rh_ok, 2 * k + c + 1)
                    pool.tensor_tensor(W["ropeL"][:, k, :, c, :], wr[:, k, :, :, c], W["ropeH"][:, k, :, c, :],
                                       ALU.subtract).then_inc(rl_ok, 1)
            for h in range(NH):
                i = h % 2
                pool.wait_ge(hi_ok, 2 * h + 1)
                pool.tensor_tensor(W["nopeL"][:, :, h, :], wt[:, i, :, :], W["nopeH"][:, :, h, :],
                                   ALU.subtract).then_inc(lo_ok, 1)
                pool.wait_ge(hi_ok, 2 * h + 2)
                pool.tensor_tensor(W["outL"][:, h, :], vt[:, i, :], W["outH"][:, h, :],
                                   ALU.subtract).then_inc(lo_ok, 1)


def ffn_weights(nc, A, W):
    with ExitStack() as ctx:
        def sb(name, shape, dt=F32):
            return ctx.enter_context(nc.sbuf_tensor(name, shape, dt))

        def sem(name):
            return ctx.enter_context(nc.semaphore(name))

        ident, ident16 = W["ident"], W["ident16"]
        TILES = 2 * KF + KD
        RING = 3
        idx = sb("hidden_order", [P, KF], I32)
        raw = sb("fw_raw", [P, RING, FF])
        y = sb("fw_y", [P, 2, FF])
        e = sb("fw_e", [P, 2, FF])
        q16 = sb("fw_q", [P, 2, FF], BF16)
        am = sb("fw_absmax", [P, TILES])
        ws = sb("fw_scale", [P, TILES])
        rs = sb("fw_rscale", [P, TILES])
        diag = sb("fw_diag", [P, 2, P])
        ones = sb("fw_ones", [P, P])
        tp = [ctx.enter_context(nc.psum_tensor(f"fw_tp{i}", [P, 8, P], BF16)) for i in range(4)]
        sp_ = [ctx.enter_context(nc.psum_tensor(f"fw_sp{i}", [P, P], F32)) for i in range(2)]
        idx_in = sem("fw_idx_in")
        raw_in = [sem(f"fw_raw_in{i}") for i in range(RING)]
        steps, y_ok, m_ok = sem("fw_steps"), sem("fw_y_ok"), sem("fw_m_ok")
        t_ok, q_ok, ones_ok, diag_ok = sem("fw_t_ok"), sem("fw_q_ok"), sem("fw_ones_ok"), sem("fw_diag_ok")
        tr_ok, tr_read, sc_ok, sc_read = sem("fw_tr_ok"), sem("fw_tr_read"), sem("fw_sc_ok"), sem("fw_sc_read")
        block = ctx.enter_context(nc.Block())

        def width(n):
            return D if n < 2 * KF else FF

        def halves(n):
            k = width(n) // P
            return [(0, k)] if k <= 8 else [(0, 8), (8, k)]

        banks = [sum(len(halves(m)) for m in range(n)) for n in range(TILES + 1)]

        @block.sync
        def _(sp):
            sp.dma_start(idx[:, :], A["down_reorder_index"].rearrange("(m p) -> p m", p=P),
                         allow_slow_non_contiguous=True).then_inc(idx_in, 16)
            sp.wait_ge(idx_in, 16)

        @block.gpsimd
        def _(pool):
            pool.memset(ones[:, :], 1.0).then_inc(ones_ok, 1)
            pool.wait_ge(idx_in, 16)

            def fetch(n):
                if n >= RING:
                    pool.wait_ge(y_ok, n - RING + 1)
                if n < 2 * KF:
                    src = A["w_gate"] if n < KF else A["w_up"]
                    m = n % KF
                    pool.indirect_dma_start(raw[:, n % RING, 0:D], None, src,
                                            bass.IndirectOffsetOnAxis(ap=idx[:, m:m + 1].bitcast(U32), axis=0)
                                            ).then_inc(raw_in[n % RING], 16)
                else:
                    m = n - 2 * KF
                    pool.dma_start(raw[:, n % RING, :], A["w_down"][m * P:(m + 1) * P, :]).then_inc(raw_in[n % RING], 16)

            for n in range(RING):
                fetch(n)
            for n in range(TILES):
                i, w = n % 2, width(n)
                pool.wait_ge(m_ok, n + 1)
                pool.tensor_tensor(y[:, i, 0:w], y[:, i, 0:w], e[:, i, 0:w], ALU.add).then_inc(t_ok, 1)
                pool.wait_ge(t_ok, n + 1)
                if n >= 2:
                    pool.wait_ge(tr_ok, banks[n - 1])
                pool.tensor_tensor(q16[:, i, 0:w], y[:, i, 0:w], e[:, i, 0:w], ALU.subtract).then_inc(q_ok, 1)
                if n >= 2:
                    pool.wait_ge(sc_ok, n - 1)
                pool.tensor_tensor(diag[:, i, :], ident[:, :], ws[:, n:n + 1].broadcast_to([P, P]),
                                   ALU.mult).then_inc(diag_ok, 1)
                if n + RING < TILES:
                    fetch(n + RING)

        @block.vector
        def _(dve):
            ch = Chain(dve, steps)
            for n in range(TILES):
                i, w = n % 2, width(n)
                src = raw[:, n % RING, 0:w]
                dve.wait_ge(raw_in[n % RING], 16 * (n // RING + 1))
                ch.link(dve.tensor_reduce(am[:, n:n + 1], src, AX.X, ALU.max, apply_absolute_value=True))
                ch.link(dve.tensor_scalar(ws[:, n:n + 1], am[:, n:n + 1], 1.0 / FP8_MAX, None, ALU.mult))
                ch.link(dve.reciprocal(rs[:, n:n + 1], ws[:, n:n + 1]))
                if n >= 2:
                    dve.wait_ge(q_ok, n - 1)
                dve.tensor_scalar(y[:, i, 0:w], src, rs[:, n:n + 1], None, ALU.mult).then_inc(y_ok, 1)
                dve.wait_ge(y_ok, n + 1)
                exponent_power(dve, ch, e[:, i, 0:w], y[:, i, 0:w]).then_inc(m_ok, 1)

        @block.tensor
        def _(pe):
            for n in range(TILES):
                i = n % 2
                pe.wait_ge(q_ok, n + 1)
                for k0, k1 in halves(n):
                    j = banks[n] + (k0 > 0)
                    if j >= 4:
                        pe.wait_ge(tr_read, j - 3)
                    for k in range(k0, k1):
                        ins = pe.transpose(tp[j % 4][:, k - k0, :], q16[:, i, k * P:(k + 1) * P], ident16[:, :])
                    ins.then_inc(tr_ok, 1)
                pe.wait_ge(diag_ok, n + 1)
                if n == 0:
                    pe.wait_ge(ones_ok, 1)
                if n >= 2:
                    pe.wait_ge(sc_read, n - 1)
                pe.matmul(sp_[i][:, :], ones[:, :], diag[:, i, :], start=True, stop=True).then_inc(sc_ok, 1)

        @block.scalar
        def _(act):
            for n in range(TILES):
                i = n % 2
                m = n % KF if n < 2 * KF else n - 2 * KF
                dst = W["gate"] if n < KF else W["up"] if n < 2 * KF else W["ffn_down"]
                for k0, k1 in halves(n):
                    j = banks[n] + (k0 > 0)
                    act.wait_ge(tr_ok, j + 1)
                    act.activation(dst[:, k0:k1, m * P:(m + 1) * P], tp[j % 4][:, 0:k1 - k0, :],
                                   ACT.Copy).then_inc(tr_read, 1)
                row = W["gate_s"] if n < KF else W["up_s"] if n < 2 * KF else W["down_s"]
                act.wait_ge(sc_ok, n + 1)
                act.activation(row[:, m * P:(m + 1) * P], sp_[i][:, :], ACT.Copy).then_inc(sc_read, 1)


def exponent_power(dve, ch, e, y):
    ch.link(dve.tensor_scalar(e.bitcast(U32), y.bitcast(U32), EXPONENT_BITS, None, ALU.bitwise_and))
    return dve.tensor_scalar(e, e, LEAST_NORMAL, ROUNDER, ALU.max, ALU.mult)


def ffn_scratch(nc, ctx, W):
    for name, shape, dt in (("gate", [P, KD, FF], BF16), ("up", [P, KD, FF], BF16), ("ffn_down", [P, KF, D], BF16),
                            ("gate_s", [P, FF], F32), ("up_s", [P, FF], F32), ("down_s", [P, D], F32)):
        W[name] = ctx.enter_context(nc.sbuf_tensor("kept_" + name, shape, dt))


def scratch(nc, ctx):
    def sb(name, shape, dt=F32):
        return ctx.enter_context(nc.sbuf_tensor(name, shape, dt))

    W = {
        "ident": sb("ident", [P, P]), "ident16": sb("ident16", [P, P], BF16),
        "mask": sb("causal_mask", [P, P], BF16),
        "nopeH": sb("nopeH", [P, KQ, NH, P], F16), "nopeL": sb("nopeL", [P, KQ, NH, P], F16),
        "ropeH": sb("ropeH", [P, KQ, GROUPS, 2, P], F16), "ropeL": sb("ropeL", [P, KQ, GROUPS, 2, P], F16),
        "outH": sb("outH", [P, NH, D], F16), "outL": sb("outL", [P, NH, D], F16),
        "down": sb("w_latents", [P, KD, QR + KV + RD]),
    }
    for name, shape in (("qcos", [P, S]), ("qsin", [P, S]), ("kcos", [P, NT, RD // 2]), ("ksin", [P, NT, RD // 2])):
        t = sb(name, shape)
        W[name] = t[:, :] if len(shape) == 2 else t[:, :, :]
    sem = ctx.enter_context(nc.semaphore("constants"))
    with nc.Block() as block:
        @block.gpsimd
        def _(pool):
            pool.memset(W["ident"][:, :], 0.0)
            pool.memset(W["ident16"][:, :], 0.0)
            pool.memset(W["mask"][:, :], 0.0).then_inc(sem, 1)
            pool.wait_ge(sem, 1)
            for name in ("ident", "ident16"):
                t = W[name][:, :]
                pool.affine_select(out=t, in_=t, compare_op=ALU.not_equal, fill=1.0, base=0,
                                   pattern=[[-1, P]], channel_multiplier=1)
            t = W["mask"][:, :]
            pool.affine_select(out=t, in_=t, compare_op=ALU.is_ge, fill=MASK, base=0,
                               pattern=[[-1, P]], channel_multiplier=1).then_inc(sem, 1)
            pool.wait_ge(sem, 2)
    return W


def layer(nc, A, W, seq, out):
    with ExitStack() as ctx:
        def sb(name, shape, dt=F32):
            return ctx.enter_context(nc.sbuf_tensor(name, shape, dt))

        sems = []

        def sem(name):
            sems.append(ctx.enter_context(nc.semaphore(name)))
            return sems[-1]

        ident, ident16 = W["ident"], W["ident16"]
        room = sb("room", [P, 2 * FF])
        x = room[:, 0:NT * D].rearrange("p (n l) -> p n l", n=NT)
        xT = room[:, NT * D:NT * D + KD * S].rearrange("p (k s) -> p k s", k=KD)
        ssq = sb("ssq", [P, 4])
        msq, rstd = sb("mean_square", [P, 4]), sb("rstd", [P, 4])
        minus_half, zeros = sb("minus_half", [P, 4]), sb("zeros", [P, 1])
        qn = room[:, 0:NT * QR].rearrange("p (n l) -> p n l", n=NT)
        kn = room[:, NT * QR:NT * (QR + KV)].rearrange("p (n l) -> p n l", n=NT)
        vH, vL = sb("vH", [P, NT, KV], F16), sb("vL", [P, NT, KV], F16)
        free = NT * D + KD * S
        kr = room[:, free:free + NT * 2 * RD].rearrange("p (n r c i) -> p n r c i", n=NT, r=2, c=2)
        squares = room[:, free + NT * 2 * RD:2 * FF].bitcast(BF16)
        ka, kb = sb("k_rope_a", [P, 2, NT, RD // 2]), sb("k_rope_b", [P, 2, NT, RD // 2])
        qnH, qnL = sb("qnH", [P, KQ, S], F16), sb("qnL", [P, KQ, S], F16)
        knH, knL = sb("knH", [P, S], F16), sb("knL", [P, S], F16)
        krH, krL = sb("krH", [P, S], F16), sb("krL", [P, S], F16)
        tc, ts = sb("ab_cos", [P, 2, S]), sb("ab_sin", [P, 2, S])
        ro = sb("rope_out", [P, 2, S])
        roH, roL = sb("ropeH_out", [P, 2, S], F16), sb("ropeL_out", [P, 2, S], F16)
        qr = sb("q_rope", [P, NH, S], F16)
        qpH, qpL = sb("qpH", [P, 2, 2, S], F16), sb("qpL", [P, 2, 2, S], F16)
        nmax = sb("nmax", [P, 2, NT, 2])
        rsum, rinv = sb("rsum", [P, 2, NT, 2]), sb("rinv", [P, 2, NT, 2])
        pr = sb("probs", [P, 2, 2, P + S])
        ptH, ptL = sb("ptH", [P, 2, P + S], F16), sb("ptL", [P, 2, P + S], F16)
        oH, oL = sb("oH", [P, NH, S], F16), sb("oL", [P, NH, S], F16)
        res = sb("residual", [P, NT, D])
        st6 = sb("bn_stats", [P, NT, 6])
        mv = sb("mean_var", [P, NT, 2])
        veps, lrs = sb("var_eps", [P, NT]), sb("ln_rstd", [P, NT])
        am, sx, rsx = sb("absmax", [P, NT]), sb("x_scale", [P, NT]), sb("x_rscale", [P, NT])
        hsx = sb("half_x_scale", [P, NT])
        HF = FF // 2
        y, e = room[:, FF:FF + HF], room[:, FF + HF:2 * FF]
        t = room[:, 0:FF]
        xq = room[:, 0:NT * D // 2].bitcast(BF16).rearrange("p (n l) -> p n l", n=NT)
        xqT = sb("xqT", [P, KD, S], BF16)
        g1, u1 = sb("g1", [P, 2, CH]), sb("u1", [P, 2, CH])
        tm, tsc, trs, tst = (sb(n, [P, NT]) for n in ("t_absmax", "t_scale", "t_rscale", "t_out_scale"))
        tq = sb("tq", [P, FF], BF16)
        tqT = sb("tqT", [P, KF, P], BF16)

        G = [ctx.enter_context(nc.psum_tensor(f"G{i}", [P, 512], F32)) for i in range(3)]
        SB = [ctx.enter_context(nc.psum_tensor(f"scores{i}", [P, 512], F32)) for i in range(2)]
        PT = ctx.enter_context(nc.psum_tensor("probsT", [P, P + S], F32))
        OT = ctx.enter_context(nc.psum_tensor("outT", [P, 2, S], F32))
        QP = ctx.enter_context(nc.psum_tensor("projections", [P, 2, S], F32))

        x_in, res_in = sem("x_in"), sem("res_in")
        half_ok, msq_ok, rstd_ok, var_ok, lrs_ok = (sem(n) for n in ("half_ok", "msq_ok", "rstd_ok", "var_ok", "lrs_ok"))
        xT_ps, xT_sb, lat_ps, ssq_ok = sem("xT_ps"), sem("xT_sb"), sem("lat_ps"), sem("ssq_ok")
        lat_sb, latT_ps, latT_hi, latT_lo = sem("lat_sb"), sem("latT_ps"), sem("latT_hi"), sem("latT_lo")
        ab_ps, ab_read, ro_ok, roh_ok, rol_ok = (sem(n) for n in ("ab_ps", "ab_read", "ro_ok", "roh_ok", "rol_ok"))
        qr_in = [sem(f"qr_in{g}") for g in range(GROUPS)]
        qp_ps, qp_hi, qp_lo = sem("qp_ps"), sem("qp_hi"), sem("qp_lo")
        s_ps, s_max, p_exp, p_inv, p_norm = (sem(n) for n in ("s_ps", "s_max", "p_exp", "p_inv", "p_norm"))
        pt_ps, pt_hi, pt_lo, o_ps, o_hi, o_lo = (sem(n) for n in ("pt_ps", "pt_hi", "pt_lo", "o_ps", "o_hi", "o_lo"))
        y_ps, h_ok, xq_ok, xqT_ps, xqT_sb = (sem(n) for n in ("y_ps", "h_ok", "xq_ok", "xqT_ps", "xqT_sb"))
        gu_ps, g1_ok, u1_ok, th_ok, gu_free, t_ok = (sem(n) for n in ("gu_ps", "g1_ok", "u1_ok", "th_ok", "gu_free", "t_ok"))
        m_ok, r_ok, tq_ok, tqT_ps, tqT_sb, d_ps, out_ok = (
            sem(n) for n in ("m_ok", "r_ok", "tq_ok", "tqT_ps", "tqT_sb", "d_ps", "out_ok"))
        out_in = sem("out_in")
        steps, stats_ok = sem("dve_steps"), sem("stats_ok")
        DVE_STEPS = 67
        N_GU = 2 * NCH * NT
        with nc.Block() as priming:
            @priming.sync
            def _(sp):
                for s in sems:
                    sp.sem_inc(s, PRIMED)
        block = ctx.enter_context(nc.Block())

        @block.sync
        def _(sp):
            with sp.Fori(0, NB) as b:
                tokens = seq[bass.ds(b, 1), :, :].rearrange("o (t p) l -> p (o t) l", p=P)
                result = out[bass.ds(b, 1), :, :].rearrange("o (t p) l -> p (o t) l", p=P)
                sp.wait_ge(out_ok, PRIMED + NT * b)
                sp.dma_start(x[:, :, :], tokens).then_inc(x_in, 16)
                for g in range(GROUPS):
                    sp.wait_ge(rol_ok, PRIMED + GROUPS * b + g + 1)
                    for part, src in ((0, roH), (1, roL)):
                        for c in range(2):
                            for j in range(4):
                                row = 64 * part + 32 * c
                                sp.dma_start(qr[row:row + 32, 4 * g + j, :], src[32 * j:32 * j + 32, c, :]
                                             ).then_inc(qr_in[g], 16)
                sp.wait_ge(out_in, PRIMED + 16 * b)
                sp.dma_start(res[:, :, :], tokens).then_inc(res_in, 16)
                sp.wait_ge(out_ok, PRIMED + NT * (b + 1))
                sp.dma_start(result, res[:, :, :]).then_inc(out_in, 16)
            sp.wait_ge(out_in, PRIMED + 16 * NB)

        @block.tensor
        def _(pe):
            def split_product(dst, aH, aL, bH, bL, first, last):
                pe.matmul(dst, aH, bH, start=first, stop=False)
                pe.matmul(dst, aH, bL, start=False, stop=False)
                return pe.matmul(dst, aL, bH, start=False, stop=last)

            def latents(b):
                pe.wait_ge(x_in, PRIMED + 16 * (b + 1))
                pe.wait_ge(out_ok, PRIMED + NT * b)
                for i in range(2):
                    for k in range(2):
                        for n in range(NT):
                            ins = pe.transpose(G[i][:, k * S + n * P:k * S + (n + 1) * P],
                                               x[:, n, (2 * i + k) * P:(2 * i + k + 1) * P], ident[:, :])
                    ins.then_inc(xT_ps, 1)
                pe.wait_ge(xT_sb, PRIMED + 2 * b + 2)
                for n in range(NT):
                    for k in range(KD):
                        ins = pe.matmul(G[n][:, 0:QR], xT[:, k, n * P:(n + 1) * P], W["down"][:, k, 0:QR],
                                        start=(k == 0), stop=(k == KD - 1))
                    ins.then_inc(lat_ps, 1)
                for n in range(NT):
                    for k in range(KD):
                        ins = pe.matmul(G[2][:, n * (KV + RD):(n + 1) * (KV + RD)], xT[:, k, n * P:(n + 1) * P],
                                        W["down"][:, k, QR:], start=(k == 0), stop=(k == KD - 1))
                ins.then_inc(lat_ps, 1)
                pe.wait_ge(lat_sb, PRIMED + b + 1)
                for i in range(2):
                    for k in range(2):
                        for n in range(NT):
                            m = 2 * i + k
                            src = qn[:, n, m * P:(m + 1) * P] if m < KQ else kn[:, n, :]
                            ins = pe.transpose(G[i][:, k * S + n * P:k * S + (n + 1) * P], src, ident[:, :])
                    ins.then_inc(latT_ps, 1)
                for n in range(NT):
                    ins = pe.transpose(G[2][:, n * P:(n + 1) * P], kr[:, n, :, :, :], ident[:, :])
                ins.then_inc(latT_ps, 1)

            def project(dst, wH, wL):
                for k in range(KQ):
                    ins = split_product(dst, wH(k), wL(k), qnH[:, k, :], qnL[:, k, :], k == 0, k == KQ - 1)
                return ins

            def projections_free(b, qps, abs_):
                pe.wait_ge(qp_lo, PRIMED + PAIRS * b + qps)
                pe.wait_ge(ab_read, PRIMED + GROUPS * b + abs_)

            def group(b, g, qps):
                if g == 0:
                    pe.wait_ge(latT_hi, PRIMED + 3 * b + 3)
                    pe.wait_ge(latT_lo, PRIMED + 3 * b + 3)
                projections_free(b, qps, g)
                for c in range(2):
                    ins = project(QP[:, c, :], lambda k: W["ropeH"][:, k, g, c, :], lambda k: W["ropeL"][:, k, g, c, :])
                ins.then_inc(ab_ps, 1)

            def pair_queries(b, i, abs_):
                projections_free(b, i, abs_)
                for c in range(2):
                    h = 2 * i + c
                    ins = project(QP[:, c, :], lambda k: W["nopeH"][:, k, h, :], lambda k: W["nopeL"][:, k, h, :])
                ins.then_inc(qp_ps, 1)

            def scores(b, i):
                pe.wait_ge(qp_hi, PRIMED + PAIRS * b + i + 1)
                pe.wait_ge(qp_lo, PRIMED + PAIRS * b + i + 1)
                if i % 2 == 0:
                    pe.wait_ge(qr_in[i // 2], PRIMED + 256 * (b + 1))
                pe.wait_ge(p_exp, PRIMED + PAIRS * b + i)
                for c in range(2):
                    h = 2 * i + c
                    for n in range(NT):
                        keys = slice(0, (n + 1) * P)
                        cols = slice(n * P, n * P + (n + 1) * P)
                        dst = SB[c][:, cols]
                        q = slice(n * P, (n + 1) * P)
                        split_product(dst, qpH[:, i % 2, c, q], qpL[:, i % 2, c, q], knH[:, keys], knL[:, keys], True, False)
                        pe.matmul(dst, qr[:, h, q], krH[:, keys], start=False, stop=False)
                        pe.matmul(dst, qr[0:64, h, q], krL[0:64, keys], start=False, stop=False)
                        ins = pe.matmul(SB[c][:, cols.stop - P:cols.stop], ident16[:, :], W["mask"][:, :],
                                        start=False, stop=True)
                    ins.then_inc(s_ps, 1)

            def turn_probs(b, h):
                i, c = h // 2, h % 2
                pe.wait_ge(p_norm, PRIMED + PAIRS * b + i + 1)
                pe.wait_ge(pt_hi, PRIMED + NH * b + h)
                pe.wait_ge(pt_lo, PRIMED + NH * b + h)
                for k in range(3):
                    ins = pe.transpose(PT[:, k * P:(k + 1) * P], pr[:, i % 2, c, k * P:(k + 1) * P], ident[:, :])
                ins.then_inc(pt_ps, 1)

            def values(b, h):
                i, c = h // 2, h % 2
                pe.wait_ge(pt_hi, PRIMED + NH * b + h + 1)
                pe.wait_ge(pt_lo, PRIMED + NH * b + h + 1)
                if c == 0:
                    pe.wait_ge(o_hi, PRIMED + PAIRS * b + i)
                    pe.wait_ge(o_lo, PRIMED + PAIRS * b + i)
                split_product(OT[:, c, :], vH[:, 0, :], vL[:, 0, :], ptH[:, c, 0:S], ptL[:, c, 0:S], True, False)
                ins = split_product(OT[:, c, P:S], vH[:, 1, :], vL[:, 1, :], ptH[:, c, S:], ptL[:, c, S:], False, True)
                ins.then_inc(o_ps, 1)

            def output(b):
                pe.wait_ge(o_hi, PRIMED + PAIRS * (b + 1))
                pe.wait_ge(o_lo, PRIMED + PAIRS * (b + 1))
                for n in range(NT):
                    q = slice(n * P, (n + 1) * P)
                    for h in range(NH):
                        ins = split_product(G[n][:, :], oH[:, h, q], oL[:, h, q], W["outH"][:, h, :],
                                            W["outL"][:, h, :], h == 0, h == NH - 1)
                    ins.then_inc(y_ps, 1)

            def turn_input(b):
                pe.wait_ge(xq_ok, PRIMED + NT * (b + 1))
                dst = G[2][:, :].bitcast(BF16).rearrange("p (k s) -> p k s", k=KD)
                for n in range(NT):
                    for k in range(KD):
                        ins = pe.transpose(dst[:, k, n * P:(n + 1) * P], xq[:, n, k * P:(k + 1) * P], ident16[:, :])
                ins.then_inc(xqT_ps, 1)

            def gate_up(b, n):
                if n == 0:
                    pe.wait_ge(xqT_sb, PRIMED + b + 1)
                for c in range(NCH):
                    for r, w in enumerate((W["gate"], W["up"])):
                        u = (n * NCH + c) * 2 + r
                        if u >= 3:
                            pe.wait_ge(gu_free, PRIMED + N_GU * b + u - 2)
                        if n == 1 and u == N_GU // 2:
                            pe.wait_ge(tqT_sb, PRIMED + 2 * NT * b + 2)
                        if n == 1 and u - N_GU // 2 < 3:
                            pe.wait_ge(out_ok, PRIMED + NT * b + 1)
                        for k in range(KD):
                            ins = pe.matmul(G[u % 3][:, 0:CH], xqT[:, k, n * P:(n + 1) * P],
                                            w[:, k, c * CH:(c + 1) * CH], start=(k == 0), stop=(k == KD - 1))
                        ins.then_inc(gu_ps, 1)

            def ffn_out(b, n):
                pe.wait_ge(tq_ok, PRIMED + NT * b + n + 1)
                pe.wait_ge(gu_free, PRIMED + N_GU * b + N_GU // NT * (n + 1))
                d0 = G[0][:, :].bitcast(BF16).rearrange("p (k s) -> p k s", s=P)
                d1 = G[1][:, :].bitcast(BF16).rearrange("p (k s) -> p k s", s=P)
                for m in range(KF):
                    dst = d0[:, m, :] if m < 8 else d1[:, m - 8, :]
                    ins = pe.transpose(dst, tq[:, m * P:(m + 1) * P], ident16[:, :])
                    if m in (7, KF - 1):
                        ins.then_inc(tqT_ps, 1)
                pe.wait_ge(tqT_sb, PRIMED + 2 * (NT * b + n) + 2)
                for m in range(KF):
                    ins = pe.matmul(G[2][:, :], tqT[:, m, :], W["ffn_down"][:, m, :], start=(m == 0), stop=(m == KF - 1))
                ins.then_inc(d_ps, 1)

            with pe.Fori(0, NB) as b:
                latents(b)
                for i in range(PAIRS + 3):
                    if i < PAIRS and i % 2 == 0:
                        group(b, i // 2, i)
                    if 1 <= i <= PAIRS:
                        scores(b, i - 1)
                    if 2 <= i <= PAIRS + 1:
                        turn_probs(b, 2 * (i - 2))
                    if i >= 3:
                        values(b, 2 * (i - 3) + 1)
                    if 2 <= i <= PAIRS + 1:
                        turn_probs(b, 2 * (i - 2) + 1)
                        values(b, 2 * (i - 2))
                    if i < PAIRS:
                        pair_queries(b, i, i // 2 + 1)
                output(b)
                turn_input(b)
                for n in range(NT):
                    gate_up(b, n)
                    ffn_out(b, n)

        @block.scalar
        def _(act):
            def latents(b):
                for i in range(2):
                    act.wait_ge(xT_ps, PRIMED + 2 * b + i + 1)
                    act.activation(xT[:, 2 * i:2 * i + 2, :], G[i][:, :].rearrange("p (k s) -> p k s", k=2),
                                   ACT.Copy).then_inc(xT_sb, 1)
                for n in range(NT):
                    act.wait_ge(lat_ps, PRIMED + 3 * b + n + 1)
                    act.activation(squares[:, n * QR:(n + 1) * QR], G[n][:, 0:QR], ACT.Square, accum_out=ssq[:, n:n + 1]).then_inc(ssq_ok, 1)
                act.wait_ge(lat_ps, PRIMED + 3 * b + 3)
                for n in range(NT):
                    c0 = n * (KV + RD)
                    act.activation(squares[:, NT * QR + n * KV:NT * QR + (n + 1) * KV], G[2][:, c0:c0 + KV], ACT.Square,
                                   accum_out=ssq[:, 2 + n:3 + n]).then_inc(ssq_ok, 1)
                act.wait_ge(latT_ps, PRIMED + 3 * b + 1)
                act.activation(qnH[:, 0:2, :], G[0][:, :].rearrange("p (k s) -> p k s", k=2), ACT.Copy)
                act.wait_ge(latT_ps, PRIMED + 3 * b + 2)
                act.activation(qnH[:, 2, :], G[1][:, 0:S], ACT.Copy).then_inc(latT_hi, 1)
                act.activation(knH[:, :], G[1][:, S:2 * S], ACT.Copy).then_inc(latT_hi, 1)
                act.wait_ge(latT_ps, PRIMED + 3 * b + 3)
                act.activation(krH[:, :], G[2][:, 0:S], ACT.Copy).then_inc(latT_hi, 1)

            def exps(b, i):
                act.wait_ge(s_max, PRIMED + PAIRS * b + i + 1)
                if i >= 2:
                    act.wait_ge(pt_ps, PRIMED + NH * b + 2 * (i - 1))
                for n in range(NT):
                    cols = slice(n * P, n * P + (n + 1) * P)
                    for c in range(2):
                        ins = act.activation(pr[:, i % 2, c, cols], SB[c][:, cols], ACT.Exp, bias=nmax[:, i % 2, n, c:c + 1],
                                             scale=SCALE / S_NOPE, accum_out=rsum[:, i % 2, n, c:c + 1])
                ins.then_inc(p_exp, 1)

            def probs_hi(b, h):
                act.wait_ge(pt_ps, PRIMED + NH * b + h + 1)
                if h >= 2:
                    act.wait_ge(o_ps, PRIMED + NH * b + h - 1)
                act.activation(ptH[:, h % 2, :], PT[:, :], ACT.Copy).then_inc(pt_hi, 1)

            def out_hi(b, i):
                act.wait_ge(o_ps, PRIMED + NH * b + 2 * i + 2)
                act.activation(oH[:, 2 * i:2 * i + 2, :], OT[:, :, :], ACT.Copy).then_inc(o_hi, 1)

            def queries_hi(b, i):
                act.wait_ge(qp_ps, PRIMED + PAIRS * b + i + 1)
                if i >= 2:
                    act.wait_ge(s_ps, PRIMED + NH * b + 2 * (i - 1))
                act.activation(qpH[:, i % 2, :, :], QP[:, :, :], ACT.Copy).then_inc(qp_hi, 1)

            with act.Fori(0, NB) as b:
                latents(b)
                for i in range(PAIRS + 3):
                    if 2 <= i <= PAIRS + 1:
                        probs_hi(b, 2 * (i - 2))
                    if i >= 3:
                        out_hi(b, i - 3)
                    if 2 <= i <= PAIRS + 1:
                        probs_hi(b, 2 * (i - 2) + 1)
                    if 1 <= i <= PAIRS:
                        exps(b, i - 1)
                    if i < PAIRS:
                        queries_hi(b, i)
                act.wait_ge(xqT_ps, PRIMED + b + 1)
                act.activation(xqT[:, :, :], G[2][:, :].bitcast(BF16).rearrange("p (k s) -> p k s", k=KD),
                               ACT.Copy).then_inc(xqT_sb, 1)
                for n in range(NT):
                    for c in range(NCH):
                        u = n * NCH + c
                        act.wait_ge(t_ok, PRIMED + 3 * (NT * NCH * b + u) + 1)
                        act.activation(g1[:, u % 2, :], g1[:, u % 2, :], ACT.Tanh, scale=hsx[:, n:n + 1]).then_inc(th_ok, 1)
                    for r, (k0, k1) in enumerate(((0, 8), (8, KF))):
                        act.wait_ge(tqT_ps, PRIMED + 2 * (NT * b + n) + r + 1)
                        act.activation(tqT[:, k0:k1, :], G[r][:, :].bitcast(BF16).rearrange("p (k s) -> p k s", s=P)
                                       [:, 0:k1 - k0, :], ACT.Copy).then_inc(tqT_sb, 1)

        @block.gpsimd
        def _(pool):
            def rope(b, g):
                n = GROUPS * b + g
                pool.wait_ge(ab_read, PRIMED + n + 1)
                pool.tensor_tensor(ro[:, 0, :], tc[:, 0, :], ts[:, 1, :], ALU.subtract)
                pool.tensor_tensor(ro[:, 1, :], ts[:, 0, :], tc[:, 1, :], ALU.add).then_inc(ro_ok, 1)
                pool.wait_ge(ro_ok, PRIMED + n + 1)
                if g:
                    pool.wait_ge(qr_in[g - 1], PRIMED + 256 * (b + 1))
                else:
                    pool.wait_ge(qr_in[GROUPS - 1], PRIMED + 256 * b)
                pool.tensor_tensor(roH[:, :, :], ro[:, :, :], zeros[:, 0:1].unsqueeze(1).broadcast_to([P, 2, S]),
                                   ALU.add).then_inc(roh_ok, 1)
                pool.wait_ge(roh_ok, PRIMED + n + 1)
                pool.tensor_tensor(roL[:, :, :], ro[:, :, :], roH[:, :, :], ALU.subtract).then_inc(rol_ok, 1)

            def latents(b):
                pool.wait_ge(msq_ok, PRIMED + 2 * b + 2)
                pool.tensor_tensor(rstd[:, :], msq[:, :], minus_half[:, :], ALU.pow).then_inc(rstd_ok, 1)

            def norm_rstd(b, k):
                pool.wait_ge(var_ok, PRIMED + 2 * NT * b + k + 1)
                pool.tensor_tensor(lrs[:, k % NT:k % NT + 1], veps[:, k % NT:k % NT + 1], minus_half[:, 0:1],
                                   ALU.pow).then_inc(lrs_ok, 1)

            def normalise(b, i):
                pool.wait_ge(p_inv, PRIMED + PAIRS * b + i + 1)
                for n in range(NT):
                    w = (n + 1) * P
                    p = pr[:, i % 2, :, n * P:n * P + w]
                    ins = pool.tensor_tensor(p, p, rinv[:, i % 2, n, :].unsqueeze(2).broadcast_to([P, 2, w]), ALU.mult)
                ins.then_inc(p_norm, 1)

            pool.memset(zeros[:, :], 0.0)
            pool.memset(minus_half[:, :], -0.5).then_inc(half_ok, 1)
            pool.wait_ge(half_ok, PRIMED + 1)
            with pool.Fori(0, NB) as b:
                latents(b)
                for i in range(PAIRS + 1):
                    if i < PAIRS and i % 2 == 0:
                        rope(b, i // 2)
                    if i >= 1:
                        normalise(b, i - 1)
                for n in range(NT):
                    norm_rstd(b, n)
                for n in range(NT):
                    for c in range(NCH):
                        u = NT * NCH * b + n * NCH + c
                        i = c % 2
                        pool.wait_ge(u1_ok, PRIMED + u + 1)
                        pool.tensor_tensor(u1[:, i, :], g1[:, i, :], u1[:, i, :], ALU.mult).then_inc(t_ok, 1)
                        pool.wait_ge(t_ok, PRIMED + 3 * u + 1)
                        pool.wait_ge(th_ok, PRIMED + u + 1)
                        if c == 0:
                            pool.wait_ge(tq_ok, PRIMED + NT * b + n)
                        pool.tensor_tensor(t[:, c * CH:(c + 1) * CH], g1[:, i, :], u1[:, i, :], ALU.mult).then_inc(t_ok, 1)
                        pool.wait_ge(t_ok, PRIMED + 3 * u + 2)
                        pool.tensor_tensor(t[:, c * CH:(c + 1) * CH], t[:, c * CH:(c + 1) * CH], u1[:, i, :], ALU.add
                                           ).then_inc(t_ok, 1)
                    norm_rstd(b, NT + n)

        @block.vector
        def _(dve):
            ch = Chain(dve, steps)
            link = ch.link
            tt, tsc_ = dve.tensor_tensor, dve.tensor_scalar

            def latents(b):
                dve.wait_ge(ssq_ok, PRIMED + 4 * b + 4)
                tsc_(msq[:, 0:2], ssq[:, 0:2], 1.0 / QR, EPS_RMS, ALU.mult, ALU.add).then_inc(msq_ok, 1)
                tsc_(msq[:, 2:4], ssq[:, 2:4], 1.0 / KV, EPS_RMS, ALU.mult, ALU.add).then_inc(msq_ok, 1)
                dve.wait_ge(rstd_ok, PRIMED + b + 1)
                for n in range(NT):
                    tsc_(qn[:, n, :], G[n][:, 0:QR], rstd[:, n:n + 1], None, ALU.mult)
                for n in range(NT):
                    c0 = n * (KV + RD)
                    ins = tsc_(kn[:, n, :], G[2][:, c0:c0 + KV], rstd[:, 2 + n:3 + n], None, ALU.mult)
                link(ins)
                kv = G[2][:, 0:NT * (KV + RD)].rearrange("p (n c) -> p n c", n=NT)[:, :, KV:].rearrange(
                    "p n (i two) -> p two n i", two=2)
                for c in range(2):
                    tt(ka[:, c, :, :], kv[:, c, :, :], W["kcos"], ALU.mult)
                    ins = tt(kb[:, c, :, :], kv[:, c, :, :], W["ksin"], ALU.mult)
                link(ins)
                tt(kr[:, :, 0, 0, :], ka[:, 0, :, :], kb[:, 1, :, :], ALU.subtract)
                link(tt(kr[:, :, 0, 1, :], kb[:, 0, :, :], ka[:, 1, :, :], ALU.add))
                dve.tensor_copy(vH[:, :, :], kn[:, :, :])
                dve.tensor_copy(kr[:, :, 1, :, :], kr[:, :, 0, :, :]).then_inc(lat_sb, 1)
                dve.wait_ge(lat_sb, PRIMED + b + 1)
                tt(vL[:, :, :], kn[:, :, :], vH[:, :, :], ALU.subtract)
                dve.wait_ge(latT_hi, PRIMED + 3 * b + 1)
                tt(qnL[:, 0:2, :], G[0][:, :].rearrange("p (k s) -> p k s", k=2), qnH[:, 0:2, :], ALU.subtract)
                dve.wait_ge(latT_hi, PRIMED + 3 * b + 2)
                tt(qnL[:, 2, :], G[1][:, 0:S], qnH[:, 2, :], ALU.subtract).then_inc(latT_lo, 1)
                tt(knL[:, :], G[1][:, S:2 * S], knH[:, :], ALU.subtract).then_inc(latT_lo, 1)
                dve.wait_ge(latT_hi, PRIMED + 3 * b + 3)
                tt(krL[0:64, :], G[2][0:64, 0:S], krH[0:64, :], ALU.subtract).then_inc(latT_lo, 1)

            def rotate(b, g):
                dve.wait_ge(ab_ps, PRIMED + GROUPS * b + g + 1)
                if g:
                    dve.wait_ge(ro_ok, PRIMED + GROUPS * b + g)
                else:
                    dve.wait_ge(ro_ok, PRIMED + GROUPS * b)
                tt(tc[:, :, :], QP[:, :, :], W["qcos"].unsqueeze(1).broadcast_to([P, 2, S]), ALU.mult)
                tt(ts[:, :, :], QP[:, :, :], W["qsin"].unsqueeze(1).broadcast_to([P, 2, S]), ALU.mult).then_inc(ab_read, 1)

            def maxima(b, i):
                for c in range(2):
                    dve.wait_ge(s_ps, PRIMED + NH * b + 2 * i + c + 1)
                    for n in range(NT):
                        ins = dve.tensor_reduce(nmax[:, i % 2, n, c:c + 1], SB[c][:, n * P:n * P + (n + 1) * P], AX.X,
                                                ALU.max, negate=True)
                link(ins)
                tsc_(nmax[:, i % 2, :, :], nmax[:, i % 2, :, :], SCALE / S_NOPE, None, ALU.mult).then_inc(s_max, 1)

            def probs_lo(b, h):
                dve.wait_ge(pt_hi, PRIMED + NH * b + h + 1)
                tt(ptL[:, h % 2, :], PT[:, :], ptH[:, h % 2, :], ALU.subtract).then_inc(pt_lo, 1)

            def out_lo(b, i):
                dve.wait_ge(o_hi, PRIMED + PAIRS * b + i + 1)
                tt(oL[:, 2 * i:2 * i + 2, :], OT[:, :, :], oH[:, 2 * i:2 * i + 2, :], ALU.subtract).then_inc(o_lo, 1)

            def queries_lo(b, i):
                dve.wait_ge(qp_hi, PRIMED + PAIRS * b + i + 1)
                tt(qpL[:, i % 2, :, :], QP[:, :, :], qpH[:, i % 2, :, :], ALU.subtract).then_inc(qp_lo, 1)

            def inverse_sums(b, i):
                dve.wait_ge(p_exp, PRIMED + PAIRS * b + i + 1)
                dve.reciprocal(rinv[:, i % 2, :, :], rsum[:, i % 2, :, :]).then_inc(p_inv, 1)

            def norm(b, k):
                n = k % NT
                link(dve.bn_stats(st6[:, n, :], res[:, n, :]))
                dve.sem_inc(stats_ok, 1)
                link(dve.bn_aggr(mv[:, n, :], st6[:, n, :]))
                tsc_(veps[:, n:n + 1], mv[:, n, 1:2], EPS_LN, None, ALU.add).then_inc(var_ok, 1)
                dve.wait_ge(lrs_ok, PRIMED + 2 * NT * b + k + 1)
                return tsc_(res[:, n, :], res[:, n, :], mv[:, n, 0:1], lrs[:, n:n + 1], ALU.subtract, ALU.mult)

            def quantize(dst, src, rscale, w):
                for c in range(0, w, HF):
                    n = min(HF, w - c)
                    link(tsc_(y[:, 0:n], src[:, c:c + n], rscale, None, ALU.mult))
                    link(exponent_power(dve, ch, e[:, 0:n], y[:, 0:n]))
                    link(tt(y[:, 0:n], y[:, 0:n], e[:, 0:n], ALU.add))
                    ins = tt(dst[:, c:c + n], y[:, 0:n], e[:, 0:n], ALU.subtract)
                    if c + n < w:
                        link(ins)
                return ins

            def attention_norm(b, n):
                dve.wait_ge(y_ps, PRIMED + NT * b + n + 1)
                dve.wait_ge(res_in, PRIMED + 16 * (b + 1))
                link(dve.scalar_tensor_tensor(out=res[:, n, :], in0=G[n][:, :], scalar=1.0 / S_VO, in1=res[:, n, :],
                                              op0=ALU.mult, op1=ALU.add))
                link(norm(b, n))
                link(dve.tensor_reduce(am[:, n:n + 1], res[:, n, :], AX.X, ALU.max, apply_absolute_value=True))
                link(tsc_(sx[:, n:n + 1], am[:, n:n + 1], 1.0 / FP8_MAX, None, ALU.mult))
                tsc_(hsx[:, n:n + 1], sx[:, n:n + 1], 0.5, None, ALU.mult)
                link(dve.reciprocal(rsx[:, n:n + 1], sx[:, n:n + 1]))
                quantize(xq[:, n, :], res[:, n, :], rsx[:, n:n + 1], D).then_inc(xq_ok, 1)

            def hidden(b, n):
                for c in range(NCH):
                    u = NT * NCH * b + n * NCH + c
                    k = n * NCH + c
                    i = k % 2
                    cols = slice(c * CH, (c + 1) * CH)
                    if k >= 2:
                        dve.wait_ge(t_ok, PRIMED + 3 * (u - 1))
                    dve.wait_ge(gu_ps, PRIMED + 2 * u + 1)
                    tt(g1[:, i, :], G[(2 * k) % 3][:, 0:CH], W["gate_s"][:, cols], ALU.mult).then_inc(g1_ok, 1)
                    dve.wait_ge(gu_ps, PRIMED + 2 * u + 2)
                    dve.wait_ge(g1_ok, PRIMED + u + 1)
                    dve.sem_inc(gu_free, 1)
                    tt(u1[:, i, :], G[(2 * k + 1) % 3][:, 0:CH], W["up_s"][:, cols], ALU.mult).then_inc(u1_ok, 1)
                    dve.wait_ge(u1_ok, PRIMED + u + 1)
                    dve.sem_inc(gu_free, 1)
                dve.wait_ge(t_ok, PRIMED + 3 * (NT * NCH * b + (n + 1) * NCH))
                link(dve.tensor_reduce(tm[:, n:n + 1], t[:, :], AX.X, ALU.max, apply_absolute_value=True))
                link(tsc_(tsc[:, n:n + 1], tm[:, n:n + 1], 1.0 / FP8_MAX, None, ALU.mult))
                link(dve.reciprocal(trs[:, n:n + 1], tsc[:, n:n + 1]))
                link(dve.scalar_tensor_tensor(out=tst[:, n:n + 1], in0=sx[:, n:n + 1], scalar=hsx[:, n:n + 1],
                                              in1=tsc[:, n:n + 1], op0=ALU.mult, op1=ALU.mult))
                quantize(tq[:, :], t[:, :], trs[:, n:n + 1], FF).then_inc(tq_ok, 1)

            def ffn_norm(b, n):
                dve.wait_ge(d_ps, PRIMED + NT * b + n + 1)
                link(tt(y[:, 0:D], G[2][:, :], W["down_s"][:, :], ALU.mult))
                link(dve.scalar_tensor_tensor(out=res[:, n, :], in0=y[:, 0:D], scalar=tst[:, n:n + 1],
                                              in1=res[:, n, :], op0=ALU.mult, op1=ALU.add))
                norm(b, NT + n).then_inc(out_ok, 1)

            with dve.Fori(0, NB) as b:
                ch.base, ch.n = PRIMED + b * DVE_STEPS, 0
                latents(b)
                for i in range(PAIRS + 3):
                    if i < PAIRS and i % 2 == 0:
                        rotate(b, i // 2)
                    if 1 <= i <= PAIRS:
                        maxima(b, i - 1)
                    if 2 <= i <= PAIRS + 1:
                        probs_lo(b, 2 * (i - 2))
                    if i >= 3:
                        out_lo(b, i - 3)
                    if 2 <= i <= PAIRS + 1:
                        probs_lo(b, 2 * (i - 2) + 1)
                    if 1 <= i <= PAIRS:
                        inverse_sums(b, i - 1)
                    if i < PAIRS:
                        queries_lo(b, i)
                for n in range(NT):
                    attention_norm(b, n)
                for n in range(NT):
                    hidden(b, n)
                    ffn_norm(b, n)
                assert ch.n == DVE_STEPS, ch.n


def vit_layer(nc, A, out):
    with ExitStack() as ctx:
        seq = nc.dram_tensor("seq", [NB, S, D], F32, kind="Internal").ap()
        token_mixer(nc, A["x"], A["log_dt"], A["B_ri"], A["inv_A_real"], A["A_imag"], seq)
        W = scratch(nc, ctx)
        attention_weights(nc, A, W)
        ffn_scratch(nc, ctx, W)
        ffn_weights(nc, A, W)
        layer(nc, A, W, seq, out)


_INS = ["x", "L0_tok_log_dt", "L0_tok_B_ri", "L0_tok_inv_A_real", "L0_tok_A_imag", "L0_attn_wq_down",
        "L0_attn_q_norm_w", "L0_attn_wq_up", "L0_attn_wq_rope", "L0_attn_wkv_down", "L0_attn_kv_norm_w",
        "L0_attn_wkv_up", "L0_attn_wk_rope", "L0_attn_wo", "L0_ffn_w_gate", "L0_ffn_w_up", "L0_ffn_w_down",
        "L0_ffn_down_reorder_index"]


def rope_tables():
    import numpy as np
    pos = np.arange(S, dtype=np.float32)
    inv = (np.float32(1.0) / np.float32(10000.0) ** (np.arange(0, RD, 2, dtype=np.float32) / np.float32(RD))
           ).astype(np.float32)
    ang = pos[:, None] * inv[None, :]
    cos, sin = np.cos(ang).astype(np.float32), np.sin(ang).astype(np.float32)
    keys = [(t * np.float32(S_RK)).reshape(NT, P, RD // 2).transpose(1, 0, 2) for t in (cos, sin)]
    return {"qcos": np.tile(cos.T, (4, 1)), "qsin": np.tile(sin.T, (4, 1)), "kcos": keys[0], "ksin": keys[1]}


def kernel(**inputs):
    import numpy as _np
    import concourse.bacc as _bacc
    from concourse import mybir as _mybir
    from concourse.bass_utils import run_bass_kernel_spmd as _run

    nc = _bacc.Bacc("TRN2", target_bir_lowering=False, num_devices=1)
    arrays, A = {}, {}
    named = [(name.replace("L0_tok_", "").replace("L0_attn_", "").replace("L0_ffn_", ""), inputs[name]) for name in _INS]
    for name, a in named + list(rope_tables().items()):
        a = _np.ascontiguousarray(a)
        arrays[f"in_{name}_dram"] = a
        A[name] = nc.dram_tensor(f"in_{name}_dram", a.shape, _mybir.dt.from_np(a.dtype), kind="ExternalInput").ap()
    out = nc.dram_tensor("out_0_dram", (NB, S, D), F32, kind="ExternalOutput").ap()
    vit_layer(nc, A, out)
    r = _run(nc, [arrays], core_ids=[0])
    return r.results[0]["out_0_dram"]
```

```python
import concourse.bass as bass
from concourse import mybir
from contextlib import ExitStack

F32 = mybir.dt.float32
F16 = mybir.dt.float16
BF16 = mybir.dt.bfloat16
I32 = mybir.dt.int32
U32 = mybir.dt.uint32
ALU = mybir.AluOpType
ACT = mybir.ActivationFunctionType
AX = mybir.AxisListType

P = 128
NB, S, D = 16, 256, 512
NSTATE = 64
NT, KD = S // P, D // P
NH, RD, HD = 16, 64, 128
QR, KV = 384, 128
KQ = QR // P
FF = 1408
KF = FF // P
NCH, CH = 4, FF // 4
PAIRS, GROUPS = NH // 2, NH // 4
A_STEPS, B_STEPS = 8, 64
HBLK = 16
NBLK = P // HBLK
EPS_RMS, EPS_LN = 1e-6, 1e-5
SCALE = float((HD + RD) ** -0.5)
S_NOPE, S_RQ, S_RK = 16.0, 64.0, 0.25
S_VO = 64.0
assert S_NOPE == S_RQ * S_RK
MASK = -1e30
PRIMED = 1
FP8_MAX = 448.0
EXPONENT_BITS = 0x7F800000
LEAST_NORMAL = 2.0 ** -6
ROUNDER = 1.5 * 2.0 ** 20


class Chain:

    def __init__(self, eng, sem):
        self.eng, self.sem, self.n, self.base = eng, sem, 0, 0

    def link(self, ins):
        self.n += 1
        ins.then_inc(self.sem, 1)
        self.eng.wait_ge(self.sem, self.base + self.n)


def token_mixer(nc, x_c, log_dt, b_ri, inv_a, a_imag, seq):
    with ExitStack() as ctx:
        def sb(name, shape, dt=F32):
            return ctx.enter_context(nc.sbuf_tensor(name, shape, dt))

        def ps(name, shape, dt=F32):
            return ctx.enter_context(nc.psum_tensor(name, shape, dt))

        def sem(name):
            return ctx.enter_context(nc.semaphore(name))

        N = NSTATE
        NL = 9
        ident = sb("tm_ident", [P, P])
        dtc = sb("tm_logdt", [P, 2])
        dt = sb("tm_dt", [P, 2])
        bri = sb("tm_b", [P, 2, N, 2])
        ia = sb("tm_inva", [P, 2, N])
        ea = sb("tm_expa", [P, 2, N])
        ai = sb("tm_aimag", [P, 2, N])
        s = {k: sb("tm_" + k, [P, 2, N]) for k in
             ("zr", "zi", "m", "t", "den", "r", "gr", "gi", "fr", "fi", "u", "v")}
        wr = sb("tm_wr", [P, NL, 2, N])
        wi = sb("tm_wi", [P, NL, 2, N])
        cin = sb("tm_cin", [P, NB, N, 2])
        cs = sb("tm_cs", [P, NB, 3, N])
        U = sb("tm_u_pow", [P, B_STEPS, 2, N])
        T1 = sb("tm_t1", [P, B_STEPS // 2, N])
        T2 = sb("tm_t2", [P, B_STEPS // 2, N])
        G = sb("tm_g", [P, A_STEPS, 4, N])
        gi_ = sb("tm_gim", [P, A_STEPS, N])
        UT = sb("tm_ut", [P, P, B_STEPS])
        P1 = sb("tm_p1", [P, P, NB])
        P2 = sb("tm_p2", [P, P, NB])
        G1 = sb("tm_g1", [P, P, A_STEPS])
        G2 = sb("tm_g2", [P, P, A_STEPS])
        X1 = sb("tm_x1", [P, 2, HBLK, NB, A_STEPS])
        X2 = sb("tm_x2", [P, 2, HBLK, NB, A_STEPS])
        Y = sb("tm_y", [P, 2, HBLK, B_STEPS])
        tp = [ps(f"tm_tp{i}", [P, 4, P]) for i in range(2)]
        yp = [ps(f"tm_yp{i}", [P, 8, B_STEPS]) for i in range(4)]

        loaded, c_loaded = sem("tm_loaded"), sem("tm_c_loaded")
        ident0, ident_ok = sem("tm_ident0"), sem("tm_ident_ok")
        exp_ok = sem("tm_exp_ok")
        steps, psteps = sem("tm_dve_steps"), sem("tm_pool_steps")
        pow_ok, cs_ok = sem("tm_pow_ok"), sem("tm_cs_ok")
        tr_done, tr_read = sem("tm_tr_done"), sem("tm_tr_read")
        x1_ok, x2_ok = sem("tm_x1_ok"), sem("tm_x2_ok")
        y_done, y_read = sem("tm_y_done"), sem("tm_y_read")
        y_stored = [sem("tm_y_stored_even"), sem("tm_y_stored_odd")]
        TR_HB = (B_STEPS + 2 * A_STEPS + 2 * NB) // 4

        block = ctx.enter_context(nc.Block())

        @block.sync
        def _(sp):
            sp.dma_start(dtc[:, :], log_dt.rearrange("(k p) -> p k", p=P), allow_slow_non_contiguous=True).then_inc(loaded, 16)
            sp.dma_start(ia[:, :, :], inv_a.rearrange("(k p) n -> p k n", p=P)).then_inc(loaded, 16)
            sp.dma_start(ai[:, :, :], a_imag.rearrange("(k p) n -> p k n", p=P)).then_inc(loaded, 16)
            sp.dma_start(bri[:, :, :, :], b_ri.rearrange("(k p) n r -> p k n r", p=P)).then_inc(loaded, 16)
            for hb in range(2):
                if hb:
                    sp.wait_ge(cs_ok, 1)
                sp.dma_start(cin[:, :, :, :], x_c[:, hb * P:(hb + 1) * P, :, :].rearrange("c h n r -> h c n r")
                             ).then_inc(c_loaded, 16)
            for i in range(2 * NBLK):
                sp.wait_ge(y_read, 2 * (i + 1))
                for c in range(NB):
                    sp.dma_start(seq[c, i * HBLK:(i + 1) * HBLK, :].rearrange("h (a b) -> a h b", b=B_STEPS),
                                 Y[c * A_STEPS:(c + 1) * A_STEPS, i % 2, :, :]).then_inc(y_stored[i % 2], 16)
            for stored in y_stored:
                sp.wait_ge(stored, 16 * NB * NBLK)

        @block.gpsimd
        def _(pool):
            pool.memset(ident[:, :], 0.0).then_inc(ident0, 1)
            pool.wait_ge(ident0, 1)
            pool.affine_select(out=ident[:, :], in_=ident[:, :], compare_op=ALU.not_equal, fill=1.0, base=0,
                               pattern=[[-1, P]], channel_multiplier=1).then_inc(ident_ok, 1)
            for hb in range(2):
                pool.wait_ge(c_loaded, 16 * (hb + 1))
                if hb:
                    pool.wait_ge(tr_done, TR_HB)
                for slot, r in ((0, 0), (1, 1), (2, 0)):
                    ins = pool.tensor_copy(cs[:, :, slot, :], cin[:, :, :, r])
                ins.then_inc(cs_ok, 1)
                for k in range(NBLK):
                    i = hb * NBLK + k
                    if k == 0:
                        pool.wait_ge(tr_read, TR_HB * (hb + 1))
                    if i >= 2:
                        pool.wait_ge(y_done, 2 * (i - 1))
                    hs = slice(k * HBLK, (k + 1) * HBLK)
                    pool.tensor_tensor(X2[:, i % 2, :, :, :],
                                       P2[:, hs, :].unsqueeze(3).broadcast_to([P, HBLK, NB, A_STEPS]),
                                       G2[:, hs, :].unsqueeze(2).broadcast_to([P, HBLK, NB, A_STEPS]),
                                       ALU.mult).then_inc(x2_ok, 1)

        @block.vector
        def _(dve):
            ch = Chain(dve, steps)
            link = ch.link
            tt = dve.tensor_tensor

            def mul(o, a, b):
                link(tt(o, a, b, ALU.mult))

            dve.wait_ge(loaded, 64)
            dve.wait_ge(exp_ok, 2)
            for hb in range(2):
                link(dve.tensor_scalar(s["zr"][:, hb, :], ea[:, hb, :], dt[:, hb:hb + 1], -0.5, ALU.mult, ALU.mult))
                link(dve.tensor_scalar(s["zi"][:, hb, :], ai[:, hb, :], dt[:, hb:hb + 1], 0.5, ALU.mult, ALU.mult))
            z = {k: v[:, :, :] for k, v in s.items()}
            mul(z["m"], z["zr"], z["zr"])
            mul(z["t"], z["zi"], z["zi"])
            link(tt(z["m"], z["m"], z["t"], ALU.add))
            link(dve.tensor_scalar(z["u"], z["zr"], -1.0, 1.0, ALU.mult, ALU.add))
            mul(z["v"], z["u"], z["u"])
            link(tt(z["den"], z["v"], z["t"], ALU.add))
            link(dve.reciprocal(z["r"], z["den"]))
            mul(z["gr"], z["u"], z["r"])
            mul(z["gi"], z["zi"], z["r"])
            link(dve.tensor_scalar(z["v"], z["m"], -1.0, 1.0, ALU.mult, ALU.add))
            mul(wr[:, 0, :, :], z["v"], z["r"])
            link(dve.tensor_scalar(wi[:, 0, :, :], z["gi"], 2.0, None, ALU.mult))
            br, bi = bri[:, :, :, 0], bri[:, :, :, 1]
            mul(z["u"], br, z["gr"])
            mul(z["v"], bi, z["gi"])
            link(tt(z["u"], z["u"], z["v"], ALU.subtract))
            mul(z["v"], br, z["gi"])
            mul(z["t"], bi, z["gr"])
            link(tt(z["v"], z["v"], z["t"], ALU.add))
            for hb in range(2):
                link(dve.tensor_scalar(s["fr"][:, hb, :], s["u"][:, hb, :], dt[:, hb:hb + 1], 2.0, ALU.mult, ALU.mult))
                link(dve.tensor_scalar(s["fi"][:, hb, :], s["v"][:, hb, :], dt[:, hb:hb + 1], 2.0, ALU.mult, ALU.mult))
            for k in range(1, NL):
                a, b = wr[:, k - 1, :, :], wi[:, k - 1, :, :]
                mul(z["u"], a, a)
                mul(z["v"], b, b)
                link(tt(wr[:, k, :, :], z["u"], z["v"], ALU.subtract))
                link(dve.scalar_tensor_tensor(out=wi[:, k, :, :], in0=a, scalar=2.0, in1=b, op0=ALU.mult, op1=ALU.mult))

            def times(o_re, o_im, a_re, a_im, k, hb, n):
                w_re = wr[:, k, hb, :].unsqueeze(1).broadcast_to([P, n, N])
                w_im = wi[:, k, hb, :].unsqueeze(1).broadcast_to([P, n, N])
                t1, t2 = T1[:, 0:n, :], T2[:, 0:n, :]
                tt(t1, a_re, w_re, ALU.mult)
                link(tt(t2, a_im, w_im, ALU.mult))
                link(tt(o_re, t1, t2, ALU.subtract))
                tt(t1, a_re, w_im, ALU.mult)
                link(tt(t2, a_im, w_re, ALU.mult))
                link(tt(o_im, t1, t2, ALU.add))

            for hb in range(2):
                if hb:
                    dve.wait_ge(tr_done, TR_HB)
                dve.memset(U[:, 0, 0, :], 1.0)
                link(dve.memset(U[:, 0, 1, :], 0.0))
                for k in range(6):
                    n = 1 << k
                    times(U[:, n:2 * n, 0, :], U[:, n:2 * n, 1, :], U[:, 0:n, 0, :], U[:, 0:n, 1, :], k, hb, n)
                dve.tensor_copy(G[:, 0, 0, :], s["fr"][:, hb, :])
                link(dve.tensor_copy(gi_[:, 0, :], s["fi"][:, hb, :]))
                for k in range(3):
                    n = 1 << k
                    times(G[:, n:2 * n, 0, :], gi_[:, n:2 * n, :], G[:, 0:n, 0, :], gi_[:, 0:n, :], 6 + k, hb, n)
                dve.tensor_scalar(G[:, :, 1, :], G[:, :, 0, :], -1.0, None, ALU.mult)
                dve.tensor_scalar(G[:, :, 2, :], gi_[:, :, :], -1.0, None, ALU.mult)
                dve.tensor_scalar(G[:, :, 3, :], gi_[:, :, :], -1.0, None, ALU.mult).then_inc(pow_ok, 1)
                for k in range(NBLK):
                    i = hb * NBLK + k
                    if k == 0:
                        dve.wait_ge(tr_read, TR_HB * (hb + 1))
                    if i >= 2:
                        dve.wait_ge(y_done, 2 * (i - 1))
                    hs = slice(k * HBLK, (k + 1) * HBLK)
                    tt(X1[:, i % 2, :, :, :], P1[:, hs, :].unsqueeze(3).broadcast_to([P, HBLK, NB, A_STEPS]),
                       G1[:, hs, :].unsqueeze(2).broadcast_to([P, HBLK, NB, A_STEPS]), ALU.mult).then_inc(x1_ok, 1)

        @block.tensor
        def _(pe):
            pe.wait_ge(ident_ok, 1)
            n = 0

            def four(sources):
                nonlocal n
                if n >= 2:
                    pe.wait_ge(tr_read, n - 1)
                for j, src in enumerate(sources):
                    ins = pe.transpose(tp[n % 2][:, j, :], src, ident[:, :])
                ins.then_inc(tr_done, 1)
                n += 1

            for hb in range(2):
                pe.wait_ge(cs_ok, hb + 1)
                for q in range(NB // 4):
                    four([cs[:, 4 * q + j, 0:2, :] for j in range(4)])
                for q in range(NB // 4):
                    four([cs[:, 4 * q + j, 1:3, :] for j in range(4)])
                pe.wait_ge(pow_ok, hb + 1)
                for q in range(A_STEPS // 4):
                    four([G[:, 4 * q + j, 0:2, :] for j in range(4)])
                for q in range(A_STEPS // 4):
                    four([G[:, 4 * q + j, 2:4, :] for j in range(4)])
                for q in range(B_STEPS // 4):
                    four([U[:, 4 * q + j, :, :] for j in range(4)])
                pe.wait_ge(tr_read, TR_HB * (hb + 1))
                for k in range(NBLK):
                    i = hb * NBLK + k
                    pe.wait_ge(x1_ok, i + 1)
                    pe.wait_ge(x2_ok, i + 1)
                    for half in range(2):
                        g = 2 * i + half
                        if g >= 4:
                            pe.wait_ge(y_read, g - 3)
                        for j in range(8):
                            h = half * 8 + j
                            rhs = UT[:, k * HBLK + h, :]
                            pe.matmul(yp[g % 4][:, j, :], X1[:, i % 2, h, :, :], rhs, start=True, stop=False)
                            ins = pe.matmul(yp[g % 4][:, j, :], X2[:, i % 2, h, :, :], rhs, start=False, stop=True)
                        ins.then_inc(y_done, 1)

        @block.scalar
        def _(act):
            act.wait_ge(loaded, 64)
            act.activation(dt[:, :], dtc[:, :], ACT.Exp).then_inc(exp_ok, 1)
            act.activation(ea[:, :, :], ia[:, :, :], ACT.Exp).then_inc(exp_ok, 1)
            n = 0
            for hb in range(2):
                for dst, count in ((P1, NB), (P2, NB), (G1, A_STEPS), (G2, A_STEPS), (UT, B_STEPS)):
                    for q in range(count // 4):
                        act.wait_ge(tr_done, n + 1)
                        if hb and q == 0:
                            act.wait_ge(y_done, 2 * NBLK)
                        act.activation(dst[:, :, 4 * q:4 * q + 4].rearrange("p h j -> p j h"), tp[n % 2][:, :, :],
                                       ACT.Copy).then_inc(tr_read, 1)
                        n += 1
                for k in range(NBLK):
                    i = hb * NBLK + k
                    if i >= 2:
                        act.wait_ge(y_stored[i % 2], 16 * NB * (i // 2))
                    for half in range(2):
                        g = 2 * i + half
                        act.wait_ge(y_done, g + 1)
                        act.activation(Y[:, i % 2, half * 8:half * 8 + 8, :], yp[g % 4][:, :, :],
                                       ACT.Copy).then_inc(y_read, 1)




def attention_weights(nc, A, W):
    with ExitStack() as ctx:
        def sb(name, shape, dt=F32):
            return ctx.enter_context(nc.sbuf_tensor(name, shape, dt))

        def sem(name):
            return ctx.enter_context(nc.semaphore(name))

        ident = W["ident"]
        wkv = sb("wkv_up", [P, NH, 2, HD])
        wqu = sb("wq_up", [P, KQ, NH, HD])
        wo = sb("wo", [P, NH, D])
        wr = sb("wq_rope", [P, KQ, GROUPS, P, 2])
        qw = sb("q_norm", [P, KQ])
        kw = sb("kv_norm", [P, 1])
        qws = sb("q_norm_scaled", [P, KQ])
        qwr = sb("q_norm_rope", [P, KQ])
        qkT = sb("qkT", [P, 2, 4, P])
        vT = sb("vT", [P, 2, P])
        wt = sb("w_nope", [P, 2, KQ, P])
        vt = sb("w_out", [P, 2, D])
        tq = [ctx.enter_context(nc.psum_tensor(f"aw_tq{i}", [P, 4, P], F32)) for i in range(2)]
        tv = [ctx.enter_context(nc.psum_tensor(f"aw_tv{i}", [P, 4, P], F32)) for i in range(2)]
        vo = [ctx.enter_context(nc.psum_tensor(f"aw_vo{i}", [P, D], F32)) for i in range(2)]
        kv_in, q_in, o_in, r_in, small_in, keep_in = (sem("aw_" + n) for n in
                                                      ("kv_in", "q_in", "o_in", "r_in", "small_in", "keep_in"))
        kv_ok, qw_ok = sem("aw_kv_ok"), sem("aw_qw_ok")
        tr_ok, tr_sb = sem("aw_tr_ok"), sem("aw_tr_sb")
        prod, wt_ok, vt_ok = sem("aw_prod"), sem("aw_wt_ok"), sem("aw_vt_ok")
        hi_ok, lo_ok, rs_ok, rh_ok, rl_ok = (sem("aw_" + n) for n in ("hi", "lo", "rs", "rh", "rl"))
        block = ctx.enter_context(nc.Block())

        @block.sync
        def _(sp):
            sp.dma_start(kw[:, :], A["kv_norm_w"].rearrange("(p o) -> p o", o=1)).then_inc(small_in, 16)
            sp.dma_start(qw[:, :], A["q_norm_w"].rearrange("(k p) -> p k", p=P),
                         allow_slow_non_contiguous=True).then_inc(small_in, 16)
            sp.dma_start(wkv[:, :, :, :], A["wkv_up"].rearrange("p (h t d) -> p h t d", h=NH, t=2)).then_inc(kv_in, 16)
            sp.dma_start(wqu[:, :, :, :], A["wq_up"].rearrange("(k p) (h d) -> p k h d", p=P, h=NH)).then_inc(q_in, 16)
            sp.dma_start(wo[:, :, :], A["wo"].rearrange("(h p) n -> p h n", p=P)).then_inc(o_in, 16)
            sp.dma_start(wr[:, :, :, :, :], A["wq_rope"].rearrange("(k p) (g m c) -> p k g m c", p=P, g=GROUPS, c=2)
                         ).then_inc(r_in, 16)
            for col, name in ((0, "wq_down"), (QR, "wkv_down"), (QR + KV, "wk_rope")):
                n = A[name].shape[1]
                sp.dma_start(W["down"][:, :, col:col + n], A[name].rearrange("(k p) n -> p k n", p=P)
                             ).then_inc(keep_in, 16)
            for name in ("qcos", "qsin", "kcos", "ksin"):
                sp.dma_start(W[name], A[name]).then_inc(keep_in, 16)
            sp.wait_ge(keep_in, 16 * 7)

        @block.tensor
        def _(pe):
            pe.wait_ge(q_in, 16)
            pe.wait_ge(kv_ok, 1)
            for h in range(NH + 1):
                if h < NH:
                    i = h % 2
                    if h >= 2:
                        pe.wait_ge(wt_ok, h - 1)
                    for k in range(KQ):
                        pe.transpose(tq[i][:, k, :], wqu[:, k, h, :], ident[:, :])
                    pe.transpose(tq[i][:, 3, :], wkv[:, h, 0, :], ident[:, :])
                    pe.transpose(tv[i][:, 0, :], wkv[:, h, 1, :], ident[:, :]).then_inc(tr_ok, 1)
                if h >= 1:
                    g, i = h - 1, (h - 1) % 2
                    pe.wait_ge(tr_sb, 2 * (g + 1))
                    if g == 0:
                        pe.wait_ge(o_in, 16)
                    if g >= 2:
                        pe.wait_ge(vt_ok, g - 1)
                    for k in range(KQ):
                        pe.matmul(tv[i][:, 1 + k, :], qkT[:, i, k, :], qkT[:, i, 3, :], start=True, stop=True)
                    pe.matmul(vo[i][:, :], vT[:, i, :], wo[:, g, :], start=True, stop=True).then_inc(prod, 1)

        @block.scalar
        def _(act):
            for h in range(NH + 1):
                if h < NH:
                    i = h % 2
                    act.wait_ge(tr_ok, h + 1)
                    if h >= 2:
                        act.wait_ge(prod, h - 1)
                    act.activation(qkT[:, i, :, :], tq[i][:, :, :], ACT.Copy).then_inc(tr_sb, 1)
                    act.activation(vT[:, i, :], tv[i][:, 0, :], ACT.Copy).then_inc(tr_sb, 1)
                if h >= 1:
                    g, i = h - 1, (h - 1) % 2
                    act.wait_ge(prod, g + 1)
                    if g >= 2:
                        act.wait_ge(lo_ok, 2 * (g - 1))
                    act.activation(vt[:, i, :], vo[i][:, :], ACT.Copy, scale=S_VO).then_inc(vt_ok, 1)

        @block.vector
        def _(dve):
            dve.wait_ge(small_in, 32)
            dve.tensor_scalar(qws[:, :], qw[:, :], S_NOPE, None, ALU.mult)
            dve.tensor_scalar(qwr[:, :], qw[:, :], S_RQ, None, ALU.mult).then_inc(qw_ok, 1)
            dve.wait_ge(kv_in, 16)
            dve.tensor_scalar(wkv[:, :, :, :], wkv[:, :, :, :], kw[:, 0:1], None, ALU.mult).then_inc(kv_ok, 1)
            dve.wait_ge(r_in, 16)
            dve.wait_ge(qw_ok, 1)
            for k in range(KQ):
                dve.tensor_scalar(wr[:, k, :, :, :], wr[:, k, :, :, :], qwr[:, k:k + 1], None, ALU.mult).then_inc(rs_ok, 1)
            dve.wait_ge(rs_ok, KQ)
            for k in range(KQ):
                for c in range(2):
                    dve.tensor_copy(W["ropeH"][:, k, :, c, :], wr[:, k, :, :, c]).then_inc(rh_ok, 1)
            for h in range(NH):
                i = h % 2
                dve.wait_ge(prod, h + 1)
                if h >= 2:
                    dve.wait_ge(lo_ok, 2 * (h - 1))
                dve.tensor_tensor(wt[:, i, :, :], tv[i][:, 1:4, :],
                                  qws[:, :].unsqueeze(2).broadcast_to([P, KQ, P]), ALU.mult).then_inc(wt_ok, 1)
                dve.wait_ge(wt_ok, h + 1)
                dve.tensor_copy(W["nopeH"][:, :, h, :], wt[:, i, :, :]).then_inc(hi_ok, 1)
                dve.wait_ge(vt_ok, h + 1)
                dve.tensor_copy(W["outH"][:, h, :], vt[:, i, :]).then_inc(hi_ok, 1)

        @block.gpsimd
        def _(pool):
            for k in range(KQ):
                for c in range(2):
                    pool.wait_ge(rh_ok, 2 * k + c + 1)
                    pool.tensor_tensor(W["ropeL"][:, k, :, c, :], wr[:, k, :, :, c], W["ropeH"][:, k, :, c, :],
                                       ALU.subtract).then_inc(rl_ok, 1)
            for h in range(NH):
                i = h % 2
                pool.wait_ge(hi_ok, 2 * h + 1)
                pool.tensor_tensor(W["nopeL"][:, :, h, :], wt[:, i, :, :], W["nopeH"][:, :, h, :],
                                   ALU.subtract).then_inc(lo_ok, 1)
                pool.wait_ge(hi_ok, 2 * h + 2)
                pool.tensor_tensor(W["outL"][:, h, :], vt[:, i, :], W["outH"][:, h, :],
                                   ALU.subtract).then_inc(lo_ok, 1)


def ffn_weights(nc, A, W):
    with ExitStack() as ctx:
        def sb(name, shape, dt=F32):
            return ctx.enter_context(nc.sbuf_tensor(name, shape, dt))

        def sem(name):
            return ctx.enter_context(nc.semaphore(name))

        ident, ident16 = W["ident"], W["ident16"]
        TILES = 2 * KF + KD
        RING = 3
        idx = sb("hidden_order", [P, KF], I32)
        raw = sb("fw_raw", [P, RING, FF])
        y = sb("fw_y", [P, 2, FF])
        e = sb("fw_e", [P, 2, FF])
        q16 = sb("fw_q", [P, 2, FF], BF16)
        am = sb("fw_absmax", [P, TILES])
        ws = sb("fw_scale", [P, TILES])
        rs = sb("fw_rscale", [P, TILES])
        diag = sb("fw_diag", [P, 2, P])
        ones = sb("fw_ones", [P, P])
        tp = [ctx.enter_context(nc.psum_tensor(f"fw_tp{i}", [P, 8, P], BF16)) for i in range(4)]
        sp_ = [ctx.enter_context(nc.psum_tensor(f"fw_sp{i}", [P, P], F32)) for i in range(2)]
        idx_in = sem("fw_idx_in")
        raw_in = [sem(f"fw_raw_in{i}") for i in range(RING)]
        steps, y_ok, m_ok = sem("fw_steps"), sem("fw_y_ok"), sem("fw_m_ok")
        t_ok, q_ok, ones_ok, diag_ok = sem("fw_t_ok"), sem("fw_q_ok"), sem("fw_ones_ok"), sem("fw_diag_ok")
        tr_ok, tr_read, sc_ok, sc_read = sem("fw_tr_ok"), sem("fw_tr_read"), sem("fw_sc_ok"), sem("fw_sc_read")
        block = ctx.enter_context(nc.Block())

        def width(n):
            return D if n < 2 * KF else FF

        def halves(n):
            k = width(n) // P
            return [(0, k)] if k <= 8 else [(0, 8), (8, k)]

        banks = [sum(len(halves(m)) for m in range(n)) for n in range(TILES + 1)]

        @block.sync
        def _(sp):
            sp.dma_start(idx[:, :], A["down_reorder_index"].rearrange("(m p) -> p m", p=P),
                         allow_slow_non_contiguous=True).then_inc(idx_in, 16)
            sp.wait_ge(idx_in, 16)

        @block.gpsimd
        def _(pool):
            pool.memset(ones[:, :], 1.0).then_inc(ones_ok, 1)
            pool.wait_ge(idx_in, 16)

            def fetch(n):
                if n >= RING:
                    pool.wait_ge(y_ok, n - RING + 1)
                if n < 2 * KF:
                    src = A["w_gate"] if n < KF else A["w_up"]
                    m = n % KF
                    pool.indirect_dma_start(raw[:, n % RING, 0:D], None, src,
                                            bass.IndirectOffsetOnAxis(ap=idx[:, m:m + 1].bitcast(U32), axis=0)
                                            ).then_inc(raw_in[n % RING], 16)
                else:
                    m = n - 2 * KF
                    pool.dma_start(raw[:, n % RING, :], A["w_down"][m * P:(m + 1) * P, :]).then_inc(raw_in[n % RING], 16)

            for n in range(RING):
                fetch(n)
            for n in range(TILES):
                i, w = n % 2, width(n)
                pool.wait_ge(m_ok, n + 1)
                pool.tensor_tensor(y[:, i, 0:w], y[:, i, 0:w], e[:, i, 0:w], ALU.add).then_inc(t_ok, 1)
                pool.wait_ge(t_ok, n + 1)
                if n >= 2:
                    pool.wait_ge(tr_ok, banks[n - 1])
                pool.tensor_tensor(q16[:, i, 0:w], y[:, i, 0:w], e[:, i, 0:w], ALU.subtract).then_inc(q_ok, 1)
                if n >= 2:
                    pool.wait_ge(sc_ok, n - 1)
                pool.tensor_tensor(diag[:, i, :], ident[:, :], ws[:, n:n + 1].broadcast_to([P, P]),
                                   ALU.mult).then_inc(diag_ok, 1)
                if n + RING < TILES:
                    fetch(n + RING)

        @block.vector
        def _(dve):
            ch = Chain(dve, steps)
            for n in range(TILES):
                i, w = n % 2, width(n)
                src = raw[:, n % RING, 0:w]
                dve.wait_ge(raw_in[n % RING], 16 * (n // RING + 1))
                ch.link(dve.tensor_reduce(am[:, n:n + 1], src, AX.X, ALU.max, apply_absolute_value=True))
                ch.link(dve.tensor_scalar(ws[:, n:n + 1], am[:, n:n + 1], 1.0 / FP8_MAX, None, ALU.mult))
                ch.link(dve.reciprocal(rs[:, n:n + 1], ws[:, n:n + 1]))
                if n >= 2:
                    dve.wait_ge(q_ok, n - 1)
                dve.tensor_scalar(y[:, i, 0:w], src, rs[:, n:n + 1], None, ALU.mult).then_inc(y_ok, 1)
                dve.wait_ge(y_ok, n + 1)
                exponent_power(dve, ch, e[:, i, 0:w], y[:, i, 0:w]).then_inc(m_ok, 1)

        @block.tensor
        def _(pe):
            for n in range(TILES):
                i = n % 2
                pe.wait_ge(q_ok, n + 1)
                for k0, k1 in halves(n):
                    j = banks[n] + (k0 > 0)
                    if j >= 4:
                        pe.wait_ge(tr_read, j - 3)
                    for k in range(k0, k1):
                        ins = pe.transpose(tp[j % 4][:, k - k0, :], q16[:, i, k * P:(k + 1) * P], ident16[:, :])
                    ins.then_inc(tr_ok, 1)
                pe.wait_ge(diag_ok, n + 1)
                if n == 0:
                    pe.wait_ge(ones_ok, 1)
                if n >= 2:
                    pe.wait_ge(sc_read, n - 1)
                pe.matmul(sp_[i][:, :], ones[:, :], diag[:, i, :], start=True, stop=True).then_inc(sc_ok, 1)

        @block.scalar
        def _(act):
            for n in range(TILES):
                i = n % 2
                m = n % KF if n < 2 * KF else n - 2 * KF
                dst = W["gate"] if n < KF else W["up"] if n < 2 * KF else W["ffn_down"]
                for k0, k1 in halves(n):
                    j = banks[n] + (k0 > 0)
                    act.wait_ge(tr_ok, j + 1)
                    act.activation(dst[:, k0:k1, m * P:(m + 1) * P], tp[j % 4][:, 0:k1 - k0, :],
                                   ACT.Copy).then_inc(tr_read, 1)
                row = W["gate_s"] if n < KF else W["up_s"] if n < 2 * KF else W["down_s"]
                act.wait_ge(sc_ok, n + 1)
                act.activation(row[:, m * P:(m + 1) * P], sp_[i][:, :], ACT.Copy).then_inc(sc_read, 1)


def exponent_power(dve, ch, e, y):
    ch.link(dve.tensor_scalar(e.bitcast(U32), y.bitcast(U32), EXPONENT_BITS, None, ALU.bitwise_and))
    return dve.tensor_scalar(e, e, LEAST_NORMAL, ROUNDER, ALU.max, ALU.mult)


def ffn_scratch(nc, ctx, W):
    for name, shape, dt in (("gate", [P, KD, FF], BF16), ("up", [P, KD, FF], BF16), ("ffn_down", [P, KF, D], BF16),
                            ("gate_s", [P, FF], F32), ("up_s", [P, FF], F32), ("down_s", [P, D], F32)):
        W[name] = ctx.enter_context(nc.sbuf_tensor("kept_" + name, shape, dt))


def scratch(nc, ctx):
    def sb(name, shape, dt=F32):
        return ctx.enter_context(nc.sbuf_tensor(name, shape, dt))

    W = {
        "ident": sb("ident", [P, P]), "ident16": sb("ident16", [P, P], BF16),
        "mask": sb("causal_mask", [P, P], BF16),
        "nopeH": sb("nopeH", [P, KQ, NH, P], F16), "nopeL": sb("nopeL", [P, KQ, NH, P], F16),
        "ropeH": sb("ropeH", [P, KQ, GROUPS, 2, P], F16), "ropeL": sb("ropeL", [P, KQ, GROUPS, 2, P], F16),
        "outH": sb("outH", [P, NH, D], F16), "outL": sb("outL", [P, NH, D], F16),
        "down": sb("w_latents", [P, KD, QR + KV + RD]),
    }
    for name, shape in (("qcos", [P, S]), ("qsin", [P, S]), ("kcos", [P, NT, RD // 2]), ("ksin", [P, NT, RD // 2])):
        t = sb(name, shape)
        W[name] = t[:, :] if len(shape) == 2 else t[:, :, :]
    sem = ctx.enter_context(nc.semaphore("constants"))
    with nc.Block() as block:
        @block.gpsimd
        def _(pool):
            pool.memset(W["ident"][:, :], 0.0)
            pool.memset(W["ident16"][:, :], 0.0)
            pool.memset(W["mask"][:, :], 0.0).then_inc(sem, 1)
            pool.wait_ge(sem, 1)
            for name in ("ident", "ident16"):
                t = W[name][:, :]
                pool.affine_select(out=t, in_=t, compare_op=ALU.not_equal, fill=1.0, base=0,
                                   pattern=[[-1, P]], channel_multiplier=1)
            t = W["mask"][:, :]
            pool.affine_select(out=t, in_=t, compare_op=ALU.is_ge, fill=MASK, base=0,
                               pattern=[[-1, P]], channel_multiplier=1).then_inc(sem, 1)
            pool.wait_ge(sem, 2)
    return W


def iteration(heads, tail, latents):
    beside = {
        (0, "group"): ["lat_load 0", "res_load", "out 0", "out 1"],
        (0, "queries"): ["lat_x 0", "out 2", "out 3"],
        (1, "scores"): ["lat_q 0", "out 4"],
        (1, "softmax"): ["out 5", "lat_qn 0"],
        (1, "queries"): ["lat_kv 0", "lat_load 1", "out 6"],
        (2, "scores"): ["out 7", "lat_kvn 0"],
        (2, "values"): ["norm 0", "lat_x 1"],
        (2, "softmax"): ["lat_q 1"],
        (2, "queries"): ["xquant 0"],
        (3, "scores"): ["norm 1", "lat_qn 1"],
        (3, "values"): ["lat_kv 1"],
        (3, "softmax"): ["xquant 1"],
        (3, "queries"): ["lat_kvn 1", "turn_input", "gate_up 0"],
        (4, "scores"): ["gate_up 1"],
        (4, "values"): ["gate_up 2"],
        (4, "queries"): ["gate_up 3"],
        (5, "scores"): ["tquant 0"],
        (5, "values"): ["gate_up 4"],
        (5, "softmax"): ["tquant 1"],
        (5, "queries"): ["gate_up 5"],
        (6, "scores"): ["tquant 2"],
        (6, "values"): ["gate_up 6"],
        (6, "softmax"): ["tquant 3"],
        (6, "queries"): ["gate_up 7"],
        (7, "scores"): ["ffn_turn 0"],
        (7, "values"): ["tquant 4"],
        (7, "softmax"): ["ffn_down 0"],
        (7, "queries"): ["tquant 5"],
        (8, "scores"): ["tquant 6"],
        (8, "values"): ["ffn_norm 0", "tquant 7"],
        (8, "softmax"): ["ffn_turn 1"],
        (9, "values"): ["ffn_down 1"],
        (10, "values"): ["ffn_norm 1", "store"],
    }
    steps = []

    def head(i, name, args):
        if heads:
            steps.extend((name, k) for k in args)
            if name == "group" and i != 0:
                return
        for line in beside.get((i, "values" if name == "head" else name), []):
            step, _, k = line.partition(" ")
            if latents if step.startswith("lat") else tail:
                steps.append((step, int(k or 0)))

    for i in range(PAIRS + 3):
        if i == 0:
            head(i, "group", [0])
        if 1 <= i <= PAIRS:
            head(i, "scores", [i - 1])
        if heads and 2 <= i <= PAIRS + 1:
            steps.append(("turn", 2 * (i - 2)))
        if i >= 3 and heads:
            steps.append(("values", 2 * (i - 3) + 1))
        if heads and 2 <= i <= PAIRS + 1:
            steps += [("turn", 2 * (i - 2) + 1), ("values", 2 * (i - 2))]
        head(i, "values", [])
        if 1 <= i <= PAIRS:
            head(i, "softmax", [i - 1])
        if i < PAIRS:
            head(i, "queries", [i])
        if i in (0, 2, 4) and heads:
            steps.append(("group", i // 2 + 1))
    if latents:
        steps.append(("lat_turn", 0))
    return steps


def layer(nc, A, W, seq, out):
    with ExitStack() as ctx:
        def sb(name, shape, dt=F32):
            return ctx.enter_context(nc.sbuf_tensor(name, shape, dt))

        sems = []

        def sem(name):
            sems.append(ctx.enter_context(nc.semaphore(name)))
            return sems[-1]

        def named(names):
            return [sem(n) for n in names.split()]

        ident, ident16 = W["ident"], W["ident16"]
        x = sb("x", [P, D])
        xT = sb("xT", [P, KD, P])
        squares = sb("squares", [P, QR], BF16)
        ssq, msq, rstd = (sb(n, [P, NT, 2]) for n in ("ssq", "mean_square", "rstd"))
        minus_half, zeros = sb("minus_half", [P, 1]), sb("zeros", [P, 1])
        qn, kn = sb("q_latent", [P, NT, QR]), sb("kv_latent", [P, NT, KV])
        kr = sb("k_rope", [P, NT, 2, 2, RD // 2])
        ka, kb = sb("k_rope_a", [P, 2, RD // 2]), sb("k_rope_b", [P, 2, RD // 2])
        vH, vL = sb("vH", [P, NT, KV], F16), sb("vL", [P, NT, KV], F16)
        qnH, qnL = sb("qnH", [P, KQ, S], F16), sb("qnL", [P, KQ, S], F16)
        knH, knL = sb("knH", [P, S], F16), sb("knL", [P, S], F16)
        krH, krL = sb("krH", [P, S], F16), sb("krL", [P, S], F16)
        ab = sb("ab_cos_sin", [P, 2, 2, S])
        ro = ab[:, :, 0, :]
        roH, roL = sb("ropeH_out", [P, 2, S], F16), sb("ropeL_out", [P, 2, S], F16)
        qr = sb("q_rope", [P, NH, S], F16)
        qpH, qpL = sb("qpH", [P, 2, 2, S], F16), sb("qpL", [P, 2, 2, S], F16)
        nmax, rsum, rinv = (sb(n, [P, 2, NT, 2]) for n in ("nmax", "rsum", "rinv"))
        pr = sb("probs", [P, 2, 2, P + S])
        ptH, ptL = sb("ptH", [P, 2, P + S], F16), sb("ptL", [P, 2, P + S], F16)
        oH, oL = sb("oH", [P, NH, S], F16), sb("oL", [P, NH, S], F16)
        res = sb("residual", [P, NT, D])
        st6 = sb("bn_stats", [P, NT, 6])
        mv = sb("mean_var", [P, NT, 2])
        veps, lrs, am, sx, rsx, hsx, tm, tsc, trs, tst = (
            sb(n, [P, NT]) for n in "var_eps ln_rstd absmax x_scale x_rscale half_x_scale t_absmax t_scale "
                                    "t_rscale t_out_scale".split())
        tm4 = sb("t_absmax_chunks", [P, NT, NCH])
        t = sb("hidden", [P, FF])
        xq = t[:, 0:NT * D // 2].bitcast(BF16).rearrange("p (n l) -> p n l", n=NT)
        ye = sb("fp8_scratch", [P, 2, CH])
        y, e = ye[:, 0, :], ye[:, 1, :]
        y_out = ye[:, :, :].rearrange("p a c -> p (a c)")[:, 0:D]
        g1, u1 = sb("g1", [P, CH]), sb("u1", [P, CH])
        tq = sb("tq", [P, FF], BF16)
        turned = sb("ffn_turned", [P, FF], BF16)
        xqT = turned[:, 0:KD * S].rearrange("p (k s) -> p k s", k=KD)
        tqT = turned[:, :].rearrange("p (k s) -> p k s", k=KF)

        G = [ctx.enter_context(nc.psum_tensor(f"G{i}", [P, 512], F32)) for i in range(3)]
        SB = [ctx.enter_context(nc.psum_tensor(f"scores{i}", [P, 512], F32)) for i in range(2)]
        PT = ctx.enter_context(nc.psum_tensor("probsT", [P, P + S], F32))
        OT = ctx.enter_context(nc.psum_tensor("outT", [P, 2, S], F32))
        QP = ctx.enter_context(nc.psum_tensor("projections", [P, 2, S], F32))

        x_in, res_in, out_in, half_ok = named("x_in res_in out_in half_ok")
        xT_ps, xT_sb, lat_ps, ssq_ok, msq_ok, rstd_ok = named("xT_ps xT_sb lat_ps ssq_ok msq_ok rstd_ok")
        lq_ok, lkv_ok, lat_sb, latT_ps, latT_hi, latT_lo = named("lq_ok lkv_ok lat_sb latT_ps latT_hi latT_lo")
        ab_ps, ab_read, ro_ok, roh_ok, rol_ok = named("ab_ps ab_read ro_ok roh_ok rol_ok")
        qr_in = [sem(f"qr_in{g}") for g in range(GROUPS)]
        qp_ps, qp_hi, qp_lo, s_ps, s_max, p_exp, p_inv, p_norm = named(
            "qp_ps qp_hi qp_lo s_ps s_max p_exp p_inv p_norm")
        pt_ps, pt_hi, pt_lo, o_ps, o_hi, o_lo, o_used = named("pt_ps pt_hi pt_lo o_ps o_hi o_lo o_used")
        var_ok, lrs_ok, stats_ok, xq_ok, xqT_ps, xqT_sb = named("var_ok lrs_ok stats_ok xq_ok xqT_ps xqT_sb")
        gu_ps, g1_ok, u1_ok, th_ok, t_ok, ty_ok, tq_ok = named("gu_ps g1_ok u1_ok th_ok t_ok ty_ok tq_ok")
        tqT_ps, tqT_sb, d_ps, d_read, out_ok = named("tqT_ps tqT_sb d_ps d_read out_ok")
        head_steps, tail_steps, lat_steps = named("dve_head_steps dve_tail_steps dve_lat_steps")
        HEAD_STEPS, TAIL_STEPS, LAT_STEPS = PAIRS, 78, 3
        NCK = NT * NCH
        with nc.Block() as priming:
            @priming.sync
            def _(sp):
                for s in sems:
                    sp.sem_inc(s, PRIMED)
        block = ctx.enter_context(nc.Block())

        def turns(eng, part):
            part(-1, iteration(False, False, True))
            part(0, iteration(True, False, True))
            with eng.Fori(1, NB - 1) as b:
                part(b, iteration(True, True, True))
            part(NB - 1, iteration(True, True, False))
            part(NB, iteration(False, True, False))

        @block.sync
        def _(sp):
            def part(b, steps):
                tail, lat = b - 1, b + 1
                names = [s for s, _ in steps]
                if "lat_load" in names:
                    tokens = [seq[bass.ds(lat, 1), n * P:(n + 1) * P, :].rearrange("o p l -> p (o l)") for n in range(NT)]
                if "res_load" in names:
                    whole = seq[bass.ds(tail, 1), :, :].rearrange("o (t p) l -> p (o t) l", p=P)
                    result = out[bass.ds(tail, 1), :, :].rearrange("o (t p) l -> p (o t) l", p=P)
                for step, i in steps:
                    if step == "lat_load":
                        sp.wait_ge(xT_ps, PRIMED + NT * lat + i)
                        sp.dma_start(x[:, :], tokens[i]).then_inc(x_in, 16)
                    if step == "res_load":
                        sp.wait_ge(out_in, PRIMED + 16 * tail)
                        sp.dma_start(res[:, :, :], whole).then_inc(res_in, 16)
                    if step == "group":
                        sp.wait_ge(rol_ok, PRIMED + GROUPS * b + i + 1)
                        for half, src in ((0, roH), (1, roL)):
                            for c in range(2):
                                for j in range(4):
                                    row = 64 * half + 32 * c
                                    sp.dma_start(qr[row:row + 32, 4 * i + j, :], src[32 * j:32 * j + 32, c, :]
                                                 ).then_inc(qr_in[i], 16)
                    if step == "store":
                        sp.wait_ge(out_ok, PRIMED + NT * (tail + 1))
                        sp.dma_start(result, res[:, :, :]).then_inc(out_in, 16)

            turns(sp, part)
            sp.wait_ge(out_in, PRIMED + 16 * NB)

        @block.tensor
        def _(pe):
            def split_product(dst, aH, aL, bH, bL, first, last):
                pe.matmul(dst, aH, bH, start=first, stop=False)
                pe.matmul(dst, aH, bL, start=False, stop=False)
                return pe.matmul(dst, aL, bH, start=False, stop=last)

            def project(dst, wH, wL):
                for k in range(KQ):
                    ins = split_product(dst, wH(k), wL(k), qnH[:, k, :], qnL[:, k, :], k == 0, k == KQ - 1)
                return ins

            def lat_x(lat, n):
                pe.wait_ge(x_in, PRIMED + 16 * (NT * lat + n + 1))
                if n == 0:
                    pe.wait_ge(latT_lo, PRIMED + 3 * lat)
                else:
                    pe.wait_ge(lkv_ok, PRIMED + NT * lat + n)
                for k in range(KD):
                    ins = pe.transpose(G[2][:, k * P:(k + 1) * P], x[:, k * P:(k + 1) * P], ident[:, :])
                ins.then_inc(xT_ps, 1)

            def lat_q(lat, n):
                pe.wait_ge(xT_sb, PRIMED + NT * lat + n + 1)
                for k in range(KD):
                    ins = pe.matmul(G[2][:, 0:QR], xT[:, k, :], W["down"][:, k, 0:QR], start=(k == 0), stop=(k == KD - 1))
                ins.then_inc(lat_ps, 1)

            def lat_kv(lat, n):
                pe.wait_ge(lq_ok, PRIMED + NT * lat + n + 1)
                for k in range(KD):
                    ins = pe.matmul(G[2][:, 0:KV + RD], xT[:, k, :], W["down"][:, k, QR:], start=(k == 0),
                                    stop=(k == KD - 1))
                ins.then_inc(lat_ps, 1)

            def lat_turn(lat, tail):
                pe.wait_ge(lat_sb, PRIMED + NT * (lat + 1))
                if tail is not None:
                    pe.wait_ge(tqT_sb, PRIMED + 2 * NT * (tail + 1))
                    pe.wait_ge(d_read, PRIMED + NT * (tail + 1))
                for i in range(2):
                    for k in range(2):
                        for n in range(NT):
                            m = 2 * i + k
                            src = qn[:, n, m * P:(m + 1) * P] if m < KQ else kn[:, n, :]
                            ins = pe.transpose(G[i][:, k * S + n * P:k * S + (n + 1) * P], src, ident[:, :])
                    ins.then_inc(latT_ps, 1)
                for n in range(NT):
                    ins = pe.transpose(G[2][:, n * P:(n + 1) * P], kr[:, n, :, :, :], ident[:, :])
                ins.then_inc(latT_ps, 1)

            def group(b, g):
                if g == 0:
                    pe.wait_ge(latT_hi, PRIMED + 3 * b + 3)
                    pe.wait_ge(latT_lo, PRIMED + 3 * b + 3)
                pe.wait_ge(qp_lo, PRIMED + PAIRS * b + (0, 1, 3, 5)[g])
                for c in range(2):
                    ins = project(QP[:, c, :], lambda k: W["ropeH"][:, k, g, c, :], lambda k: W["ropeL"][:, k, g, c, :])
                ins.then_inc(ab_ps, 1)

            def queries(b, i):
                pe.wait_ge(qp_lo, PRIMED + PAIRS * b + i)
                pe.wait_ge(ab_read, PRIMED + GROUPS * b + (1, 2, 2, 3, 3, 4, 4, 4)[i])
                for c in range(2):
                    h = 2 * i + c
                    ins = project(QP[:, c, :], lambda k: W["nopeH"][:, k, h, :], lambda k: W["nopeL"][:, k, h, :])
                ins.then_inc(qp_ps, 1)

            def scores(b, i):
                pe.wait_ge(qp_hi, PRIMED + PAIRS * b + i + 1)
                pe.wait_ge(qp_lo, PRIMED + PAIRS * b + i + 1)
                if i % 2 == 0:
                    pe.wait_ge(qr_in[i // 2], PRIMED + 256 * (b + 1))
                pe.wait_ge(p_exp, PRIMED + PAIRS * b + i)
                for c in range(2):
                    h = 2 * i + c
                    for n in range(NT):
                        keys = slice(0, (n + 1) * P)
                        cols = slice(n * P, n * P + (n + 1) * P)
                        dst = SB[c][:, cols]
                        q = slice(n * P, (n + 1) * P)
                        split_product(dst, qpH[:, i % 2, c, q], qpL[:, i % 2, c, q], knH[:, keys], knL[:, keys], True, False)
                        pe.matmul(dst, qr[:, h, q], krH[:, keys], start=False, stop=False)
                        pe.matmul(dst, qr[0:64, h, q], krL[0:64, keys], start=False, stop=False)
                        ins = pe.matmul(SB[c][:, cols.stop - P:cols.stop], ident16[:, :], W["mask"][:, :],
                                        start=False, stop=True)
                    ins.then_inc(s_ps, 1)

            def turn(b, h):
                i, c = h // 2, h % 2
                pe.wait_ge(p_norm, PRIMED + PAIRS * b + i + 1)
                pe.wait_ge(pt_hi, PRIMED + NH * b + h)
                pe.wait_ge(pt_lo, PRIMED + NH * b + h)
                for k in range(3):
                    ins = pe.transpose(PT[:, k * P:(k + 1) * P], pr[:, i % 2, c, k * P:(k + 1) * P], ident[:, :])
                ins.then_inc(pt_ps, 1)

            def values(b, h):
                i, c = h // 2, h % 2
                pe.wait_ge(pt_hi, PRIMED + NH * b + h + 1)
                pe.wait_ge(pt_lo, PRIMED + NH * b + h + 1)
                if c == 0:
                    pe.wait_ge(o_hi, PRIMED + PAIRS * b + i)
                    pe.wait_ge(o_lo, PRIMED + PAIRS * b + i)
                split_product(OT[:, c, :], vH[:, 0, :], vL[:, 0, :], ptH[:, c, 0:S], ptL[:, c, 0:S], True, False)
                ins = split_product(OT[:, c, P:S], vH[:, 1, :], vL[:, 1, :], ptH[:, c, S:], ptL[:, c, S:], False, True)
                ins.then_inc(o_ps, 1)

            def output(tail, i, turned_latents):
                if i == 0:
                    pe.wait_ge(o_hi, PRIMED + PAIRS * (tail + 1))
                    pe.wait_ge(o_lo, PRIMED + PAIRS * (tail + 1))
                    if turned_latents:
                        pe.wait_ge(latT_lo, PRIMED + 3 * (tail + 2))
                    else:
                        pe.wait_ge(out_ok, PRIMED + NT * tail)
                for n in range(NT):
                    q = slice(n * P, (n + 1) * P)
                    for h in (2 * i, 2 * i + 1):
                        ins = split_product(G[n][:, :], oH[:, h, q], oL[:, h, q], W["outH"][:, h, :],
                                            W["outL"][:, h, :], h == 0, h == NH - 1)
                ins.then_inc(o_used, 1)

            def turn_input(tail, with_latents):
                pe.wait_ge(xq_ok, PRIMED + NT * (tail + 1))
                if with_latents:
                    pe.wait_ge(lkv_ok, PRIMED + NT * (tail + 3))
                dst = G[2][:, :].bitcast(BF16).rearrange("p (k s) -> p k s", k=KD)
                for n in range(NT):
                    for k in range(KD):
                        ins = pe.transpose(dst[:, k, n * P:(n + 1) * P], xq[:, n, k * P:(k + 1) * P], ident16[:, :])
                ins.then_inc(xqT_ps, 1)

            def gate_up(tail, k):
                n, c = k // NCH, k % NCH
                if k == 0:
                    pe.wait_ge(xqT_sb, PRIMED + tail + 1)
                pe.wait_ge(u1_ok, PRIMED + NCK * tail + k)
                for r, w in enumerate((W["gate"], W["up"])):
                    for m in range(KD):
                        ins = pe.matmul(G[r][:, 0:CH], xqT[:, m, n * P:(n + 1) * P], w[:, m, c * CH:(c + 1) * CH],
                                        start=(m == 0), stop=(m == KD - 1))
                    ins.then_inc(gu_ps, 1)

            def ffn_turn(tail, n):
                pe.wait_ge(tq_ok, PRIMED + NCK * tail + NCH * (n + 1))
                pe.wait_ge(u1_ok, PRIMED + NCK * (tail + 1))
                pe.wait_ge(tqT_sb, PRIMED + 2 * (NT * tail + n))
                for m in range(KF):
                    dst = G[m // 8][:, :].bitcast(BF16)[:, m % 8 * P:(m % 8 + 1) * P]
                    ins = pe.transpose(dst, tq[:, m * P:(m + 1) * P], ident16[:, :])
                    if m in (7, KF - 1):
                        ins.then_inc(tqT_ps, 1)

            def ffn_down(tail, n):
                pe.wait_ge(tqT_sb, PRIMED + 2 * (NT * tail + n) + 2)
                pe.wait_ge(d_read, PRIMED + NT * tail + n)
                for m in range(KF):
                    ins = pe.matmul(G[2][:, :], tqT[:, m, :], W["ffn_down"][:, m, :], start=(m == 0), stop=(m == KF - 1))
                ins.then_inc(d_ps, 1)

            def part(b, steps):
                names = {s for s, _ in steps}
                has_tail, has_lat, has_heads = "out" in names, "lat_x" in names, "scores" in names
                for step, i in steps:
                    if step == "lat_x":
                        lat_x(b + 1, i)
                    elif step == "lat_q":
                        lat_q(b + 1, i)
                    elif step == "lat_kv":
                        lat_kv(b + 1, i)
                    elif step == "lat_turn":
                        lat_turn(b + 1, b - 1 if has_tail else None)
                    elif step == "group":
                        group(b, i)
                    elif step == "queries":
                        queries(b, i)
                    elif step == "scores":
                        scores(b, i)
                    elif step == "turn":
                        turn(b, i)
                    elif step == "values":
                        values(b, i)
                    elif step == "out":
                        output(b - 1, i, has_heads)
                    elif step == "turn_input":
                        turn_input(b - 1, has_lat)
                    elif step == "gate_up":
                        gate_up(b - 1, i)
                    elif step == "ffn_turn":
                        ffn_turn(b - 1, i)
                    elif step == "ffn_down":
                        ffn_down(b - 1, i)

            turns(pe, part)

        @block.scalar
        def _(act):
            def lat_x(lat, n):
                act.wait_ge(xT_ps, PRIMED + NT * lat + n + 1)
                act.activation(xT[:, :, :], G[2][:, :].rearrange("p (k s) -> p k s", k=KD), ACT.Copy).then_inc(xT_sb, 1)

            def mean_square(lat, n, r, width):
                k = 2 * (NT * lat + n) + r
                act.wait_ge(lat_ps, PRIMED + k + 1)
                act.wait_ge(ssq_ok, PRIMED + k)
                act.activation(squares[:, 0:width], G[2][:, 0:width], ACT.Square,
                               accum_out=ssq[:, n, r:r + 1]).then_inc(ssq_ok, 1)

            def lat_turn(lat):
                act.wait_ge(latT_ps, PRIMED + 3 * lat + 1)
                act.activation(qnH[:, 0:2, :], G[0][:, :].rearrange("p (k s) -> p k s", k=2), ACT.Copy).then_inc(latT_hi, 1)
                act.wait_ge(latT_ps, PRIMED + 3 * lat + 2)
                act.activation(qnH[:, 2, :], G[1][:, 0:S], ACT.Copy)
                act.activation(knH[:, :], G[1][:, S:2 * S], ACT.Copy).then_inc(latT_hi, 1)
                act.wait_ge(latT_ps, PRIMED + 3 * lat + 3)
                act.activation(krH[:, :], G[2][:, 0:S], ACT.Copy).then_inc(latT_hi, 1)

            def queries(b, i):
                act.wait_ge(qp_ps, PRIMED + PAIRS * b + i + 1)
                if i >= 2:
                    act.wait_ge(s_ps, PRIMED + NH * b + 2 * (i - 1))
                act.activation(qpH[:, i % 2, :, :], QP[:, :, :], ACT.Copy).then_inc(qp_hi, 1)

            def softmax(b, i):
                act.wait_ge(s_max, PRIMED + PAIRS * b + i + 1)
                if i >= 2:
                    act.wait_ge(pt_ps, PRIMED + NH * b + 2 * (i - 1))
                for n in range(NT):
                    cols = slice(n * P, n * P + (n + 1) * P)
                    for c in range(2):
                        ins = act.activation(pr[:, i % 2, c, cols], SB[c][:, cols], ACT.Exp, bias=nmax[:, i % 2, n, c:c + 1],
                                             scale=SCALE / S_NOPE, accum_out=rsum[:, i % 2, n, c:c + 1])
                ins.then_inc(p_exp, 1)

            def turn(b, h):
                act.wait_ge(pt_ps, PRIMED + NH * b + h + 1)
                if h >= 2:
                    act.wait_ge(o_ps, PRIMED + NH * b + h - 1)
                act.activation(ptH[:, h % 2, :], PT[:, :], ACT.Copy).then_inc(pt_hi, 1)

            def values(b, h, has_tail):
                if h % 2 == 0:
                    return
                i = h // 2
                act.wait_ge(o_ps, PRIMED + NH * b + h + 1)
                if has_tail:
                    act.wait_ge(o_used, PRIMED + PAIRS * (b - 1) + i + 1)
                act.activation(oH[:, 2 * i:2 * i + 2, :], OT[:, :, :], ACT.Copy).then_inc(o_hi, 1)

            def turn_input(tail):
                act.wait_ge(xqT_ps, PRIMED + tail + 1)
                act.activation(xqT, G[2][:, :].bitcast(BF16).rearrange("p (k s) -> p k s", k=KD), ACT.Copy).then_inc(xqT_sb, 1)

            def gate_up(tail, k):
                act.wait_ge(t_ok, PRIMED + 3 * (NCK * tail + k) + 1)
                act.activation(g1[:, :], g1[:, :], ACT.Tanh, scale=hsx[:, k // NCH:k // NCH + 1]).then_inc(th_ok, 1)

            def ffn_turn(tail, n):
                for r, (k0, k1) in enumerate(((0, 8), (8, KF))):
                    act.wait_ge(tqT_ps, PRIMED + 2 * (NT * tail + n) + r + 1)
                    act.activation(turned[:, k0 * P:k1 * P], G[r][:, :].bitcast(BF16)[:, 0:(k1 - k0) * P],
                                   ACT.Copy).then_inc(tqT_sb, 1)

            def part(b, steps):
                has_tail = ("out", 0) in steps
                for step, i in steps:
                    if step == "lat_x":
                        lat_x(b + 1, i)
                    elif step == "lat_q":
                        mean_square(b + 1, i, 0, QR)
                    elif step == "lat_kv":
                        mean_square(b + 1, i, 1, KV)
                    elif step == "lat_turn":
                        lat_turn(b + 1)
                    elif step == "queries":
                        queries(b, i)
                    elif step == "softmax":
                        softmax(b, i)
                    elif step == "turn":
                        turn(b, i)
                    elif step == "values":
                        values(b, i, has_tail)
                    elif step == "turn_input":
                        turn_input(b - 1)
                    elif step == "gate_up":
                        gate_up(b - 1, i)
                    elif step == "ffn_turn":
                        ffn_turn(b - 1, i)

            turns(act, part)

        @block.gpsimd
        def _(pool):
            def lat_rstd(lat, n, r):
                k = 2 * (NT * lat + n) + r
                pool.wait_ge(msq_ok, PRIMED + k + 1)
                pool.tensor_tensor(rstd[:, n, r:r + 1], msq[:, n, r:r + 1], minus_half[:, :], ALU.pow).then_inc(rstd_ok, 1)

            def norm_rstd(tail, k):
                n = k % NT
                pool.wait_ge(var_ok, PRIMED + 2 * NT * tail + k + 1)
                pool.tensor_tensor(lrs[:, n:n + 1], veps[:, n:n + 1], minus_half[:, :], ALU.pow).then_inc(lrs_ok, 1)

            def group(b, g):
                n = GROUPS * b + g
                pool.wait_ge(ab_read, PRIMED + n + 1)
                pool.tensor_tensor(ab[:, 0, 0, :], ab[:, 0, 0, :], ab[:, 1, 1, :], ALU.subtract)
                pool.tensor_tensor(ab[:, 1, 0, :], ab[:, 1, 0, :], ab[:, 0, 1, :], ALU.add).then_inc(ro_ok, 1)
                pool.wait_ge(ro_ok, PRIMED + n + 1)
                if g:
                    pool.wait_ge(qr_in[g - 1], PRIMED + 256 * (b + 1))
                else:
                    pool.wait_ge(qr_in[GROUPS - 1], PRIMED + 256 * b)
                pool.tensor_tensor(roH[:, :, :], ro, zeros[:, 0:1].unsqueeze(1).broadcast_to([P, 2, S]),
                                   ALU.add).then_inc(roh_ok, 1)
                pool.wait_ge(roh_ok, PRIMED + n + 1)
                pool.tensor_tensor(roL[:, :, :], ro, roH[:, :, :], ALU.subtract).then_inc(rol_ok, 1)

            def softmax(b, i):
                pool.wait_ge(p_inv, PRIMED + PAIRS * b + i + 1)
                for n in range(NT):
                    w = (n + 1) * P
                    p = pr[:, i % 2, :, n * P:n * P + w]
                    ins = pool.tensor_tensor(p, p, rinv[:, i % 2, n, :].unsqueeze(2).broadcast_to([P, 2, w]), ALU.mult)
                ins.then_inc(p_norm, 1)

            def gate_up(tail, k):
                u = NCK * tail + k
                cols = slice(k % NCH * CH, (k % NCH + 1) * CH)
                pool.wait_ge(u1_ok, PRIMED + u + 1)
                pool.tensor_tensor(u1[:, :], g1[:, :], u1[:, :], ALU.mult).then_inc(t_ok, 1)
                pool.wait_ge(t_ok, PRIMED + 3 * u + 1)
                pool.wait_ge(th_ok, PRIMED + u + 1)
                if k >= NCH:
                    pool.wait_ge(ty_ok, PRIMED + NCK * tail + k - NCH + 1)
                pool.tensor_tensor(t[:, cols], g1[:, :], u1[:, :], ALU.mult).then_inc(t_ok, 1)
                pool.wait_ge(t_ok, PRIMED + 3 * u + 2)
                pool.tensor_tensor(t[:, cols], t[:, cols], u1[:, :], ALU.add).then_inc(t_ok, 1)

            def part(b, steps):
                for step, i in steps:
                    if step == "lat_q":
                        lat_rstd(b + 1, i, 0)
                    elif step == "lat_kv":
                        lat_rstd(b + 1, i, 1)
                    elif step == "group":
                        group(b, i)
                    elif step == "softmax":
                        softmax(b, i)
                    elif step == "norm":
                        norm_rstd(b - 1, i)
                    elif step == "gate_up":
                        gate_up(b - 1, i)
                    elif step == "ffn_norm":
                        norm_rstd(b - 1, NT + i)

            pool.memset(zeros[:, :], 0.0)
            pool.memset(minus_half[:, :], -0.5).then_inc(half_ok, 1)
            pool.wait_ge(half_ok, PRIMED + 1)
            turns(pool, part)

        @block.vector
        def _(dve):
            heads, tails, lats = Chain(dve, head_steps), Chain(dve, tail_steps), Chain(dve, lat_steps)
            tt, ts = dve.tensor_tensor, dve.tensor_scalar

            def mean(lat, n, r, width):
                k = 2 * (NT * lat + n) + r
                dve.wait_ge(ssq_ok, PRIMED + k + 1)
                ts(msq[:, n, r:r + 1], ssq[:, n, r:r + 1], 1.0 / width, EPS_RMS, ALU.mult, ALU.add).then_inc(msq_ok, 1)

            def lat_qn(lat, n):
                dve.wait_ge(rstd_ok, PRIMED + 2 * (NT * lat + n) + 1)
                dve.wait_ge(latT_ps, PRIMED + 3 * lat)
                ts(qn[:, n, :], G[2][:, 0:QR], rstd[:, n, 0:1], None, ALU.mult).then_inc(lq_ok, 1)

            def lat_kvn(lat, n):
                dve.wait_ge(rstd_ok, PRIMED + 2 * (NT * lat + n) + 2)
                ts(kn[:, n, :], G[2][:, 0:KV], rstd[:, n, 1:2], None, ALU.mult)
                pairs = G[2][:, KV:KV + RD].rearrange("p (i two) -> p two i", two=2)
                cos, sin = (W[name][:, n:n + 1, :].broadcast_to([P, 2, RD // 2]) for name in ("kcos", "ksin"))
                tt(ka[:, :, :], pairs, cos, ALU.mult)
                tt(kb[:, :, :], pairs, sin, ALU.mult).then_inc(lkv_ok, 1)
                dve.wait_ge(lkv_ok, PRIMED + NT * lat + n + 1)
                tt(kr[:, n, 0, 0, :], ka[:, 0, :], kb[:, 1, :], ALU.subtract)
                lats.link(tt(kr[:, n, 0, 1, :], kb[:, 0, :], ka[:, 1, :], ALU.add))
                dve.tensor_copy(kr[:, n, 1, :, :], kr[:, n, 0, :, :]).then_inc(lat_sb, 1)

            def lat_turn(lat):
                dve.wait_ge(latT_ps, PRIMED + 3 * lat + 3)
                lats.link(dve.tensor_copy(vH[:, :, :], kn[:, :, :]))
                tt(vL[:, :, :], kn[:, :, :], vH[:, :, :], ALU.subtract)
                dve.wait_ge(latT_hi, PRIMED + 3 * lat + 1)
                tt(qnL[:, 0:2, :], G[0][:, :].rearrange("p (k s) -> p k s", k=2), qnH[:, 0:2, :], ALU.subtract
                   ).then_inc(latT_lo, 1)
                dve.wait_ge(latT_hi, PRIMED + 3 * lat + 2)
                tt(qnL[:, 2, :], G[1][:, 0:S], qnH[:, 2, :], ALU.subtract)
                tt(knL[:, :], G[1][:, S:2 * S], knH[:, :], ALU.subtract).then_inc(latT_lo, 1)
                dve.wait_ge(latT_hi, PRIMED + 3 * lat + 3)
                tt(krL[0:64, :], G[2][0:64, 0:S], krH[0:64, :], ALU.subtract).then_inc(latT_lo, 1)

            def group(b, g):
                dve.wait_ge(ab_ps, PRIMED + GROUPS * b + g + 1)
                dve.wait_ge(rol_ok, PRIMED + GROUPS * b + g)
                tt(ab[:, :, 0, :], QP[:, :, :], W["qcos"].unsqueeze(1).broadcast_to([P, 2, S]), ALU.mult)
                tt(ab[:, :, 1, :], QP[:, :, :], W["qsin"].unsqueeze(1).broadcast_to([P, 2, S]), ALU.mult
                   ).then_inc(ab_read, 1)

            def queries(b, i):
                dve.wait_ge(qp_hi, PRIMED + PAIRS * b + i + 1)
                tt(qpL[:, i % 2, :, :], QP[:, :, :], qpH[:, i % 2, :, :], ALU.subtract).then_inc(qp_lo, 1)

            def scores(b, i):
                for c in range(2):
                    dve.wait_ge(s_ps, PRIMED + NH * b + 2 * i + c + 1)
                    for n in range(NT):
                        ins = dve.tensor_reduce(nmax[:, i % 2, n, c:c + 1], SB[c][:, n * P:n * P + (n + 1) * P], AX.X,
                                                ALU.max, negate=True)
                heads.link(ins)
                ts(nmax[:, i % 2, :, :], nmax[:, i % 2, :, :], SCALE / S_NOPE, None, ALU.mult).then_inc(s_max, 1)

            def softmax(b, i):
                dve.wait_ge(p_exp, PRIMED + PAIRS * b + i + 1)
                dve.reciprocal(rinv[:, i % 2, :, :], rsum[:, i % 2, :, :]).then_inc(p_inv, 1)

            def turn(b, h):
                dve.wait_ge(pt_hi, PRIMED + NH * b + h + 1)
                tt(ptL[:, h % 2, :], PT[:, :], ptH[:, h % 2, :], ALU.subtract).then_inc(pt_lo, 1)

            def values(b, h):
                if h % 2:
                    i = h // 2
                    dve.wait_ge(o_hi, PRIMED + PAIRS * b + i + 1)
                    tt(oL[:, 2 * i:2 * i + 2, :], OT[:, :, :], oH[:, 2 * i:2 * i + 2, :], ALU.subtract).then_inc(o_lo, 1)

            def norm(tail, k):
                n = k % NT
                tails.link(dve.bn_stats(st6[:, n, :], res[:, n, :]))
                dve.sem_inc(stats_ok, 1)
                tails.link(dve.bn_aggr(mv[:, n, :], st6[:, n, :]))
                ts(veps[:, n:n + 1], mv[:, n, 1:2], EPS_LN, None, ALU.add).then_inc(var_ok, 1)
                dve.wait_ge(lrs_ok, PRIMED + 2 * NT * tail + k + 1)
                return ts(res[:, n, :], res[:, n, :], mv[:, n, 0:1], lrs[:, n:n + 1], ALU.subtract, ALU.mult)

            def attention_norm(tail, n):
                dve.wait_ge(o_used, PRIMED + PAIRS * (tail + 1))
                dve.wait_ge(res_in, PRIMED + 16 * (tail + 1))
                tails.link(dve.scalar_tensor_tensor(out=res[:, n, :], in0=G[n][:, :], scalar=1.0 / S_VO,
                                                    in1=res[:, n, :], op0=ALU.mult, op1=ALU.add))
                tails.link(norm(tail, n))

            def xquant(tail, n):
                tails.link(dve.tensor_reduce(am[:, n:n + 1], res[:, n, :], AX.X, ALU.max, apply_absolute_value=True))
                tails.link(ts(sx[:, n:n + 1], am[:, n:n + 1], 1.0 / FP8_MAX, None, ALU.mult))
                ts(hsx[:, n:n + 1], sx[:, n:n + 1], 0.5, None, ALU.mult)
                tails.link(dve.reciprocal(rsx[:, n:n + 1], sx[:, n:n + 1]))
                half = D // 2
                for c in range(2):
                    cols = slice(c * half, (c + 1) * half)
                    tails.link(ts(y[:, 0:half], res[:, n, cols], rsx[:, n:n + 1], None, ALU.mult))
                    ins = round_fp8(xq[:, n, cols], half)
                    if c == 0:
                        tails.link(ins)
                ins.then_inc(xq_ok, 1)

            def round_fp8(dst, w):
                tails.link(exponent_power(dve, tails, e[:, 0:w], y[:, 0:w]))
                tails.link(tt(y[:, 0:w], y[:, 0:w], e[:, 0:w], ALU.add))
                return tt(dst, y[:, 0:w], e[:, 0:w], ALU.subtract)

            def chunk_absmax(tail, k):
                n, c = k // NCH, k % NCH
                dve.wait_ge(t_ok, PRIMED + 3 * (NCK * tail + k + 1))
                tails.link(dve.tensor_reduce(tm4[:, n, c:c + 1], t[:, c * CH:(c + 1) * CH], AX.X, ALU.max,
                                             apply_absolute_value=True))

            def gate_up(tail, k):
                u = NCK * tail + k
                cols = slice(k % NCH * CH, (k % NCH + 1) * CH)
                dve.wait_ge(gu_ps, PRIMED + 2 * u + 1)
                dve.wait_ge(t_ok, PRIMED + 3 * u)
                tt(g1[:, :], G[0][:, 0:CH], W["gate_s"][:, cols], ALU.mult).then_inc(g1_ok, 1)
                dve.wait_ge(gu_ps, PRIMED + 2 * u + 2)
                tt(u1[:, :], G[1][:, 0:CH], W["up_s"][:, cols], ALU.mult).then_inc(u1_ok, 1)
                if k % NCH:
                    chunk_absmax(tail, k - 1)

            def tquant(tail, k):
                n, c = k // NCH, k % NCH
                cols = slice(c * CH, (c + 1) * CH)
                s = slice(n, n + 1)
                if c == 0:
                    chunk_absmax(tail, k + NCH - 1)
                    tails.link(dve.tensor_reduce(tm[:, s], tm4[:, n, :], AX.X, ALU.max))
                    tails.link(ts(tsc[:, s], tm[:, s], 1.0 / FP8_MAX, None, ALU.mult))
                    tails.link(dve.reciprocal(trs[:, s], tsc[:, s]))
                    tails.link(dve.scalar_tensor_tensor(out=tst[:, s], in0=sx[:, s], scalar=hsx[:, s], in1=tsc[:, s],
                                                        op0=ALU.mult, op1=ALU.mult))
                    dve.wait_ge(tqT_ps, PRIMED + 2 * (NT * tail + n))
                ts(y[:, :], t[:, cols], trs[:, s], None, ALU.mult).then_inc(ty_ok, 1)
                dve.wait_ge(ty_ok, PRIMED + NCK * tail + k + 1)
                round_fp8(tq[:, cols], CH).then_inc(tq_ok, 1)
                dve.wait_ge(tq_ok, PRIMED + NCK * tail + k + 1)

            def ffn_norm(tail, n):
                dve.wait_ge(d_ps, PRIMED + NT * tail + n + 1)
                tt(y_out, G[2][:, :], W["down_s"][:, :], ALU.mult).then_inc(d_read, 1)
                dve.wait_ge(d_read, PRIMED + NT * tail + n + 1)
                tails.link(dve.scalar_tensor_tensor(out=res[:, n, :], in0=y_out, scalar=tst[:, n:n + 1],
                                                    in1=res[:, n, :], op0=ALU.mult, op1=ALU.add))
                norm(tail, NT + n).then_inc(out_ok, 1)

            def part(b, steps):
                heads.base, heads.n = PRIMED + HEAD_STEPS * b, 0
                tails.base, tails.n = PRIMED + TAIL_STEPS * (b - 1), 0
                lats.base, lats.n = PRIMED + LAT_STEPS * (b + 1), 0
                for step, i in steps:
                    if step == "lat_q":
                        mean(b + 1, i, 0, QR)
                    elif step == "lat_qn":
                        lat_qn(b + 1, i)
                    elif step == "lat_kv":
                        mean(b + 1, i, 1, KV)
                    elif step == "lat_kvn":
                        lat_kvn(b + 1, i)
                    elif step == "lat_turn":
                        lat_turn(b + 1)
                    elif step == "group":
                        group(b, i)
                    elif step == "queries":
                        queries(b, i)
                    elif step == "scores":
                        scores(b, i)
                    elif step == "softmax":
                        softmax(b, i)
                    elif step == "turn":
                        turn(b, i)
                    elif step == "values":
                        values(b, i)
                    elif step == "norm":
                        attention_norm(b - 1, i)
                    elif step == "xquant":
                        xquant(b - 1, i)
                    elif step == "gate_up":
                        gate_up(b - 1, i)
                    elif step == "tquant":
                        tquant(b - 1, i)
                    elif step == "ffn_norm":
                        ffn_norm(b - 1, i)
                for chain, count in ((heads, HEAD_STEPS), (tails, TAIL_STEPS), (lats, LAT_STEPS)):
                    assert chain.n in (0, count), (chain.sem, chain.n, count)

            turns(dve, part)


def vit_layer(nc, A, out):
    with ExitStack() as ctx:
        seq = nc.dram_tensor("seq", [NB, S, D], F32, kind="Internal").ap()
        token_mixer(nc, A["x"], A["log_dt"], A["B_ri"], A["inv_A_real"], A["A_imag"], seq)
        W = scratch(nc, ctx)
        attention_weights(nc, A, W)
        ffn_scratch(nc, ctx, W)
        ffn_weights(nc, A, W)
        layer(nc, A, W, seq, out)


_INS = ["x", "L0_tok_log_dt", "L0_tok_B_ri", "L0_tok_inv_A_real", "L0_tok_A_imag", "L0_attn_wq_down",
        "L0_attn_q_norm_w", "L0_attn_wq_up", "L0_attn_wq_rope", "L0_attn_wkv_down", "L0_attn_kv_norm_w",
        "L0_attn_wkv_up", "L0_attn_wk_rope", "L0_attn_wo", "L0_ffn_w_gate", "L0_ffn_w_up", "L0_ffn_w_down",
        "L0_ffn_down_reorder_index"]


def rope_tables():
    import numpy as np
    pos = np.arange(S, dtype=np.float32)
    inv = (np.float32(1.0) / np.float32(10000.0) ** (np.arange(0, RD, 2, dtype=np.float32) / np.float32(RD))
           ).astype(np.float32)
    ang = pos[:, None] * inv[None, :]
    cos, sin = np.cos(ang).astype(np.float32), np.sin(ang).astype(np.float32)
    keys = [(t * np.float32(S_RK)).reshape(NT, P, RD // 2).transpose(1, 0, 2) for t in (cos, sin)]
    return {"qcos": np.tile(cos.T, (4, 1)), "qsin": np.tile(sin.T, (4, 1)), "kcos": keys[0], "ksin": keys[1]}


def kernel(**inputs):
    import numpy as _np
    import concourse.bacc as _bacc
    from concourse import mybir as _mybir
    from concourse.bass_utils import run_bass_kernel_spmd as _run

    nc = _bacc.Bacc("TRN2", target_bir_lowering=False, num_devices=1)
    arrays, A = {}, {}
    named = [(name.replace("L0_tok_", "").replace("L0_attn_", "").replace("L0_ffn_", ""), inputs[name]) for name in _INS]
    for name, a in named + list(rope_tables().items()):
        a = _np.ascontiguousarray(a)
        arrays[f"in_{name}_dram"] = a
        A[name] = nc.dram_tensor(f"in_{name}_dram", a.shape, _mybir.dt.from_np(a.dtype), kind="ExternalInput").ap()
    out = nc.dram_tensor("out_0_dram", (NB, S, D), F32, kind="ExternalOutput").ap()
    vit_layer(nc, A, out)
    r = _run(nc, [arrays], core_ids=[0])
    return r.results[0]["out_0_dram"]
```

```python
import concourse.bass as bass
from concourse import mybir
from contextlib import ExitStack

F32 = mybir.dt.float32
F16 = mybir.dt.float16
BF16 = mybir.dt.bfloat16
I32 = mybir.dt.int32
U32 = mybir.dt.uint32
ALU = mybir.AluOpType
ACT = mybir.ActivationFunctionType
AX = mybir.AxisListType

P = 128
NB, S, D = 16, 256, 512
NSTATE = 64
NT, KD = S // P, D // P
NH, RD, HD = 16, 64, 128
QR, KV = 384, 128
KQ = QR // P
FF = 1408
KF = FF // P
NCH, CH = 4, FF // 4
PAIRS, GROUPS = NH // 2, NH // 4
A_STEPS, B_STEPS = 8, 64
HBLK = 16
NBLK = P // HBLK
EPS_RMS, EPS_LN = 1e-6, 1e-5
SCALE = float((HD + RD) ** -0.5)
S_NOPE, S_RQ, S_RK = 16.0, 64.0, 0.25
S_VO = 64.0
assert S_NOPE == S_RQ * S_RK
MASK = -1e30
PRIMED = 1
FP8_MAX = 448.0
EXPONENT_BITS = 0x7F800000
LEAST_NORMAL = 2.0 ** -6
ROUNDER = 1.5 * 2.0 ** 20


class Chain:

    def __init__(self, eng, sem):
        self.eng, self.sem, self.n, self.base = eng, sem, 0, 0

    def link(self, ins):
        self.n += 1
        ins.then_inc(self.sem, 1)
        self.eng.wait_ge(self.sem, self.base + self.n)


def token_mixer(nc, x_c, log_dt, b_ri, inv_a, a_imag, seq):
    with ExitStack() as ctx:
        def sb(name, shape, dt=F32):
            return ctx.enter_context(nc.sbuf_tensor(name, shape, dt))

        def ps(name, shape, dt=F32):
            return ctx.enter_context(nc.psum_tensor(name, shape, dt))

        def sem(name):
            return ctx.enter_context(nc.semaphore(name))

        N = NSTATE
        NL = 9
        ident = sb("tm_ident", [P, P])
        dtc = sb("tm_logdt", [P, 2])
        dt = sb("tm_dt", [P, 2])
        bri = sb("tm_b", [P, 2, N, 2])
        ia = sb("tm_inva", [P, 2, N])
        ea = sb("tm_expa", [P, 2, N])
        ai = sb("tm_aimag", [P, 2, N])
        s = {k: sb("tm_" + k, [P, 2, N]) for k in
             ("zr", "zi", "m", "t", "den", "r", "gr", "gi", "fr", "fi", "u", "v")}
        wr = sb("tm_wr", [P, NL, 2, N])
        wi = sb("tm_wi", [P, NL, 2, N])
        cin = sb("tm_cin", [P, NB, N, 2])
        cs = sb("tm_cs", [P, NB, 3, N])
        U = sb("tm_u_pow", [P, B_STEPS, 2, N])
        T1 = sb("tm_t1", [P, B_STEPS // 2, N])
        T2 = sb("tm_t2", [P, B_STEPS // 2, N])
        G = sb("tm_g", [P, A_STEPS, 4, N])
        gi_ = sb("tm_gim", [P, A_STEPS, N])
        UT = sb("tm_ut", [P, P, B_STEPS])
        P1 = sb("tm_p1", [P, P, NB])
        P2 = sb("tm_p2", [P, P, NB])
        G1 = sb("tm_g1", [P, P, A_STEPS])
        G2 = sb("tm_g2", [P, P, A_STEPS])
        X1 = sb("tm_x1", [P, 2, HBLK, NB, A_STEPS])
        X2 = sb("tm_x2", [P, 2, HBLK, NB, A_STEPS])
        Y = sb("tm_y", [P, 2, HBLK, B_STEPS])
        tp = [ps(f"tm_tp{i}", [P, 4, P]) for i in range(2)]
        yp = [ps(f"tm_yp{i}", [P, 8, B_STEPS]) for i in range(4)]

        loaded, c_loaded = sem("tm_loaded"), sem("tm_c_loaded")
        ident0, ident_ok = sem("tm_ident0"), sem("tm_ident_ok")
        exp_ok = sem("tm_exp_ok")
        steps, psteps = sem("tm_dve_steps"), sem("tm_pool_steps")
        pow_ok, cs_ok = sem("tm_pow_ok"), sem("tm_cs_ok")
        tr_done, tr_read = sem("tm_tr_done"), sem("tm_tr_read")
        x1_ok, x2_ok, x_ok = sem("tm_x1_ok"), sem("tm_x2_ok"), sem("tm_x_ok")
        y_done, y_read = sem("tm_y_done"), sem("tm_y_read")
        y_stored = [sem("tm_y_stored_even"), sem("tm_y_stored_odd")]
        TR_HB = (B_STEPS + 2 * A_STEPS + 2 * NB) // 4
        TR_X = TR_HB - B_STEPS // 8

        block = ctx.enter_context(nc.Block())

        @block.sync
        def _(sp):
            sp.dma_start(dtc[:, :], log_dt.rearrange("(k p) -> p k", p=P), allow_slow_non_contiguous=True).then_inc(loaded, 16)
            sp.dma_start(ia[:, :, :], inv_a.rearrange("(k p) n -> p k n", p=P)).then_inc(loaded, 16)
            sp.dma_start(ai[:, :, :], a_imag.rearrange("(k p) n -> p k n", p=P)).then_inc(loaded, 16)
            sp.dma_start(bri[:, :, :, :], b_ri.rearrange("(k p) n r -> p k n r", p=P)).then_inc(loaded, 16)
            for hb in range(2):
                if hb:
                    sp.wait_ge(cs_ok, 1)
                sp.dma_start(cin[:, :, :, :], x_c[:, hb * P:(hb + 1) * P, :, :].rearrange("c h n r -> h c n r")
                             ).then_inc(c_loaded, 16)
            for i in range(2 * NBLK):
                sp.wait_ge(y_read, 2 * (i + 1))
                sp.dma_start(seq[i * HBLK:(i + 1) * HBLK, :, :].rearrange("h c (a b) -> (c a) h b", b=B_STEPS),
                             Y[:, i % 2, :, :]).then_inc(y_stored[i % 2], 16)
            for stored in y_stored:
                sp.wait_ge(stored, 16 * NBLK)

        @block.gpsimd
        def _(pool):
            pool.memset(ident[:, :], 0.0).then_inc(ident0, 1)
            pool.wait_ge(ident0, 1)
            pool.affine_select(out=ident[:, :], in_=ident[:, :], compare_op=ALU.not_equal, fill=1.0, base=0,
                               pattern=[[-1, P]], channel_multiplier=1).then_inc(ident_ok, 1)
            def rearrange(hb):
                pool.wait_ge(c_loaded, 16 * (hb + 1))
                if hb:
                    pool.wait_ge(tr_done, TR_HB)
                for slot, r in ((0, 0), (1, 1), (2, 0)):
                    ins = pool.tensor_copy(cs[:, :, slot, :], cin[:, :, :, r])
                ins.then_inc(cs_ok, 1)

            rearrange(0)
            for i in range(2 * NBLK):
                k = i % NBLK
                if i == 4:
                    rearrange(1)
                if k == 0:
                    pool.wait_ge(tr_read, TR_HB * (i // NBLK) + TR_X)
                if i >= 2:
                    pool.wait_ge(x_ok, i - 1)
                hs = slice(k * HBLK, (k + 1) * HBLK)
                pool.tensor_tensor(X2[:, i % 2, :, :, :],
                                   P2[:, hs, :].unsqueeze(3).broadcast_to([P, HBLK, NB, A_STEPS]),
                                   G2[:, hs, :].unsqueeze(2).broadcast_to([P, HBLK, NB, A_STEPS]),
                                   ALU.mult).then_inc(x2_ok, 1)

        @block.vector
        def _(dve):
            ch = Chain(dve, steps)
            link = ch.link
            tt = dve.tensor_tensor

            def mul(o, a, b):
                link(tt(o, a, b, ALU.mult))

            dve.wait_ge(loaded, 64)
            dve.wait_ge(exp_ok, 2)
            for hb in range(2):
                link(dve.tensor_scalar(s["zr"][:, hb, :], ea[:, hb, :], dt[:, hb:hb + 1], -0.5, ALU.mult, ALU.mult))
                link(dve.tensor_scalar(s["zi"][:, hb, :], ai[:, hb, :], dt[:, hb:hb + 1], 0.5, ALU.mult, ALU.mult))
            z = {k: v[:, :, :] for k, v in s.items()}
            mul(z["m"], z["zr"], z["zr"])
            mul(z["t"], z["zi"], z["zi"])
            link(tt(z["m"], z["m"], z["t"], ALU.add))
            link(dve.tensor_scalar(z["u"], z["zr"], -1.0, 1.0, ALU.mult, ALU.add))
            mul(z["v"], z["u"], z["u"])
            link(tt(z["den"], z["v"], z["t"], ALU.add))
            link(dve.reciprocal(z["r"], z["den"]))
            mul(z["gr"], z["u"], z["r"])
            mul(z["gi"], z["zi"], z["r"])
            link(dve.tensor_scalar(z["v"], z["m"], -1.0, 1.0, ALU.mult, ALU.add))
            mul(wr[:, 0, :, :], z["v"], z["r"])
            link(dve.tensor_scalar(wi[:, 0, :, :], z["gi"], 2.0, None, ALU.mult))
            br, bi = bri[:, :, :, 0], bri[:, :, :, 1]
            mul(z["u"], br, z["gr"])
            mul(z["v"], bi, z["gi"])
            link(tt(z["u"], z["u"], z["v"], ALU.subtract))
            mul(z["v"], br, z["gi"])
            mul(z["t"], bi, z["gr"])
            link(tt(z["v"], z["v"], z["t"], ALU.add))
            for hb in range(2):
                link(dve.tensor_scalar(s["fr"][:, hb, :], s["u"][:, hb, :], dt[:, hb:hb + 1], 2.0, ALU.mult, ALU.mult))
                link(dve.tensor_scalar(s["fi"][:, hb, :], s["v"][:, hb, :], dt[:, hb:hb + 1], 2.0, ALU.mult, ALU.mult))
            for k in range(1, NL):
                a, b = wr[:, k - 1, :, :], wi[:, k - 1, :, :]
                mul(z["u"], a, a)
                mul(z["v"], b, b)
                link(tt(wr[:, k, :, :], z["u"], z["v"], ALU.subtract))
                link(dve.scalar_tensor_tensor(out=wi[:, k, :, :], in0=a, scalar=2.0, in1=b, op0=ALU.mult, op1=ALU.mult))

            def times(o_re, o_im, a_re, a_im, k, hb, n):
                w_re = wr[:, k, hb, :].unsqueeze(1).broadcast_to([P, n, N])
                w_im = wi[:, k, hb, :].unsqueeze(1).broadcast_to([P, n, N])
                t1, t2 = T1[:, 0:n, :], T2[:, 0:n, :]
                tt(t1, a_re, w_re, ALU.mult)
                link(tt(t2, a_im, w_im, ALU.mult))
                link(tt(o_re, t1, t2, ALU.subtract))
                tt(t1, a_re, w_im, ALU.mult)
                link(tt(t2, a_im, w_re, ALU.mult))
                link(tt(o_im, t1, t2, ALU.add))

            def power_step(hb, k):
                n = 1 << (k if k < 6 else k - 6)
                if k == 0:
                    if hb:
                        dve.wait_ge(tr_done, TR_HB)
                    dve.memset(U[:, 0, 0, :], 1.0)
                    link(dve.memset(U[:, 0, 1, :], 0.0))
                    dve.tensor_copy(G[:, 0, 0, :], s["fr"][:, hb, :])
                    link(dve.tensor_copy(gi_[:, 0, :], s["fi"][:, hb, :]))
                if k < 6:
                    times(U[:, n:2 * n, 0, :], U[:, n:2 * n, 1, :], U[:, 0:n, 0, :], U[:, 0:n, 1, :], k, hb, n)
                else:
                    times(G[:, n:2 * n, 0, :], gi_[:, n:2 * n, :], G[:, 0:n, 0, :], gi_[:, 0:n, :], k, hb, n)
                if k in (4, 5):
                    dve.sem_inc(pow_ok, 1)
                if k == 8:
                    dve.tensor_scalar(G[:, :, 1, :], G[:, :, 0, :], -1.0, None, ALU.mult)
                    dve.tensor_scalar(G[:, :, 2, :], gi_[:, :, :], -1.0, None, ALU.mult)
                    dve.tensor_scalar(G[:, :, 3, :], gi_[:, :, :], -1.0, None, ALU.mult).then_inc(pow_ok, 1)

            for k in (0, 1, 2, 3, 4, 6, 7, 8, 5):
                power_step(0, k)
            for hb in range(2):
                for k in range(NBLK):
                    i = hb * NBLK + k
                    if k == 0:
                        dve.wait_ge(tr_read, TR_HB * hb + TR_X)
                    if i >= 2:
                        dve.wait_ge(y_done, 2 * (i - 1))
                    hs = slice(k * HBLK, (k + 1) * HBLK)
                    tt(X1[:, i % 2, :, :, :], P1[:, hs, :].unsqueeze(3).broadcast_to([P, HBLK, NB, A_STEPS]),
                       G1[:, hs, :].unsqueeze(2).broadcast_to([P, HBLK, NB, A_STEPS]), ALU.mult).then_inc(x1_ok, 1)
                    if hb == 0:
                        for step in ([0, 1, 2, 3], [4], [6], [7], [8], [], [5], [])[k]:
                            power_step(1, step)
                    dve.wait_ge(x1_ok, i + 1)
                    dve.wait_ge(x2_ok, i + 1)
                    tt(X1[:, i % 2, :, :, :], X1[:, i % 2, :, :, :], X2[:, i % 2, :, :, :], ALU.add).then_inc(x_ok, 1)

        @block.tensor
        def _(pe):
            pe.wait_ge(ident_ok, 1)
            n = 0

            def four(sources):
                nonlocal n
                if n >= 2:
                    pe.wait_ge(tr_read, n - 1)
                for j, src in enumerate(sources):
                    ins = pe.transpose(tp[n % 2][:, j, :], src, ident[:, :])
                ins.then_inc(tr_done, 1)
                n += 1

            for hb in range(2):
                pe.wait_ge(cs_ok, hb + 1)
                for q in range(NB // 4):
                    four([cs[:, 4 * q + j, 0:2, :] for j in range(4)])
                for q in range(NB // 4):
                    four([cs[:, 4 * q + j, 1:3, :] for j in range(4)])
                pe.wait_ge(pow_ok, 3 * hb + 1)
                for q in range(B_STEPS // 8):
                    four([U[:, 4 * q + j, :, :] for j in range(4)])
                pe.wait_ge(pow_ok, 3 * hb + 2)
                for q in range(A_STEPS // 4):
                    four([G[:, 4 * q + j, 0:2, :] for j in range(4)])
                for q in range(A_STEPS // 4):
                    four([G[:, 4 * q + j, 2:4, :] for j in range(4)])
                pe.wait_ge(pow_ok, 3 * hb + 3)
                for q in range(B_STEPS // 8, B_STEPS // 4):
                    four([U[:, 4 * q + j, :, :] for j in range(4)])
                pe.wait_ge(tr_read, TR_HB * (hb + 1))
                for k in range(NBLK):
                    i = hb * NBLK + k
                    pe.wait_ge(x_ok, i + 1)
                    for half in range(2):
                        g = 2 * i + half
                        if g >= 4:
                            pe.wait_ge(y_read, g - 3)
                        for j in range(8):
                            h = half * 8 + j
                            ins = pe.matmul(yp[g % 4][:, j, :], X1[:, i % 2, h, :, :], UT[:, k * HBLK + h, :],
                                            start=True, stop=True)
                        ins.then_inc(y_done, 1)

        @block.scalar
        def _(act):
            act.wait_ge(loaded, 64)
            act.activation(dt[:, :], dtc[:, :], ACT.Exp).then_inc(exp_ok, 1)
            act.activation(ea[:, :, :], ia[:, :, :], ACT.Exp).then_inc(exp_ok, 1)
            n = 0
            for hb in range(2):
                for dst, q0, q1 in ((P1, 0, NB // 4), (P2, 0, NB // 4), (UT, 0, B_STEPS // 8), (G1, 0, A_STEPS // 4),
                                    (G2, 0, A_STEPS // 4), (UT, B_STEPS // 8, B_STEPS // 4)):
                    for q in range(q0, q1):
                        act.wait_ge(tr_done, n + 1)
                        if hb and q == q0:
                            act.wait_ge(y_done, 2 * NBLK)
                        act.activation(dst[:, :, 4 * q:4 * q + 4].rearrange("p h j -> p j h"), tp[n % 2][:, :, :],
                                       ACT.Copy).then_inc(tr_read, 1)
                        n += 1
                for k in range(NBLK):
                    i = hb * NBLK + k
                    if i >= 2:
                        act.wait_ge(y_stored[i % 2], 16 * (i // 2))
                    for half in range(2):
                        g = 2 * i + half
                        act.wait_ge(y_done, g + 1)
                        act.activation(Y[:, i % 2, half * 8:half * 8 + 8, :], yp[g % 4][:, :, :],
                                       ACT.Copy).then_inc(y_read, 1)




def attention_weights(nc, A, W):
    with ExitStack() as ctx:
        def sb(name, shape, dt=F32):
            return ctx.enter_context(nc.sbuf_tensor(name, shape, dt))

        def sem(name):
            return ctx.enter_context(nc.semaphore(name))

        ident = W["ident"]
        wkv = sb("wkv_up", [P, NH, 2, HD])
        wqu = sb("wq_up", [P, KQ, NH, HD])
        wo = sb("wo", [P, NH, D])
        wr = sb("wq_rope", [P, KQ, GROUPS, P, 2])
        qw = sb("q_norm", [P, KQ])
        kw = sb("kv_norm", [P, 1])
        qws = sb("q_norm_scaled", [P, KQ])
        qwr = sb("q_norm_rope", [P, KQ])
        qkT = sb("qkT", [P, 2, 4, P])
        vT = sb("vT", [P, 2, P])
        wt = sb("w_nope", [P, 2, KQ, P])
        vt = sb("w_out", [P, 2, D])
        tq = [ctx.enter_context(nc.psum_tensor(f"aw_tq{i}", [P, 4, P], F32)) for i in range(2)]
        tv = [ctx.enter_context(nc.psum_tensor(f"aw_tv{i}", [P, 4, P], F32)) for i in range(2)]
        vo = [ctx.enter_context(nc.psum_tensor(f"aw_vo{i}", [P, D], F32)) for i in range(2)]
        QUARTER = NH // 4
        kv_in, q_in, o_in = ([sem(f"aw_{n}_in{c}") for c in range(4)] for n in ("kv", "q", "o"))
        r_in, small_in, keep_in = (sem("aw_" + n) for n in ("r_in", "small_in", "keep_in"))
        kv_ok, qw_ok = sem("aw_kv_ok"), sem("aw_qw_ok")
        tr_ok, tr_sb = sem("aw_tr_ok"), sem("aw_tr_sb")
        prod, wt_ok, vt_ok = sem("aw_prod"), sem("aw_wt_ok"), sem("aw_vt_ok")
        hi_ok, lo_ok, rs_ok, rh_ok, rl_ok = (sem("aw_" + n) for n in ("hi", "lo", "rs", "rh", "rl"))
        block = ctx.enter_context(nc.Block())

        @block.sync
        def _(sp):
            sp.dma_start(kw[:, :], A["kv_norm_w"].rearrange("(p o) -> p o", o=1)).then_inc(small_in, 16)
            sp.dma_start(qw[:, :], A["q_norm_w"].rearrange("(k p) -> p k", p=P),
                         allow_slow_non_contiguous=True).then_inc(small_in, 16)
            kv_up = A["wkv_up"].rearrange("p (h t d) -> p h t d", h=NH, t=2)
            q_up = A["wq_up"].rearrange("(k p) (h d) -> p k h d", p=P, h=NH)
            w_o = A["wo"].rearrange("(h p) n -> p h n", p=P)
            for c in range(4):
                heads = slice(c * QUARTER, (c + 1) * QUARTER)
                sp.dma_start(wkv[:, heads, :, :], kv_up[:, heads, :, :]).then_inc(kv_in[c], 16)
                sp.dma_start(wqu[:, :, heads, :], q_up[:, :, heads, :]).then_inc(q_in[c], 16)
                sp.dma_start(wo[:, heads, :], w_o[:, heads, :]).then_inc(o_in[c], 16)
                if c == 1:
                    sp.dma_start(wr[:, :, :, :, :], A["wq_rope"].rearrange("(k p) (g m c) -> p k g m c", p=P, g=GROUPS, c=2)
                                 ).then_inc(r_in, 16)
            for col, name in ((0, "wq_down"), (QR, "wkv_down"), (QR + KV, "wk_rope")):
                n = A[name].shape[1]
                sp.dma_start(W["down"][:, :, col:col + n], A[name].rearrange("(k p) n -> p k n", p=P)
                             ).then_inc(keep_in, 16)
            for name in ("qcos", "qsin", "kcos", "ksin"):
                sp.dma_start(W[name], A[name]).then_inc(keep_in, 16)
            sp.wait_ge(keep_in, 16 * 7)

        @block.tensor
        def _(pe):
            for h in range(NH + 1):
                if h < NH:
                    i = h % 2
                    if h % QUARTER == 0:
                        pe.wait_ge(q_in[h // QUARTER], 16)
                        pe.wait_ge(kv_ok, h // QUARTER + 1)
                    if h >= 2:
                        pe.wait_ge(wt_ok, h - 1)
                    for k in range(KQ):
                        pe.transpose(tq[i][:, k, :], wqu[:, k, h, :], ident[:, :])
                    pe.transpose(tq[i][:, 3, :], wkv[:, h, 0, :], ident[:, :])
                    pe.transpose(tv[i][:, 0, :], wkv[:, h, 1, :], ident[:, :]).then_inc(tr_ok, 1)
                if h >= 1:
                    g, i = h - 1, (h - 1) % 2
                    pe.wait_ge(tr_sb, 2 * (g + 1))
                    if g % QUARTER == 0:
                        pe.wait_ge(o_in[g // QUARTER], 16)
                    if g >= 2:
                        pe.wait_ge(vt_ok, g - 1)
                    for k in range(KQ):
                        pe.matmul(tv[i][:, 1 + k, :], qkT[:, i, k, :], qkT[:, i, 3, :], start=True, stop=True)
                    pe.matmul(vo[i][:, :], vT[:, i, :], wo[:, g, :], start=True, stop=True).then_inc(prod, 1)

        @block.scalar
        def _(act):
            for h in range(NH + 1):
                if h < NH:
                    i = h % 2
                    act.wait_ge(tr_ok, h + 1)
                    if h >= 2:
                        act.wait_ge(prod, h - 1)
                    act.activation(qkT[:, i, :, :], tq[i][:, :, :], ACT.Copy).then_inc(tr_sb, 1)
                    act.activation(vT[:, i, :], tv[i][:, 0, :], ACT.Copy).then_inc(tr_sb, 1)
                if h >= 1:
                    g, i = h - 1, (h - 1) % 2
                    act.wait_ge(prod, g + 1)
                    if g >= 2:
                        act.wait_ge(lo_ok, 2 * (g - 1))
                    act.activation(vt[:, i, :], vo[i][:, :], ACT.Copy, scale=S_VO).then_inc(vt_ok, 1)

        @block.vector
        def _(dve):
            dve.wait_ge(small_in, 32)
            dve.tensor_scalar(qws[:, :], qw[:, :], S_NOPE, None, ALU.mult)
            dve.tensor_scalar(qwr[:, :], qw[:, :], S_RQ, None, ALU.mult).then_inc(qw_ok, 1)

            def scaled(c):
                heads = slice(c * QUARTER, (c + 1) * QUARTER)
                dve.wait_ge(kv_in[c], 16)
                dve.tensor_scalar(wkv[:, heads, :, :], wkv[:, heads, :, :], kw[:, 0:1], None, ALU.mult).then_inc(kv_ok, 1)

            def rope():
                dve.wait_ge(r_in, 16)
                dve.wait_ge(qw_ok, 1)
                for k in range(KQ):
                    dve.tensor_scalar(wr[:, k, :, :, :], wr[:, k, :, :, :], qwr[:, k:k + 1], None, ALU.mult).then_inc(rs_ok, 1)
                dve.wait_ge(rs_ok, KQ)
                for k in range(KQ):
                    for c in range(2):
                        dve.tensor_copy(W["ropeH"][:, k, :, c, :], wr[:, k, :, :, c]).then_inc(rh_ok, 1)

            scaled(0)
            for h in range(NH):
                i = h % 2
                if h % QUARTER == QUARTER - 2 and h < NH - QUARTER:
                    scaled(h // QUARTER + 1)
                if h == NH // 2:
                    rope()
                dve.wait_ge(prod, h + 1)
                if h == 0:
                    dve.wait_ge(qw_ok, 1)
                if h >= 2:
                    dve.wait_ge(lo_ok, 2 * (h - 1))
                dve.tensor_tensor(wt[:, i, :, :], tv[i][:, 1:4, :],
                                  qws[:, :].unsqueeze(2).broadcast_to([P, KQ, P]), ALU.mult).then_inc(wt_ok, 1)
                dve.wait_ge(wt_ok, h + 1)
                dve.tensor_copy(W["nopeH"][:, :, h, :], wt[:, i, :, :]).then_inc(hi_ok, 1)
                dve.wait_ge(vt_ok, h + 1)
                dve.tensor_copy(W["outH"][:, h, :], vt[:, i, :]).then_inc(hi_ok, 1)

        @block.gpsimd
        def _(pool):
            for h in range(NH):
                i = h % 2
                if h == NH // 2 + 1:
                    for k in range(KQ):
                        for c in range(2):
                            pool.wait_ge(rh_ok, 2 * k + c + 1)
                            pool.tensor_tensor(W["ropeL"][:, k, :, c, :], wr[:, k, :, :, c], W["ropeH"][:, k, :, c, :],
                                               ALU.subtract).then_inc(rl_ok, 1)
                pool.wait_ge(hi_ok, 2 * h + 1)
                pool.tensor_tensor(W["nopeL"][:, :, h, :], wt[:, i, :, :], W["nopeH"][:, :, h, :],
                                   ALU.subtract).then_inc(lo_ok, 1)
                pool.wait_ge(hi_ok, 2 * h + 2)
                pool.tensor_tensor(W["outL"][:, h, :], vt[:, i, :], W["outH"][:, h, :],
                                   ALU.subtract).then_inc(lo_ok, 1)


def exponent_power(dve, ch, e, y):
    ch.link(dve.tensor_scalar(e.bitcast(U32), y.bitcast(U32), EXPONENT_BITS, None, ALU.bitwise_and))
    return dve.tensor_scalar(e, e, LEAST_NORMAL, ROUNDER, ALU.max, ALU.mult)


def ffn_scratch(nc, ctx, W):
    for name, shape, dt in (("gate", [P, KD, FF], BF16), ("up", [P, KD, FF], BF16), ("ffn_down", [P, KF, D], BF16),
                            ("gate_s", [P, FF], F32), ("up_s", [P, FF], F32), ("down_s", [P, D], F32)):
        W[name] = ctx.enter_context(nc.sbuf_tensor("kept_" + name, shape, dt))


def scratch(nc, ctx):
    def sb(name, shape, dt=F32):
        return ctx.enter_context(nc.sbuf_tensor(name, shape, dt))

    W = {
        "ident": sb("ident", [P, P]), "ident16": sb("ident16", [P, P], BF16),
        "identh": sb("identh", [P, P], F16),
        "mask": sb("causal_mask", [P, P], BF16),
        "nopeH": sb("nopeH", [P, KQ, NH, P], F16), "nopeL": sb("nopeL", [P, KQ, NH, P], F16),
        "ropeH": sb("ropeH", [P, KQ, GROUPS, 2, P], F16), "ropeL": sb("ropeL", [P, KQ, GROUPS, 2, P], F16),
        "outH": sb("outH", [P, NH, D], F16), "outL": sb("outL", [P, NH, D], F16),
        "down": sb("w_latents", [P, KD, QR + KV + RD]),
    }
    for name, shape in (("qcos", [P, S]), ("qsin", [P, S]), ("kcos", [P, NT, RD // 2]), ("ksin", [P, NT, RD // 2])):
        t = sb(name, shape)
        W[name] = t[:, :] if len(shape) == 2 else t[:, :, :]
    sem = ctx.enter_context(nc.semaphore("constants"))
    with nc.Block() as block:
        @block.gpsimd
        def _(pool):
            pool.memset(W["ident"][:, :], 0.0)
            pool.memset(W["ident16"][:, :], 0.0)
            pool.memset(W["identh"][:, :], 0.0)
            pool.memset(W["mask"][:, :], 0.0).then_inc(sem, 1)
            pool.wait_ge(sem, 1)
            for name in ("ident", "ident16", "identh"):
                t = W[name][:, :]
                pool.affine_select(out=t, in_=t, compare_op=ALU.not_equal, fill=1.0, base=0,
                                   pattern=[[-1, P]], channel_multiplier=1)
            t = W["mask"][:, :]
            pool.affine_select(out=t, in_=t, compare_op=ALU.is_ge, fill=MASK, base=0,
                               pattern=[[-1, P]], channel_multiplier=1).then_inc(sem, 1)
            pool.wait_ge(sem, 2)
    return W


FW_TILES = 2 * KF + KD
FW_FIRST = 20
HEAD_NAMES = ("group cos_sin rope q_rope queries q_hi q_lo scores max exp p_inv p_hi p_lo turn turn_sb values "
              "o_hi o_lo").split()
ORDER = """
    lat_load 0, group 1, out 0, res_load 0, cos_sin 1, rope 1, out 1, out 2, scores 0, lat_x 0, lat_load 1,
    out 3, max 0, scores 1, lat_x_sb 0, max 1, lat_down 0, lat_square 0, queries 1, exp 0, lat_mean 0,
    out 4, q_hi 1, q_lo 1, p_inv 0, p_hi 0, lat_qn 0, out 5, q_rope 1, lat_down 1, p_lo 0, scores 2, max 2,
    norm 0, turn 0, queries 2, turn_sb 0, turn 1, turn_sb 1, scores 3, max 3, lat_square 1, lat_mean 1,
    out 6, x_scale 0, q_hi 2, values 0, exp 1, q_lo 2, values 1, p_inv 1, o_hi 0, o_lo 0, p_hi 1, group 2,
    lat_kvn 0, cos_sin 2, rope 2, q_rope 2, p_lo 1, x_scaled 0, lat_x 1, lat_x_sb 1, scores 4, x_round 0,
    lat_down 2, turn 2, lat_square 2, lat_mean 2, scores 5, turn_sb 2, max 4, max 5, turn 3, turn_sb 3,
    lat_qn 1, exp 2, p_inv 2, queries 3, values 2, q_hi 3, q_lo 3, lat_down 3, p_hi 2, x_quantised 0,
    p_lo 2, values 3, o_hi 1, lat_square 3, lat_mean 3, scores 6, max 6, scores 7, o_lo 1, lat_kvn 1,
    turn 4, out 7, turn_sb 4, max 7, turn 5, turn_sb 5, turn_input 0, norm 1, input_sb 0, queries 4, exp 3,
    x_scale 1, x_scaled 1, gate_up 0, values 4, gate_out 0, q_hi 4, q_lo 4, p_inv 3, x_round 1, group 3,
    cos_sin 3, p_hi 3, values 5, gate_up 1, x_quantised 1, rope 3, q_rope 3, p_lo 3, scores 8, o_hi 2,
    o_lo 2, tanh 0, hidden 0, turn 6, max 8, turn_sb 6, scores 9, max 9, gate_out 1, turn 7, exp 4,
    queries 5, gate_up 2, p_inv 4, q_hi 5, q_lo 5, scores 10, values 6, turn_sb 7, tanh 1, hidden 1,
    values 7, o_hi 3, p_hi 4, gate_out 2, tanh 2, p_lo 4, max 10, turn 8, turn_input 1, gate_up 3,
    scores 11, hidden 2, gate_out 3, o_lo 3, max 11, turn_sb 8, turn 9, values 8, tanh 3, input_sb 1,
    turn_sb 9, hidden 3, t_scale 0, t_scaled 0, t_round 0, t_quantised 0, queries 6, values 9, exp 5,
    p_inv 5, p_hi 5, gate_up 4, q_hi 6, q_lo 6, o_hi 4, scores 12, gate_out 4, t_round 1, p_lo 5, tanh 4,
    hidden 4, o_lo 4, t_scaled 1, gate_up 5, t_quantised 1, gate_out 5, max 12, turn 10, turn_sb 10,
    scores 13, values 10, turn 11, max 13, gate_up 6, tanh 5, turn_sb 11, t_round 2, exp 6, t_quantised 2,
    queries 7, q_hi 7, hidden 5, values 11, o_hi 5, p_inv 6, p_hi 6, gate_out 6, q_lo 7, t_round 3,
    t_quantised 3, tanh 6, p_lo 6, lat_turn 0, lat_hi 0, scores 14, o_lo 5, lat_lo 0, max 14, scores 15,
    hidden 6, lat_turn 1, lat_hi 1, gate_up 7, gate_out 7, turn 12, turn_sb 12, max 15, values 12, tanh 7,
    ffn_turn 0, hidden 7, t_scale 1, lat_lo 1, turn 13, turn_sb 13, t_scaled 2, t_round 4, exp 7,
    t_quantised 4, t_round 5, t_quantised 5, t_scaled 3, values 13, o_hi 6, p_inv 7, next_group 0,
    next_cos_sin 0, t_round 6, p_hi 7, o_lo 6, ffn_turn_sb 0, next_rope 0, t_quantised 6, t_round 7,
    t_quantised 7, lat_turn 2, p_lo 7, next_queries 0, next_q_hi 0, next_q_lo 0, lat_hi 2, ffn_down 0,
    turn 14, turn_sb 14, turn 15, turn_sb 15, ffn_turn 1, ffn_norm 0, ffn_turn_sb 1, lat_lo 2,
    next_q_rope 0, values 14, values 15, o_hi 7, o_lo 7, ffn_down 1, ffn_norm 1, store 0, lat_v 0
"""


def iteration(heads, tail, latents):
    return [(step, k) for step, k in named_steps(ORDER)
            if (heads if step in HEAD_NAMES else latents if step.startswith(("lat", "next")) else tail)]


def named_steps(text):
    return [(name, int(k)) for name, k in (line.split() for line in text.split(","))]


FIRST_TURN = named_steps("""
    group 1, fw_absmax 20, fw_turn 18, lat_load 0, fw_scaled 20, fw_round 19, fw_kept 18, fw_quantised 19,
    cos_sin 1, lat_x 0, rope 1, scores 0, scores 1, lat_load 1, max 0, lat_x_sb 0, max 1, lat_down 0,
    lat_square 0, queries 1, exp 0, q_hi 1, lat_mean 0, p_inv 0, p_hi 0, lat_qn 0, fw_round 20,
    fw_quantised 20, lat_down 1, fw_turn 19, fw_absmax 21, q_lo 1, q_rope 1, p_lo 0, scores 2, fw_kept 19,
    max 2, turn 0, queries 2, turn_sb 0, turn 1, fw_scaled 21, turn_sb 1, lat_square 1, lat_mean 1,
    scores 3, q_hi 2, max 3, values 0, exp 1, q_lo 2, values 1, p_inv 1, o_hi 0, o_lo 0, p_hi 1, group 2,
    cos_sin 2, rope 2, fw_turn 20, lat_kvn 0, q_rope 2, p_lo 1, fw_round 21, fw_quantised 21, scores 4,
    turn 2, fw_absmax 22, fw_scaled 22, lat_x 1, lat_x_sb 1, fw_kept 20, lat_down 2, scores 5, turn_sb 2,
    fw_absmax 23, lat_square 2, max 4, lat_mean 2, max 5, turn 3, exp 2, turn_sb 3, lat_qn 1, p_inv 2,
    fw_scaled 23, values 2, queries 3, fw_round 22, q_hi 3, q_lo 3, lat_down 3, lat_square 3, p_hi 2,
    fw_quantised 22, fw_turn 21, values 3, p_lo 2, fw_kept 21, scores 6, max 6, o_hi 1, lat_mean 3, turn 4,
    turn_sb 4, o_lo 1, scores 7, lat_kvn 1, max 7, turn 5, turn_sb 5, queries 4, exp 3, values 4, q_hi 4,
    q_lo 4, p_inv 3, p_hi 3, group 3, fw_absmax 24, cos_sin 3, rope 3, values 5, q_rope 3, fw_scaled 24,
    p_lo 3, fw_round 23, fw_quantised 23, turn 6, fw_turn 22, fw_kept 22, o_hi 2, scores 8, o_lo 2,
    turn_sb 6, scores 9, max 8, max 9, turn 7, exp 4, queries 5, p_inv 4, q_hi 5, q_lo 5, values 6,
    turn_sb 7, values 7, scores 10, o_hi 3, p_hi 4, p_lo 4, o_lo 3, max 10, turn 8, scores 11, fw_absmax 25,
    fw_round 24, fw_quantised 24, max 11, turn_sb 8, values 8, turn 9, turn_sb 9, queries 6, values 9,
    q_hi 6, exp 5, o_hi 4, fw_turn 23, fw_scaled 25, p_inv 5, p_hi 5, fw_kept 23, q_lo 6, scores 12, p_lo 5,
    o_lo 4, max 12, turn 10, turn_sb 10, scores 13, max 13, turn 11, turn_sb 11, values 10, fw_round 25,
    fw_quantised 25, queries 7, exp 6, fw_turn 24, values 11, q_hi 7, fw_kept 24, o_hi 5, p_inv 6, p_hi 6,
    q_lo 7, o_lo 5, p_lo 6, scores 14, lat_turn 0, lat_hi 0, lat_lo 0, scores 15, lat_turn 1, lat_hi 1,
    max 14, turn 12, turn_sb 12, lat_lo 1, turn 13, max 15, values 12, exp 7, turn_sb 13, fw_turn 25,
    fw_kept 25, values 13, o_hi 6, p_inv 7, next_group 0, p_hi 7, lat_turn 2, o_lo 6, next_cos_sin 0,
    lat_hi 2, p_lo 7, next_queries 0, next_rope 0, next_q_hi 0, next_q_lo 0, turn 14, turn_sb 14, turn 15,
    turn_sb 15, lat_lo 2, next_q_rope 0, values 14, values 15, o_hi 7, lat_v 0, o_lo 7
""")


def with_weights(steps, first, last):
    result, done = [], first
    for k, step in enumerate(steps + [None]):
        while done < last and (done - first) * len(steps) <= k * (last - first):
            for lag, names in enumerate((("fw_absmax", "fw_scaled"), ("fw_round", "fw_quantised"), ("fw_turn", "fw_kept"))):
                if 0 <= done - lag < FW_TILES:
                    result += [(name, done - lag) for name in names]
            done += 1
        if step:
            result.append(step)
    return result


def layer(nc, A, W, seq, out):
    with ExitStack() as ctx:
        def sb(name, shape, dt=F32):
            return ctx.enter_context(nc.sbuf_tensor(name, shape, dt))

        sems = []

        def sem(name):
            sems.append(ctx.enter_context(nc.semaphore(name)))
            return sems[-1]

        def named(names):
            return [sem(n) for n in names.split()]

        ident, ident16 = W["ident"], W["ident16"]
        x = sb("x", [P, D])
        xT = sb("xT", [P, KD, P])
        squares = sb("squares", [P, QR], BF16)
        ssq, msq, rstd = (sb(n, [P, NT, 2]) for n in ("ssq", "mean_square", "rstd"))
        minus_half, zeros = sb("minus_half", [P, 1]), sb("zeros", [P, 1])
        qn, kn = sb("q_latent", [P, NT, QR]), sb("kv_latent", [P, NT, KV])
        kr = sb("k_rope", [P, NT, 2, 2, RD // 2])
        ka, kb = sb("k_rope_a", [P, 2, RD // 2]), sb("k_rope_b", [P, 2, RD // 2])
        vH, vL = sb("vH", [P, NT, KV], F16), sb("vL", [P, NT, KV], F16)
        qnH, qnL = sb("qnH", [P, KQ, S], F16), sb("qnL", [P, KQ, S], F16)
        knH, knL = sb("knH", [P, S], F16), sb("knL", [P, S], F16)
        krH, krL = sb("krH", [P, S], F16), sb("krL", [P, S], F16)
        ab = sb("ab_cos_sin", [P, 2, 2, S])
        ro = ab[:, :, 0, :]
        roH, roL = sb("ropeH_out", [P, 2, S], F16), sb("ropeL_out", [P, 2, S], F16)
        qr = sb("q_rope", [P, NH, S], F16)
        qpH, qpL = sb("qpH", [P, 2, 2, S], F16), sb("qpL", [P, 2, 2, S], F16)
        nmax, rsum, rinv = (sb(n, [P, 2, NT, 2]) for n in ("nmax", "rsum", "rinv"))
        ex = sb("exp_scores", [P, 2, P + S])
        prH, prL = sb("probsH", [P, 2, P + S], F16), sb("probsL", [P, 2, P + S], F16)
        pt = sb("probsT", [P, 2, 2, P + S], F16)
        oH, oL = sb("oH", [P, NH, S], F16), sb("oL", [P, NH, S], F16)
        res = sb("residual", [P, NT, D])
        st6 = sb("bn_stats", [P, NT, 6])
        mv = sb("mean_var", [P, NT, 2])
        veps, lrs, am, sx, rsx, hsx, tm, tsc, trs, tst = (
            sb(n, [P, NT]) for n in "var_eps ln_rstd absmax x_scale x_rscale half_x_scale t_absmax t_scale "
                                    "t_rscale t_out_scale".split())
        tm4 = sb("t_absmax_chunks", [P, NT, NCH])
        t = sb("hidden", [P, FF])
        xy, xe = t[:, 0:D], t[:, D:2 * D]
        te = sb("rounders", [P, 2, CH])
        y_out = te[:, :, :].rearrange("p a c -> p (a c)")[:, 0:D]
        g1, u1 = sb("g1", [P, CH]), sb("u1", [P, CH])
        tq = sb("tq", [P, FF], BF16)
        xq = tq[:, 0:NT * D].rearrange("p (n l) -> p n l", n=NT)
        turned = sb("ffn_turned", [P, FF], BF16)
        xqT = turned[:, 0:KD * S].rearrange("p (k s) -> p k s", k=KD)
        tqT = turned[:, :].rearrange("p (k s) -> p k s", k=KF)

        fw_idx = sb("fw_hidden_order", [P, KF], I32)
        fw_am, fw_ws, fw_rs = (sb(n, [P, FW_TILES]) for n in ("fw_absmax", "fw_scale", "fw_rscale"))
        fw_am2 = sb("fw_absmax_halves", [P, KD, 2])
        fw_ones = u1[:, 0:P]
        fw_e = te[:, :, :].rearrange("p a c -> p (a c)")
        HALF = FF // 2
        late = turned[:, :].bitcast(F32)

        def fw_raw(n):
            if n < 2 * KF:
                return [(t[:, 0:D], t[:, D:2 * D], res[:, 0, :], res[:, 1, :])[n % 4]]
            if n % 2:
                return [t[:, 0:HALF], t[:, HALF:FF]]
            return [late, res[:, :, :].rearrange("p n l -> p (n l)")[:, 0:HALF]]

        def fw_pieces(n):
            return n + max(n - 2 * KF, 0)

        def fw_after(n):
            if n < 2 * KF - 4:
                return n + 4
            return {2 * KF - 3: 2 * KF, 2 * KF - 1: 2 * KF + 1, 2 * KF: 2 * KF + 2, 2 * KF + 1: 2 * KF + 3}.get(n)

        G = [ctx.enter_context(nc.psum_tensor(f"G{i}", [P, 512], F32)) for i in range(3)]
        SB = [ctx.enter_context(nc.psum_tensor(f"scores{i}", [P, 512], F32)) for i in range(2)]
        PT = ctx.enter_context(nc.psum_tensor("probsT_ps", [P, 2, P + S], F16))
        OT = ctx.enter_context(nc.psum_tensor("outT", [P, 2, S], F32))
        QP = ctx.enter_context(nc.psum_tensor("projections", [P, 2, S], F32))

        LT = [QP[:, :, :].rearrange("p c s -> p (c s)")] * 2 + [SB[1]]

        def once(name):
            return ctx.enter_context(nc.semaphore(name))

        fw_idx_in, fw_ones_ok, fw_steps, fw_rs_ok, fw_y_ok, fw_diag_ok = (
            once("fw_" + n) for n in "idx_in ones_ok steps rs_ok y_ok diag_ok".split())
        fw_r_ok, fw_q_ok, fw_tr_ok, fw_kept = (once("fw_" + n) for n in "r_ok q_ok tr_ok kept".split())
        fw_in = [once(f"fw_in{i}") for i in range(4)]
        fw_down_in = [once(f"fw_down_in{i}") for i in range(2)]
        x_in, res_in, out_in, half_ok = named("x_in res_in out_in half_ok")
        xT_ps, xT_sb, lat_ps, ssq_ok, msq_ok, rstd_ok = named("xT_ps xT_sb lat_ps ssq_ok msq_ok rstd_ok")
        lq_ok, lkv_ok, lat_sb, latT_ps, latT_hi, latT_lo = named("lq_ok lkv_ok lat_sb latT_ps latT_hi latT_lo")
        ab_ps, ab_read, ro_ok, roh_ok, rol_ok = named("ab_ps ab_read ro_ok roh_ok rol_ok")
        qr_in = [sem(f"qr_in{g}") for g in range(GROUPS)]
        qp_ps, qp_hi, qp_lo, s_ps, s_max, p_exp, p_inv, p_hi, p_lo = named(
            "qp_ps qp_hi qp_lo s_ps s_max p_exp p_inv p_hi p_lo")
        pt_ps, pt_sb, o_ps, o_hi, o_lo, o_used = named("pt_ps pt_sb o_ps o_hi o_lo o_used")
        var_ok, lrs_ok, stats_ok, rsx_ok, xy_ok, xr_ok, xq_ok, xqT_ps, xqT_sb = named(
            "var_ok lrs_ok stats_ok rsx_ok xy_ok xr_ok xq_ok xqT_ps xqT_sb")
        gu_ps, g1_ok, u1_ok, gu_ok, th_ok, t_ok = named("gu_ps g1_ok u1_ok gu_ok th_ok t_ok")
        trs_ok, ty_ok, tr_ok, tq_ok = named("trs_ok ty_ok tr_ok tq_ok")
        tqT_ps, tqT_sb, d_ps, d_read, out_ok = named("tqT_ps tqT_sb d_ps d_read out_ok")
        head_steps, tail_steps, lat_steps = named("dve_head_steps dve_tail_steps dve_lat_steps")
        HEAD_STEPS, TAIL_STEPS, LAT_STEPS = PAIRS, 52, 3
        OUTS = NT * GROUPS
        QR_DMAS = 16
        NCK = NT * NCH
        with nc.Block() as priming:
            @priming.sync
            def _(sp):
                for s in sems:
                    sp.sem_inc(s, PRIMED)
        block = ctx.enter_context(nc.Block())

        def turns(eng, part):
            part(-1, with_weights(iteration(False, False, True), 0, FW_FIRST))
            part(0, FIRST_TURN)
            eng.wait_ge(fw_kept, FW_TILES)
            with eng.Fori(1, NB - 1) as b:
                part(b, iteration(True, True, True))
            part(NB - 1, iteration(True, True, False))
            part(NB, iteration(False, True, False))

        @block.sync
        def _(sp):
            def part(b, steps):
                tail, lat = b - 1, b + 1
                names = [s for s, _ in steps]
                if "lat_load" in names:
                    tokens = [seq[n * P:(n + 1) * P, bass.ds(lat, 1), :].rearrange("p o l -> p (o l)") for n in range(NT)]
                if "res_load" in names:
                    whole = seq[:, bass.ds(tail, 1), :].rearrange("(t p) o l -> p (o t) l", p=P)
                    result = out[bass.ds(tail, 1), :, :].rearrange("o (t p) l -> p (o t) l", p=P)
                for step, i in steps:
                    if step == "lat_load":
                        sp.wait_ge(xT_ps, PRIMED + NT * lat + i)
                        sp.dma_start(x[:, :], tokens[i]).then_inc(x_in, 16)
                    if step == "res_load":
                        sp.wait_ge(out_in, PRIMED + 16 * tail)
                        sp.dma_start(res[:, :, :], whole).then_inc(res_in, 16)
                    if step in ("q_rope", "next_q_rope"):
                        at = b if step == "q_rope" else b + 1
                        sp.wait_ge(rol_ok, PRIMED + GROUPS * at + i + 1)
                        for half, src in ((0, roH), (1, roL)):
                            for c in range(2):
                                for j in range(4):
                                    row = 64 * half + 32 * c
                                    sp.dma_start(qr[row:row + 32, 4 * i + j, :], src[32 * j:32 * j + 32, c, :]
                                                 ).then_inc(qr_in[i], 16)
                    if step == "store":
                        sp.wait_ge(out_ok, PRIMED + NT * (tail + 1))
                        sp.dma_start(result, res[:, :, :]).then_inc(out_in, 16)

            sp.dma_start(fw_idx[:, :], A["down_reorder_index"].rearrange("(m p) -> p m", p=P),
                         allow_slow_non_contiguous=True).then_inc(fw_idx_in, 16)
            turns(sp, part)
            sp.wait_ge(out_in, PRIMED + 16 * NB)

        @block.tensor
        def _(pe):
            def split_product(dst, aH, aL, bH, bL, first, last):
                pe.matmul(dst, aH, bH, start=first, stop=False)
                pe.matmul(dst, aH, bL, start=False, stop=False)
                return pe.matmul(dst, aL, bH, start=False, stop=last)

            def project(dst, wH, wL):
                for k in range(KQ):
                    ins = split_product(dst, wH(k), wL(k), qnH[:, k, :], qnL[:, k, :], k == 0, k == KQ - 1)
                return ins

            def lat_x(lat, n, tail):
                pe.wait_ge(x_in, PRIMED + 16 * (NT * lat + n + 1))
                if n == 0:
                    if tail is not None:
                        pe.wait_ge(d_read, PRIMED + NT * tail)
                else:
                    pe.wait_ge(lkv_ok, PRIMED + NT * lat + n)
                for k in range(KD):
                    ins = pe.transpose(G[2][:, k * P:(k + 1) * P], x[:, k * P:(k + 1) * P], ident[:, :])
                ins.then_inc(xT_ps, 1)

            def lat_down(lat, k):
                if k % 2 == 0:
                    pe.wait_ge(xT_sb, PRIMED + NT * lat + k // 2 + 1)
                    cols = slice(0, QR)
                else:
                    pe.wait_ge(lq_ok, PRIMED + NT * lat + k // 2 + 1)
                    cols = slice(QR, QR + KV + RD)
                for m in range(KD):
                    ins = pe.matmul(G[2][:, 0:cols.stop - cols.start], xT[:, m, :], W["down"][:, m, cols],
                                    start=(m == 0), stop=(m == KD - 1))
                ins.then_inc(lat_ps, 1)

            def lat_turn(lat, r):
                if r == 0:
                    pe.wait_ge(lat_sb, PRIMED + NT * (lat + 1))
                    pe.wait_ge(qp_lo, PRIMED + PAIRS * lat)
                elif r == 1:
                    pe.wait_ge(latT_lo, PRIMED + 4 * lat + 1)
                else:
                    pe.wait_ge(p_exp, PRIMED + PAIRS * lat)
                for k, parts in enumerate(([qn[:, :, 0:P], qn[:, :, P:2 * P]], [qn[:, :, 2 * P:]],
                                           [kn, kr[:, :, :, :, :].rearrange("p n a b c -> p n (a b c)")])[r]):
                    for n in range(NT):
                        ins = pe.transpose(LT[r][:, k * S + n * P:k * S + (n + 1) * P], parts[:, n, :], ident[:, :])
                ins.then_inc(latT_ps, 1)

            def group(b, g):
                if g == 0:
                    pe.wait_ge(latT_hi, PRIMED + 3 * b + 2)
                    pe.wait_ge(latT_lo, PRIMED + 4 * b + 2)
                pe.wait_ge(qp_lo, PRIMED + PAIRS * b + (0, 1, 3, 5)[g])
                for c in range(2):
                    ins = project(QP[:, c, :], lambda k: W["ropeH"][:, k, g, c, :], lambda k: W["ropeL"][:, k, g, c, :])
                ins.then_inc(ab_ps, 1)

            def queries(b, i):
                pe.wait_ge(qp_lo, PRIMED + PAIRS * b + i)
                pe.wait_ge(ab_read, PRIMED + GROUPS * b + (1, 2, 2, 3, 3, 4, 4, 4)[i])
                for c in range(2):
                    h = 2 * i + c
                    ins = project(QP[:, c, :], lambda k: W["nopeH"][:, k, h, :], lambda k: W["nopeL"][:, k, h, :])
                ins.then_inc(qp_ps, 1)

            def scores(b, h):
                i, c = h // 2, h % 2
                if c == 0:
                    pe.wait_ge(qp_hi, PRIMED + PAIRS * b + i + 1)
                    pe.wait_ge(qp_lo, PRIMED + PAIRS * b + i + 1)
                    if i % 2 == 0:
                        pe.wait_ge(qr_in[i // 2], PRIMED + QR_DMAS * 16 * (b + 1))
                    pe.wait_ge(p_exp, PRIMED + PAIRS * b + i)
                    if i == 0:
                        pe.wait_ge(latT_hi, PRIMED + 3 * b + 3)
                        pe.wait_ge(latT_lo, PRIMED + 4 * b + 3)
                for n in range(NT):
                    keys = slice(0, (n + 1) * P)
                    cols = slice(n * P, n * P + (n + 1) * P)
                    dst = SB[c][:, cols]
                    q = slice(n * P, (n + 1) * P)
                    split_product(dst, qpH[:, i % 2, c, q], qpL[:, i % 2, c, q], knH[:, keys], knL[:, keys], True, False)
                    pe.matmul(dst, qr[:, h, q], krH[:, keys], start=False, stop=False)
                    pe.matmul(dst, qr[0:64, h, q], krL[0:64, keys], start=False, stop=False)
                    ins = pe.matmul(SB[c][:, cols.stop - P:cols.stop], ident16[:, :], W["mask"][:, :],
                                    start=False, stop=True)
                ins.then_inc(s_ps, 1)

            def turn(b, h):
                i, c = h // 2, h % 2
                if c == 0:
                    pe.wait_ge(p_lo, PRIMED + PAIRS * b + i + 1)
                pe.wait_ge(pt_sb, PRIMED + NH * b + h)
                for part, src in enumerate((prH, prL)):
                    for k in range(3):
                        ins = pe.transpose(PT[:, part, k * P:(k + 1) * P], src[:, c, k * P:(k + 1) * P], W["identh"][:, :])
                ins.then_inc(pt_ps, 1)

            def values(b, h):
                i, c = h // 2, h % 2
                pe.wait_ge(pt_sb, PRIMED + NH * b + h + 1)
                if h == 0:
                    pe.wait_ge(latT_lo, PRIMED + 4 * b + 4)
                if c == 0:
                    pe.wait_ge(o_hi, PRIMED + PAIRS * b + i)
                    pe.wait_ge(o_lo, PRIMED + PAIRS * b + i)
                split_product(OT[:, c, :], vH[:, 0, :], vL[:, 0, :], pt[:, c, 0, 0:S], pt[:, c, 1, 0:S], True, False)
                ins = split_product(OT[:, c, P:S], vH[:, 1, :], vL[:, 1, :], pt[:, c, 0, S:], pt[:, c, 1, S:], False, True)
                ins.then_inc(o_ps, 1)

            def output(tail, i):
                if i == 0:
                    pe.wait_ge(o_hi, PRIMED + PAIRS * (tail + 1))
                    pe.wait_ge(o_lo, PRIMED + PAIRS * (tail + 1))
                    pe.wait_ge(tqT_sb, PRIMED + 2 * NT * tail)
                n, k = i // GROUPS, i % GROUPS
                q = slice(n * P, (n + 1) * P)
                for h in range(4 * k, 4 * k + 4):
                    ins = split_product(G[n][:, :], oH[:, h, q], oL[:, h, q], W["outH"][:, h, :],
                                        W["outL"][:, h, :], h == 0, h == NH - 1)
                ins.then_inc(o_used, 1)

            def turn_input(tail, n, with_latents):
                pe.wait_ge(xq_ok, PRIMED + NT * tail + n + 1)
                pe.wait_ge(xqT_sb, PRIMED + NT * tail + n)
                if with_latents and n == 0:
                    pe.wait_ge(lkv_ok, PRIMED + NT * (tail + 3))
                dst = G[2][:, :].bitcast(BF16)
                for k in range(KD):
                    ins = pe.transpose(dst[:, k * P:(k + 1) * P], xq[:, n, k * P:(k + 1) * P], ident16[:, :])
                ins.then_inc(xqT_ps, 1)

            def gate_up(tail, k):
                n, c = k // NCH, k % NCH
                if c == 0:
                    pe.wait_ge(xqT_sb, PRIMED + NT * tail + n + 1)
                if k == 0:
                    pe.wait_ge(var_ok, PRIMED + 2 * NT * tail + NT)
                else:
                    pe.wait_ge(u1_ok, PRIMED + NCK * tail + k)
                for r, w in enumerate((W["gate"], W["up"])):
                    for m in range(KD):
                        ins = pe.matmul(G[r][:, 0:CH], xqT[:, m, n * P:(n + 1) * P], w[:, m, c * CH:(c + 1) * CH],
                                        start=(m == 0), stop=(m == KD - 1))
                    ins.then_inc(gu_ps, 1)

            def ffn_turn(tail, n):
                pe.wait_ge(tq_ok, PRIMED + NCK * tail + NCH * (n + 1))
                pe.wait_ge(u1_ok, PRIMED + NCK * (tail + 1))
                pe.wait_ge(tqT_sb, PRIMED + 2 * (NT * tail + n))
                for m in range(KF):
                    dst = G[m // 8][:, :].bitcast(BF16)[:, m % 8 * P:(m % 8 + 1) * P]
                    ins = pe.transpose(dst, tq[:, m * P:(m + 1) * P], ident16[:, :])
                    if m in (7, KF - 1):
                        ins.then_inc(tqT_ps, 1)

            def ffn_down(tail, n):
                pe.wait_ge(tqT_sb, PRIMED + 2 * (NT * tail + n) + 2)
                pe.wait_ge(d_read, PRIMED + NT * tail + n)
                for m in range(KF):
                    ins = pe.matmul(G[2][:, :], tqT[:, m, :], W["ffn_down"][:, m, :], start=(m == 0), stop=(m == KF - 1))
                ins.then_inc(d_ps, 1)

            def fw_turn(n):
                pe.wait_ge(fw_q_ok, fw_pieces(n + 1))
                if n:
                    pe.wait_ge(fw_kept, n)
                for m in range(KD if n < 2 * KF else KF):
                    pe.transpose(G[m // 8][:, :].bitcast(BF16)[:, m % 8 * P:(m % 8 + 1) * P],
                                 tq[:, m * P:(m + 1) * P], ident16[:, :])
                pe.wait_ge(fw_diag_ok, n + 1)
                if n == 0:
                    pe.wait_ge(fw_ones_ok, 1)
                pe.matmul(G[1][:, 2 * P:3 * P], fw_ones, g1[:, n % 2 * P:(n % 2 + 1) * P], start=True, stop=True
                          ).then_inc(fw_tr_ok, 1)

            def part(b, steps):
                names = {s for s, _ in steps}
                has_tail, has_lat = "out" in names, "lat_x" in names
                for step, i in steps:
                    if step == "fw_turn":
                        fw_turn(i)
                    elif step == "lat_x":
                        lat_x(b + 1, i, b - 1 if has_tail else None)
                    elif step == "lat_down":
                        lat_down(b + 1, i)
                    elif step == "lat_turn":
                        lat_turn(b + 1, i)
                    elif step == "group":
                        group(b, i)
                    elif step == "next_group":
                        group(b + 1, i)
                    elif step == "queries":
                        queries(b, i)
                    elif step == "next_queries":
                        queries(b + 1, i)
                    elif step == "scores":
                        scores(b, i)
                    elif step == "turn":
                        turn(b, i)
                    elif step == "values":
                        values(b, i)
                    elif step == "out":
                        output(b - 1, i)
                    elif step == "turn_input":
                        turn_input(b - 1, i, has_lat)
                    elif step == "gate_up":
                        gate_up(b - 1, i)
                    elif step == "ffn_turn":
                        ffn_turn(b - 1, i)
                    elif step == "ffn_down":
                        ffn_down(b - 1, i)

            turns(pe, part)

        @block.scalar
        def _(act):
            def lat_x(lat, n):
                act.wait_ge(xT_ps, PRIMED + NT * lat + n + 1)
                act.activation(xT[:, :, :], G[2][:, :].rearrange("p (k s) -> p k s", k=KD), ACT.Copy).then_inc(xT_sb, 1)

            def lat_square(lat, i):
                n, r, width = i // 2, i % 2, (QR, KV)[i % 2]
                k = 2 * NT * lat + i
                act.wait_ge(lat_ps, PRIMED + k + 1)
                act.wait_ge(ssq_ok, PRIMED + k)
                act.activation(squares[:, 0:width], G[2][:, 0:width], ACT.Square,
                               accum_out=ssq[:, n, r:r + 1]).then_inc(ssq_ok, 1)

            def lat_turn(lat, r):
                act.wait_ge(latT_ps, PRIMED + 3 * lat + r + 1)
                if r == 0:
                    ins = act.activation(qnH[:, 0:2, :], LT[0].rearrange("p (k s) -> p k s", k=2), ACT.Copy)
                elif r == 1:
                    ins = act.activation(qnH[:, 2, :], LT[1][:, 0:S], ACT.Copy)
                else:
                    act.activation(knH[:, :], LT[2][:, 0:S], ACT.Copy)
                    ins = act.activation(krH[:, :], LT[2][:, S:2 * S], ACT.Copy)
                ins.then_inc(latT_hi, 1)

            def queries(b, i):
                act.wait_ge(qp_ps, PRIMED + PAIRS * b + i + 1)
                if i >= 2:
                    act.wait_ge(s_ps, PRIMED + NH * b + 2 * (i - 1))
                act.activation(qpH[:, i % 2, :, :], QP[:, :, :], ACT.Copy).then_inc(qp_hi, 1)

            def softmax(b, i):
                act.wait_ge(s_max, PRIMED + PAIRS * b + i + 1)
                act.wait_ge(p_lo, PRIMED + PAIRS * b + i)
                for n in range(NT):
                    cols = slice(n * P, n * P + (n + 1) * P)
                    for c in range(2):
                        ins = act.activation(ex[:, c, cols], SB[c][:, cols], ACT.Exp, bias=nmax[:, i % 2, n, c:c + 1],
                                             scale=SCALE / S_NOPE, accum_out=rsum[:, i % 2, n, c:c + 1])
                ins.then_inc(p_exp, 1)

            def turn(b, h):
                act.wait_ge(pt_ps, PRIMED + NH * b + h + 1)
                if h >= 2:
                    act.wait_ge(o_ps, PRIMED + NH * b + h - 1)
                act.activation(pt[:, h % 2, :, :], PT[:, :, :], ACT.Copy).then_inc(pt_sb, 1)

            def values(b, i, has_tail):
                act.wait_ge(o_ps, PRIMED + NH * b + 2 * i + 2)
                if has_tail:
                    act.wait_ge(o_used, PRIMED + OUTS * (b - 1) + GROUPS + i // 2 + 1)
                act.activation(oH[:, 2 * i:2 * i + 2, :], OT[:, :, :], ACT.Copy).then_inc(o_hi, 1)

            def turn_input(tail, n):
                act.wait_ge(xqT_ps, PRIMED + NT * tail + n + 1)
                act.activation(xqT[:, :, n * P:(n + 1) * P],
                               G[2][:, :].bitcast(BF16)[:, 0:D].rearrange("p (k s) -> p k s", k=KD),
                               ACT.Copy).then_inc(xqT_sb, 1)

            def tanh(tail, k):
                act.wait_ge(gu_ok, PRIMED + NCK * tail + k + 1)
                act.activation(g1[:, :], g1[:, :], ACT.Tanh, scale=hsx[:, k // NCH:k // NCH + 1]).then_inc(th_ok, 1)

            def x_scaled(tail, n):
                act.wait_ge(rsx_ok, PRIMED + NT * tail + n + 1)
                if n == 0:
                    act.wait_ge(tq_ok, PRIMED + NCK * tail)
                else:
                    act.wait_ge(xq_ok, PRIMED + NT * tail + n)
                act.activation(xy, res[:, n, :], ACT.Copy, scale=rsx[:, n:n + 1]).then_inc(xy_ok, 1)

            def t_scaled(tail, i):
                n, half = i // 2, slice(i % 2 * FF // 2, (i % 2 + 1) * FF // 2)
                act.wait_ge(trs_ok, PRIMED + NT * tail + n + 1)
                act.wait_ge(t_ok, PRIMED + NCK * tail + NCH * (n + 1))
                act.activation(t[:, half], t[:, half], ACT.Copy, scale=trs[:, n:n + 1]).then_inc(ty_ok, 1)

            def ffn_turn(tail, n):
                for r, (k0, k1) in enumerate(((0, 8), (8, KF))):
                    act.wait_ge(tqT_ps, PRIMED + 2 * (NT * tail + n) + r + 1)
                    act.activation(turned[:, k0 * P:k1 * P], G[r][:, :].bitcast(BF16)[:, 0:(k1 - k0) * P],
                                   ACT.Copy).then_inc(tqT_sb, 1)

            def fw_scaled(n):
                act.wait_ge(fw_rs_ok, n + 1)
                for raw in fw_raw(n):
                    act.activation(raw, raw, ACT.Copy, scale=fw_rs[:, n:n + 1]).then_inc(fw_y_ok, 1)
                if n >= 2:
                    act.wait_ge(fw_tr_ok, n - 1)
                act.activation(g1[:, n % 2 * P:(n % 2 + 1) * P], ident[:, :], ACT.Copy,
                               scale=fw_ws[:, n:n + 1]).then_inc(fw_diag_ok, 1)

            def fw_kept_(n):
                dst, row = ((W["gate"], W["gate_s"]), (W["up"], W["up_s"]), (W["ffn_down"], W["down_s"]))[n // KF]
                m = n % KF
                act.wait_ge(fw_tr_ok, n + 1)
                for g, (k0, k1) in enumerate([(0, KD)] if n < 2 * KF else [(0, 8), (8, KF)]):
                    src = G[g][:, :].bitcast(BF16)[:, 0:(k1 - k0) * P].rearrange("p (k s) -> p k s", s=P)
                    act.activation(dst[:, k0:k1, m * P:(m + 1) * P], src, ACT.Copy)
                act.activation(row[:, m * P:(m + 1) * P], G[1][:, 2 * P:3 * P], ACT.Copy).then_inc(fw_kept, 1)

            def part(b, steps):
                has_tail = ("out", 0) in steps
                for step, i in steps:
                    if step == "fw_scaled":
                        fw_scaled(i)
                    elif step == "fw_kept":
                        fw_kept_(i)
                    elif step == "lat_x_sb":
                        lat_x(b + 1, i)
                    elif step == "lat_square":
                        lat_square(b + 1, i)
                    elif step == "lat_hi":
                        lat_turn(b + 1, i)
                    elif step == "q_hi":
                        queries(b, i)
                    elif step == "next_q_hi":
                        queries(b + 1, i)
                    elif step == "exp":
                        softmax(b, i)
                    elif step == "turn_sb":
                        turn(b, i)
                    elif step == "o_hi":
                        values(b, i, has_tail)
                    elif step == "input_sb":
                        turn_input(b - 1, i)
                    elif step == "x_scaled":
                        x_scaled(b - 1, i)
                    elif step == "tanh":
                        tanh(b - 1, i)
                    elif step == "t_scaled":
                        t_scaled(b - 1, i)
                    elif step == "ffn_turn_sb":
                        ffn_turn(b - 1, i)

            turns(act, part)

        @block.gpsimd
        def _(pool):
            def lat_rstd(lat, i):
                n, r = i // 2, i % 2
                k = 2 * NT * lat + i
                pool.wait_ge(msq_ok, PRIMED + k + 1)
                pool.tensor_tensor(rstd[:, n, r:r + 1], msq[:, n, r:r + 1], minus_half[:, :], ALU.pow).then_inc(rstd_ok, 1)

            def norm_rstd(tail, k):
                n = k % NT
                pool.wait_ge(var_ok, PRIMED + 2 * NT * tail + k + 1)
                pool.tensor_tensor(lrs[:, n:n + 1], veps[:, n:n + 1], minus_half[:, :], ALU.pow).then_inc(lrs_ok, 1)

            def group(b, g):
                n = GROUPS * b + g
                pool.wait_ge(ab_read, PRIMED + n + 1)
                pool.tensor_tensor(ab[:, 0, 0, :], ab[:, 0, 0, :], ab[:, 1, 1, :], ALU.subtract)
                pool.tensor_tensor(ab[:, 1, 0, :], ab[:, 1, 0, :], ab[:, 0, 1, :], ALU.add).then_inc(ro_ok, 1)
                pool.wait_ge(ro_ok, PRIMED + n + 1)
                if g:
                    pool.wait_ge(qr_in[g - 1], PRIMED + QR_DMAS * 16 * (b + 1))
                else:
                    pool.wait_ge(qr_in[GROUPS - 1], PRIMED + QR_DMAS * 16 * b)
                pool.tensor_tensor(roH[:, :, :], ro, zeros[:, 0:1].unsqueeze(1).broadcast_to([P, 2, S]),
                                   ALU.add).then_inc(roh_ok, 1)
                pool.wait_ge(roh_ok, PRIMED + n + 1)
                pool.tensor_tensor(roL[:, :, :], ro, roH[:, :, :], ALU.subtract).then_inc(rol_ok, 1)

            def softmax(b, i):
                pool.wait_ge(p_inv, PRIMED + PAIRS * b + i + 1)
                pool.wait_ge(pt_ps, PRIMED + NH * b + 2 * i)
                for n in range(NT):
                    w = (n + 1) * P
                    cols = slice(n * P, n * P + w)
                    ins = pool.tensor_tensor(prH[:, :, cols], ex[:, :, cols],
                                             rinv[:, i % 2, n, :].unsqueeze(2).broadcast_to([P, 2, w]), ALU.mult)
                ins.then_inc(p_hi, 1)

            def gate_up(tail, k):
                u = NCK * tail + k
                pool.wait_ge(u1_ok, PRIMED + u + 1)
                pool.tensor_tensor(u1[:, :], g1[:, :], u1[:, :], ALU.mult).then_inc(gu_ok, 1)

            def x_quantised(tail, n):
                pool.wait_ge(xr_ok, PRIMED + NT * tail + n + 1)
                if n == 0:
                    pool.wait_ge(tqT_ps, PRIMED + 2 * NT * tail)
                pool.tensor_tensor(xq[:, n, :], xy, xe, ALU.subtract).then_inc(xq_ok, 1)

            def t_quantised(tail, k):
                cols = slice(k % NCH * CH, (k % NCH + 1) * CH)
                if k == 0:
                    pool.wait_ge(xqT_ps, PRIMED + NT * (tail + 1))
                if k == NCH:
                    pool.wait_ge(tqT_ps, PRIMED + 2 * NT * tail + 2)
                pool.wait_ge(tr_ok, PRIMED + NCK * tail + k + 1)
                pool.tensor_tensor(tq[:, cols], t[:, cols], te[:, k % 2, :], ALU.subtract).then_inc(tq_ok, 1)

            def fw_fetch(n):
                m = n % KF
                if n < 2 * KF:
                    pool.indirect_dma_start(fw_raw(n)[0], None, A["w_gate"] if n < KF else A["w_up"],
                                            bass.IndirectOffsetOnAxis(ap=fw_idx[:, m:m + 1].bitcast(U32), axis=0)
                                            ).then_inc(fw_in[n % 4], 16)
                else:
                    for c, raw in enumerate(fw_raw(n)):
                        pool.dma_start(raw, A["w_down"][m * P:(m + 1) * P, c * HALF:(c + 1) * HALF]
                                       ).then_inc(fw_down_in[m % 2], 16)

            def fw_quantised(n):
                for c, raw in enumerate(fw_raw(n)):
                    w = raw.shape[1]
                    k = fw_pieces(n) + c + 1
                    pool.wait_ge(fw_r_ok, k)
                    if n and c == 0:
                        pool.wait_ge(fw_tr_ok, n)
                    pool.tensor_tensor(tq[:, c * w:(c + 1) * w], raw, fw_e[:, 0:w], ALU.subtract).then_inc(fw_q_ok, 1)
                if fw_after(n) is not None:
                    pool.wait_ge(fw_q_ok, k)
                    fw_fetch(fw_after(n))

            def part(b, steps):
                for step, i in steps:
                    if step == "fw_quantised":
                        fw_quantised(i)
                    elif step == "lat_mean":
                        lat_rstd(b + 1, i)
                    elif step == "rope":
                        group(b, i)
                    elif step == "next_rope":
                        group(b + 1, i)
                    elif step == "p_hi":
                        softmax(b, i)
                    elif step == "norm":
                        norm_rstd(b - 1, i)
                    elif step == "x_quantised":
                        x_quantised(b - 1, i)
                    elif step == "gate_out":
                        gate_up(b - 1, i)
                    elif step == "t_quantised":
                        t_quantised(b - 1, i)
                    elif step == "ffn_norm":
                        norm_rstd(b - 1, NT + i)

            pool.memset(zeros[:, :], 0.0)
            pool.memset(minus_half[:, :], -0.5).then_inc(half_ok, 1)
            pool.wait_ge(half_ok, PRIMED + 1)
            pool.memset(fw_ones, 1.0).then_inc(fw_ones_ok, 1)
            pool.wait_ge(fw_idx_in, 16)
            for n in range(4):
                fw_fetch(n)
            turns(pool, part)

        @block.vector
        def _(dve):
            heads, tails, lats = Chain(dve, head_steps), Chain(dve, tail_steps), Chain(dve, lat_steps)
            weights = Chain(dve, fw_steps)
            tt, ts = dve.tensor_tensor, dve.tensor_scalar

            def mean(lat, i):
                n, r, width = i // 2, i % 2, (QR, KV)[i % 2]
                k = 2 * NT * lat + i
                dve.wait_ge(ssq_ok, PRIMED + k + 1)
                ts(msq[:, n, r:r + 1], ssq[:, n, r:r + 1], 1.0 / width, EPS_RMS, ALU.mult, ALU.add).then_inc(msq_ok, 1)

            def lat_qn(lat, n):
                dve.wait_ge(rstd_ok, PRIMED + 2 * (NT * lat + n) + 1)
                dve.wait_ge(latT_ps, PRIMED + 3 * lat)
                dve.wait_ge(latT_lo, PRIMED + 4 * lat)
                ts(qn[:, n, :], G[2][:, 0:QR], rstd[:, n, 0:1], None, ALU.mult).then_inc(lq_ok, 1)

            def lat_kvn(lat, n):
                dve.wait_ge(rstd_ok, PRIMED + 2 * (NT * lat + n) + 2)
                ts(kn[:, n, :], G[2][:, 0:KV], rstd[:, n, 1:2], None, ALU.mult)
                pairs = G[2][:, KV:KV + RD].rearrange("p (i two) -> p two i", two=2)
                cos, sin = (W[name][:, n:n + 1, :].broadcast_to([P, 2, RD // 2]) for name in ("kcos", "ksin"))
                tt(ka[:, :, :], pairs, cos, ALU.mult)
                tt(kb[:, :, :], pairs, sin, ALU.mult).then_inc(lkv_ok, 1)
                dve.wait_ge(lkv_ok, PRIMED + NT * lat + n + 1)
                tt(kr[:, n, 0, 0, :], ka[:, 0, :], kb[:, 1, :], ALU.subtract)
                lats.link(tt(kr[:, n, 0, 1, :], kb[:, 0, :], ka[:, 1, :], ALU.add))
                dve.tensor_copy(kr[:, n, 1, :, :], kr[:, n, 0, :, :]).then_inc(lat_sb, 1)

            def lat_turn(lat, r):
                dve.wait_ge(latT_hi, PRIMED + 3 * lat + r + 1)
                if r == 0:
                    ins = tt(qnL[:, 0:2, :], LT[0].rearrange("p (k s) -> p k s", k=2), qnH[:, 0:2, :], ALU.subtract)
                elif r == 1:
                    ins = tt(qnL[:, 2, :], LT[1][:, 0:S], qnH[:, 2, :], ALU.subtract)
                else:
                    tt(knL[:, :], LT[2][:, 0:S], knH[:, :], ALU.subtract)
                    ins = tt(krL[0:64, :], LT[2][0:64, S:2 * S], krH[0:64, :], ALU.subtract)
                ins.then_inc(latT_lo, 1)

            def lat_v(lat):
                dve.wait_ge(o_ps, PRIMED + NH * lat)
                lats.link(dve.tensor_copy(vH[:, :, :], kn[:, :, :]))
                tt(vL[:, :, :], kn[:, :, :], vH[:, :, :], ALU.subtract).then_inc(latT_lo, 1)

            def group(b, g):
                dve.wait_ge(ab_ps, PRIMED + GROUPS * b + g + 1)
                dve.wait_ge(rol_ok, PRIMED + GROUPS * b + g)
                tt(ab[:, :, 0, :], QP[:, :, :], W["qcos"].unsqueeze(1).broadcast_to([P, 2, S]), ALU.mult)
                tt(ab[:, :, 1, :], QP[:, :, :], W["qsin"].unsqueeze(1).broadcast_to([P, 2, S]), ALU.mult
                   ).then_inc(ab_read, 1)

            def queries(b, i):
                dve.wait_ge(qp_hi, PRIMED + PAIRS * b + i + 1)
                tt(qpL[:, i % 2, :, :], QP[:, :, :], qpH[:, i % 2, :, :], ALU.subtract).then_inc(qp_lo, 1)

            def scores(b, h):
                i, c = h // 2, h % 2
                dve.wait_ge(s_ps, PRIMED + NH * b + h + 1)
                for n in range(NT):
                    ins = dve.tensor_reduce(nmax[:, i % 2, n, c:c + 1], SB[c][:, n * P:n * P + (n + 1) * P], AX.X,
                                            ALU.max, negate=True)
                if c:
                    heads.link(ins)
                    ts(nmax[:, i % 2, :, :], nmax[:, i % 2, :, :], SCALE / S_NOPE, None, ALU.mult).then_inc(s_max, 1)

            def softmax(b, i):
                dve.wait_ge(p_exp, PRIMED + PAIRS * b + i + 1)
                dve.reciprocal(rinv[:, i % 2, :, :], rsum[:, i % 2, :, :]).then_inc(p_inv, 1)

            def split(b, i):
                dve.wait_ge(p_hi, PRIMED + PAIRS * b + i + 1)
                for n in range(NT):
                    cols = slice(n * P, n * P + (n + 1) * P)
                    for c in range(2):
                        ins = dve.scalar_tensor_tensor(out=prL[:, c, cols], in0=ex[:, c, cols],
                                                       scalar=rinv[:, i % 2, n, c:c + 1], in1=prH[:, c, cols],
                                                       op0=ALU.mult, op1=ALU.subtract)
                ins.then_inc(p_lo, 1)

            def values(b, i):
                dve.wait_ge(o_hi, PRIMED + PAIRS * b + i + 1)
                tt(oL[:, 2 * i:2 * i + 2, :], OT[:, :, :], oH[:, 2 * i:2 * i + 2, :], ALU.subtract).then_inc(o_lo, 1)

            def norm(tail, k):
                n = k % NT
                tails.link(dve.bn_stats(st6[:, n, :], res[:, n, :]))
                dve.sem_inc(stats_ok, 1)
                tails.link(dve.bn_aggr(mv[:, n, :], st6[:, n, :]))
                ts(veps[:, n:n + 1], mv[:, n, 1:2], EPS_LN, None, ALU.add).then_inc(var_ok, 1)
                dve.wait_ge(lrs_ok, PRIMED + 2 * NT * tail + k + 1)
                return ts(res[:, n, :], res[:, n, :], mv[:, n, 0:1], lrs[:, n:n + 1], ALU.subtract, ALU.mult)

            def attention_norm(tail, n):
                dve.wait_ge(o_used, PRIMED + OUTS * tail + GROUPS * (n + 1))
                dve.wait_ge(res_in, PRIMED + 16 * (tail + 1))
                tails.link(dve.scalar_tensor_tensor(out=res[:, n, :], in0=G[n][:, :], scalar=1.0 / S_VO,
                                                    in1=res[:, n, :], op0=ALU.mult, op1=ALU.add))
                tails.link(norm(tail, n))

            def x_scale(tail, n):
                tails.link(dve.tensor_reduce(am[:, n:n + 1], res[:, n, :], AX.X, ALU.max, apply_absolute_value=True))
                tails.link(ts(sx[:, n:n + 1], am[:, n:n + 1], 1.0 / FP8_MAX, None, ALU.mult))
                ts(hsx[:, n:n + 1], sx[:, n:n + 1], 0.5, None, ALU.mult)
                dve.reciprocal(rsx[:, n:n + 1], sx[:, n:n + 1]).then_inc(rsx_ok, 1)

            def x_round(tail, n):
                dve.wait_ge(xy_ok, PRIMED + NT * tail + n + 1)
                tails.link(exponent_power(dve, tails, xe, xy))
                tt(xy, xy, xe, ALU.add).then_inc(xr_ok, 1)

            def hidden(tail, k):
                n, c = k // NCH, k % NCH
                dve.wait_ge(th_ok, PRIMED + NCK * tail + k + 1)
                if n == 0:
                    dve.wait_ge(xq_ok, PRIMED + NT * (tail + 1))
                else:
                    dve.wait_ge(tq_ok, PRIMED + NCK * tail + k - NCH + 1)
                chunk = t[:, c * CH:(c + 1) * CH]
                dve.scalar_tensor_tensor(out=chunk, in0=g1[:, :], scalar=1.0, in1=u1[:, :], op0=ALU.add,
                                         op1=ALU.mult).then_inc(t_ok, 1)
                dve.wait_ge(t_ok, PRIMED + NCK * tail + k + 1)
                tails.link(dve.tensor_reduce(tm4[:, n, c:c + 1], chunk, AX.X, ALU.max, apply_absolute_value=True))

            def gate_up(tail, k):
                u = NCK * tail + k
                cols = slice(k % NCH * CH, (k % NCH + 1) * CH)
                dve.wait_ge(gu_ps, PRIMED + 2 * u + 1)
                tt(g1[:, :], G[0][:, 0:CH], W["gate_s"][:, cols], ALU.mult).then_inc(g1_ok, 1)
                dve.wait_ge(gu_ps, PRIMED + 2 * u + 2)
                tt(u1[:, :], G[1][:, 0:CH], W["up_s"][:, cols], ALU.mult).then_inc(u1_ok, 1)

            def t_scale(tail, n):
                s = slice(n, n + 1)
                tails.link(dve.tensor_reduce(tm[:, s], tm4[:, n, :], AX.X, ALU.max))
                tails.link(ts(tsc[:, s], tm[:, s], 1.0 / FP8_MAX, None, ALU.mult))
                dve.reciprocal(trs[:, s], tsc[:, s]).then_inc(trs_ok, 1)
                tails.link(dve.scalar_tensor_tensor(out=tst[:, s], in0=sx[:, s], scalar=hsx[:, s], in1=tsc[:, s],
                                                    op0=ALU.mult, op1=ALU.mult))

            def t_round(tail, k):
                cols = slice(k % NCH * CH, (k % NCH + 1) * CH)
                e = te[:, k % 2, :]
                dve.wait_ge(ty_ok, PRIMED + NCK // 2 * tail + k // 2 + 1)
                dve.wait_ge(tq_ok, PRIMED + NCK * tail + max(k - 1, 0))
                if k == 0:
                    dve.wait_ge(d_read, PRIMED + NT * tail)
                tails.link(exponent_power(dve, tails, e, t[:, cols]))
                tt(t[:, cols], t[:, cols], e, ALU.add).then_inc(tr_ok, 1)

            def ffn_norm(tail, n):
                dve.wait_ge(d_ps, PRIMED + NT * tail + n + 1)
                dve.wait_ge(tq_ok, PRIMED + NCK * (tail + 1))
                tt(y_out, G[2][:, :], W["down_s"][:, :], ALU.mult).then_inc(d_read, 1)
                dve.wait_ge(d_read, PRIMED + NT * tail + n + 1)
                tails.link(dve.scalar_tensor_tensor(out=res[:, n, :], in0=y_out, scalar=tst[:, n:n + 1],
                                                    in1=res[:, n, :], op0=ALU.mult, op1=ALU.add))
                norm(tail, NT + n).then_inc(out_ok, 1)

            def fw_absmax(n):
                if n < 2 * KF:
                    dve.wait_ge(fw_in[n % 4], 16 * (n // 4 + 1))
                    weights.link(dve.tensor_reduce(fw_am[:, n:n + 1], fw_raw(n)[0], AX.X, ALU.max, apply_absolute_value=True))
                else:
                    m = n - 2 * KF
                    dve.wait_ge(fw_down_in[m % 2], 32 * (m // 2 + 1))
                    for c, raw in enumerate(fw_raw(n)):
                        ins = dve.tensor_reduce(fw_am2[:, m, c:c + 1], raw, AX.X, ALU.max, apply_absolute_value=True)
                    weights.link(ins)
                    weights.link(dve.tensor_reduce(fw_am[:, n:n + 1], fw_am2[:, m, :], AX.X, ALU.max))
                weights.link(ts(fw_ws[:, n:n + 1], fw_am[:, n:n + 1], 1.0 / FP8_MAX, None, ALU.mult))
                dve.reciprocal(fw_rs[:, n:n + 1], fw_ws[:, n:n + 1]).then_inc(fw_rs_ok, 1)

            def fw_round(n):
                for c, raw in enumerate(fw_raw(n)):
                    w = raw.shape[1]
                    k = fw_pieces(n) + c
                    dve.wait_ge(fw_y_ok, k + 1)
                    if k:
                        dve.wait_ge(fw_q_ok, k)
                    weights.link(exponent_power(dve, weights, fw_e[:, 0:w], raw))
                    tt(raw, raw, fw_e[:, 0:w], ALU.add).then_inc(fw_r_ok, 1)

            def part(b, steps):
                heads.base, heads.n = PRIMED + HEAD_STEPS * b, 0
                tails.base, tails.n = PRIMED + TAIL_STEPS * (b - 1), 0
                lats.base, lats.n = PRIMED + LAT_STEPS * (b + 1), 0
                for step, i in steps:
                    if step == "fw_absmax":
                        fw_absmax(i)
                    elif step == "fw_round":
                        fw_round(i)
                    elif step == "lat_mean":
                        mean(b + 1, i)
                    elif step == "lat_qn":
                        lat_qn(b + 1, i)
                    elif step == "lat_kvn":
                        lat_kvn(b + 1, i)
                    elif step == "lat_lo":
                        lat_turn(b + 1, i)
                    elif step == "lat_v":
                        lat_v(b + 1)
                    elif step == "cos_sin":
                        group(b, i)
                    elif step == "next_cos_sin":
                        group(b + 1, i)
                    elif step == "q_lo":
                        queries(b, i)
                    elif step == "next_q_lo":
                        queries(b + 1, i)
                    elif step == "max":
                        scores(b, i)
                    elif step == "p_inv":
                        softmax(b, i)
                    elif step == "p_lo":
                        split(b, i)
                    elif step == "o_lo":
                        values(b, i)
                    elif step == "norm":
                        attention_norm(b - 1, i)
                    elif step == "x_scale":
                        x_scale(b - 1, i)
                    elif step == "x_round":
                        x_round(b - 1, i)
                    elif step == "gate_out":
                        gate_up(b - 1, i)
                    elif step == "hidden":
                        hidden(b - 1, i)
                    elif step == "t_scale":
                        t_scale(b - 1, i)
                    elif step == "t_round":
                        t_round(b - 1, i)
                    elif step == "ffn_norm":
                        ffn_norm(b - 1, i)
                for chain, count in ((heads, HEAD_STEPS), (tails, TAIL_STEPS), (lats, LAT_STEPS)):
                    assert chain.n in (0, count), (chain.sem, chain.n, count)

            turns(dve, part)


def vit_layer(nc, A, out):
    with ExitStack() as ctx:
        seq = nc.dram_tensor("seq", [S, NB, D], F32, kind="Internal").ap()
        token_mixer(nc, A["x"], A["log_dt"], A["B_ri"], A["inv_A_real"], A["A_imag"], seq)
        W = scratch(nc, ctx)
        attention_weights(nc, A, W)
        ffn_scratch(nc, ctx, W)
        layer(nc, A, W, seq, out)


_INS = ["x", "L0_tok_log_dt", "L0_tok_B_ri", "L0_tok_inv_A_real", "L0_tok_A_imag", "L0_attn_wq_down",
        "L0_attn_q_norm_w", "L0_attn_wq_up", "L0_attn_wq_rope", "L0_attn_wkv_down", "L0_attn_kv_norm_w",
        "L0_attn_wkv_up", "L0_attn_wk_rope", "L0_attn_wo", "L0_ffn_w_gate", "L0_ffn_w_up", "L0_ffn_w_down",
        "L0_ffn_down_reorder_index"]


def rope_tables():
    import numpy as np
    pos = np.arange(S, dtype=np.float32)
    inv = (np.float32(1.0) / np.float32(10000.0) ** (np.arange(0, RD, 2, dtype=np.float32) / np.float32(RD))
           ).astype(np.float32)
    ang = pos[:, None] * inv[None, :]
    cos, sin = np.cos(ang).astype(np.float32), np.sin(ang).astype(np.float32)
    keys = [(t * np.float32(S_RK)).reshape(NT, P, RD // 2).transpose(1, 0, 2) for t in (cos, sin)]
    return {"qcos": np.tile(cos.T, (4, 1)), "qsin": np.tile(sin.T, (4, 1)), "kcos": keys[0], "ksin": keys[1]}


def kernel(**inputs):
    import numpy as _np
    import concourse.bacc as _bacc
    from concourse import mybir as _mybir
    from concourse.bass_utils import run_bass_kernel_spmd as _run

    nc = _bacc.Bacc("TRN2", target_bir_lowering=False, num_devices=1)
    arrays, A = {}, {}
    named = [(name.replace("L0_tok_", "").replace("L0_attn_", "").replace("L0_ffn_", ""), inputs[name]) for name in _INS]
    for name, a in named + list(rope_tables().items()):
        a = _np.ascontiguousarray(a)
        arrays[f"in_{name}_dram"] = a
        A[name] = nc.dram_tensor(f"in_{name}_dram", a.shape, _mybir.dt.from_np(a.dtype), kind="ExternalInput").ap()
    out = nc.dram_tensor("out_0_dram", (NB, S, D), F32, kind="ExternalOutput").ap()
    vit_layer(nc, A, out)
    r = _run(nc, [arrays], core_ids=[0])
    return r.results[0]["out_0_dram"]
```
